# Optimizing a Trainium2 kernel written in Bass

```python
import numpy as np
import jax
import jax.numpy as jnp

def _softmax(x, axis=-1):
    return jax.nn.softmax(x, axis=axis)

def _gelu(x):
    return jax.nn.gelu(x, approximate=True)

def _silu(x):
    return jax.nn.silu(x)

def _sigmoid(x):
    return jax.nn.sigmoid(x)

def _layernorm(x, axis=-1, eps=1e-05):
    m = jnp.mean(x, axis=axis, keepdims=True)
    v = jnp.var(x, axis=axis, keepdims=True)
    return (x - m) / jnp.sqrt(v + eps)

def _scatter_add(tgt, idx, src, axis=0):
    return tgt.at[idx].add(src)

def _segment_sum(src, seg, n):
    return jax.ops.segment_sum(src, seg, n)
kernel_name = 'mk_prb_d1_jaxref_r8_f93990'

def setup_inputs(seed: int=0):
    np.random.seed(seed)
    _w = jnp.asarray

    def _L0_attn_setup():
        import jax, jax.numpy as jnp
        import numpy as np
        D_MODEL = 128
        N_HEADS = 16
        WINDOW = 64
        HEAD_DIM = D_MODEL // N_HEADS
        HALF = WINDOW // 2
        NWIN = WINDOW + 1
        LN_EPS = 1e-05

        def _layernorm(x, g, b):
            mu = jnp.mean(x, axis=-1, keepdims=True)
            var = jnp.var(x, axis=-1, keepdims=True)
            return (x - mu) * jax.lax.rsqrt(var + LN_EPS) * g + b

        def _linear_attention(q, k, v):
            q = jax.nn.elu(q) + 1.0
            k = jax.nn.elu(k) + 1.0
            kv = jnp.einsum('bsd,bse->bde', k, v)
            num = jnp.einsum('bsd,bde->bse', q, kv)
            denom = jnp.einsum('bsd,bd->bs', q, k.sum(axis=1))
            return num / (denom[..., None] + 1e-06)

        def _window_attention(q, k, v, rel_bias):
            B, S, _ = q.shape
            qh = q.reshape(B, S, N_HEADS, HEAD_DIM).transpose(0, 2, 1, 3)
            kh = k.reshape(B, S, N_HEADS, HEAD_DIM).transpose(0, 2, 1, 3)
            vh = v.reshape(B, S, N_HEADS, HEAD_DIM).transpose(0, 2, 1, 3)
            kp = jnp.pad(kh, ((0, 0), (0, 0), (HALF, HALF), (0, 0)))
            vp = jnp.pad(vh, ((0, 0), (0, 0), (HALF, HALF), (0, 0)))
            pos = jnp.arange(S)
            scale = np.float32(1.0 / np.sqrt(HEAD_DIM))

            def score_step(_, w):
                off = w - HALF
                ks = jax.lax.dynamic_slice_in_dim(kp, w, S, axis=2)
                s = jnp.einsum('bhsd,bhsd->bhs', qh, ks) * scale
                s = s + rel_bias[off + WINDOW][None, :, None]
                valid = (pos + off >= 0) & (pos + off < S)
                s = jnp.where(valid[None, None, :], s, -jnp.inf)
                return (None, s)
            _, scores = jax.lax.scan(score_step, None, jnp.arange(NWIN))
            attn = jax.nn.softmax(scores, axis=0)

            def out_step(acc, aw):
                a, w = aw
                vs = jax.lax.dynamic_slice_in_dim(vp, w, S, axis=2)
                return (acc + a[..., None] * vs, None)
            out, _ = jax.lax.scan(out_step, jnp.zeros_like(qh), (attn, jnp.arange(NWIN)))
            return out.transpose(0, 2, 1, 3).reshape(B, S, D_MODEL)
        key = jax.random.key(seed)
        ks = jax.random.split(key, 16)

        def lin(k, fan_in, shape):
            return (jax.random.normal(k, shape, jnp.float32) / np.sqrt(fan_in)).astype(jnp.float32)
        D = D_MODEL
        inp = {'x': jax.random.normal(ks[0], (2, 256, D), jnp.float32), 'wq_lin': lin(ks[1], D, (D, D)), 'bq_lin': jnp.zeros((D,), jnp.float32), 'wk_lin': lin(ks[2], D, (D, D)), 'bk_lin': jnp.zeros((D,), jnp.float32), 'wv_lin': lin(ks[3], D, (D, D)), 'bv_lin': jnp.zeros((D,), jnp.float32), 'wq_loc': lin(ks[4], D, (D, D)), 'bq_loc': jnp.zeros((D,), jnp.float32), 'wk_loc': lin(ks[5], D, (D, D)), 'bk_loc': jnp.zeros((D,), jnp.float32), 'wv_loc': lin(ks[6], D, (D, D)), 'bv_loc': jnp.zeros((D,), jnp.float32), 'wo': lin(ks[7], D, (D, D)), 'bo': jnp.zeros((D,), jnp.float32), 'wg1': lin(ks[8], 3 * D, (3 * D, D)), 'bg1': jnp.zeros((D,), jnp.float32), 'wg2': lin(ks[9], D, (D, D)), 'bg2': jnp.zeros((D,), jnp.float32), 'rel_bias': jax.random.normal(ks[10], (2 * WINDOW + 1, N_HEADS), jnp.float32), 'ln_g': jnp.ones((D,), jnp.float32), 'ln_b': jnp.zeros((D,), jnp.float32)}
        return inp
    _L0_attn_in = _L0_attn_setup()

    def _L0_ffn_setup():
        import jax, jax.numpy as jnp
        import numpy as np
        from jax.scipy.linalg import expm
        B, S, D, E, K, NROT = (2, 256, 128, 8, 2, 3)
        DF = 4 * D
        EPS = 1e-05
        key = jax.random.key(seed)
        ks = jax.random.split(key, 8)
        s = lambda d: 1.0 / np.sqrt(d)
        return {'x': jax.random.normal(ks[0], (B, S, D), jnp.float32), 'ln_g': jnp.ones((D,), jnp.float32), 'ln_b': jnp.zeros((D,), jnp.float32), 'abel_w': jax.random.normal(ks[1], (D, D), jnp.float32) * s(D), 'abel_b': jnp.zeros((D,), jnp.float32), 'gate_w_moe': jax.random.normal(ks[2], (D, E), jnp.float32) * s(D), 'gate_b_moe': jnp.zeros((E,), jnp.float32), 'w1': jax.random.normal(ks[3], (E, D, DF), jnp.float32) * s(D), 'b1': jnp.zeros((E, DF), jnp.float32), 'w2': jax.random.normal(ks[4], (E, DF, D), jnp.float32) * s(DF), 'b2': jnp.zeros((E, D), jnp.float32), 'gens': jax.random.normal(ks[5], (NROT, D, D), jnp.float32) * 0.02, 'mix_w': jax.random.normal(ks[6], (2 * D, 1), jnp.float32) * s(2 * D), 'mix_b': jnp.zeros((1,), jnp.float32)}
    _L0_ffn_in = _L0_ffn_setup()
    _d = {'L0_attn_x': _L0_attn_in['x'], 'L0_attn_wq_lin': _L0_attn_in['wq_lin'], 'L0_attn_bq_lin': _L0_attn_in['bq_lin'], 'L0_attn_wk_lin': _L0_attn_in['wk_lin'], 'L0_attn_bk_lin': _L0_attn_in['bk_lin'], 'L0_attn_wv_lin': _L0_attn_in['wv_lin'], 'L0_attn_bv_lin': _L0_attn_in['bv_lin'], 'L0_attn_wq_loc': _L0_attn_in['wq_loc'], 'L0_attn_bq_loc': _L0_attn_in['bq_loc'], 'L0_attn_wk_loc': _L0_attn_in['wk_loc'], 'L0_attn_bk_loc': _L0_attn_in['bk_loc'], 'L0_attn_wv_loc': _L0_attn_in['wv_loc'], 'L0_attn_bv_loc': _L0_attn_in['bv_loc'], 'L0_attn_wo': _L0_attn_in['wo'], 'L0_attn_bo': _L0_attn_in['bo'], 'L0_attn_wg1': _L0_attn_in['wg1'], 'L0_attn_bg1': _L0_attn_in['bg1'], 'L0_attn_wg2': _L0_attn_in['wg2'], 'L0_attn_bg2': _L0_attn_in['bg2'], 'L0_attn_rel_bias': _L0_attn_in['rel_bias'], 'L0_attn_ln_g': _L0_attn_in['ln_g'], 'L0_attn_ln_b': _L0_attn_in['ln_b'], 'L0_ffn_ln_g': _L0_ffn_in['ln_g'], 'L0_ffn_ln_b': _L0_ffn_in['ln_b'], 'L0_ffn_abel_w': _L0_ffn_in['abel_w'], 'L0_ffn_abel_b': _L0_ffn_in['abel_b'], 'L0_ffn_gate_w_moe': _L0_ffn_in['gate_w_moe'], 'L0_ffn_gate_b_moe': _L0_ffn_in['gate_b_moe'], 'L0_ffn_w1': _L0_ffn_in['w1'], 'L0_ffn_b1': _L0_ffn_in['b1'], 'L0_ffn_w2': _L0_ffn_in['w2'], 'L0_ffn_b2': _L0_ffn_in['b2'], 'L0_ffn_gens': _L0_ffn_in['gens'], 'L0_ffn_mix_w': _L0_ffn_in['mix_w'], 'L0_ffn_mix_b': _L0_ffn_in['mix_b']}
    _x0 = _d['L0_attn_x']
    _d['L0_attn_x'] = jax.random.normal(jax.random.fold_in(jax.random.key(seed), 1), (4, 512, 128), dtype=_x0.dtype)
    del _x0
    return _d

def reference(L0_attn_x, L0_attn_wq_lin, L0_attn_bq_lin, L0_attn_wk_lin, L0_attn_bk_lin, L0_attn_wv_lin, L0_attn_bv_lin, L0_attn_wq_loc, L0_attn_bq_loc, L0_attn_wk_loc, L0_attn_bk_loc, L0_attn_wv_loc, L0_attn_bv_loc, L0_attn_wo, L0_attn_bo, L0_attn_wg1, L0_attn_bg1, L0_attn_wg2, L0_attn_bg2, L0_attn_rel_bias, L0_attn_ln_g, L0_attn_ln_b, L0_ffn_ln_g, L0_ffn_ln_b, L0_ffn_abel_w, L0_ffn_abel_b, L0_ffn_gate_w_moe, L0_ffn_gate_b_moe, L0_ffn_w1, L0_ffn_b1, L0_ffn_w2, L0_ffn_b2, L0_ffn_gens, L0_ffn_mix_w, L0_ffn_mix_b):

    def _L0_attn_ref(x, wq_lin, bq_lin, wk_lin, bk_lin, wv_lin, bv_lin, wq_loc, bq_loc, wk_loc, bk_loc, wv_loc, bv_loc, wo, bo, wg1, bg1, wg2, bg2, rel_bias, ln_g, ln_b):
        import jax, jax.numpy as jnp
        import numpy as np
        D_MODEL = 128
        N_HEADS = 16
        WINDOW = 64
        HEAD_DIM = D_MODEL // N_HEADS
        HALF = WINDOW // 2
        NWIN = WINDOW + 1
        LN_EPS = 1e-05

        def _layernorm(x, g, b):
            mu = jnp.mean(x, axis=-1, keepdims=True)
            var = jnp.var(x, axis=-1, keepdims=True)
            return (x - mu) * jax.lax.rsqrt(var + LN_EPS) * g + b

        def _linear_attention(q, k, v):
            q = jax.nn.elu(q) + 1.0
            k = jax.nn.elu(k) + 1.0
            kv = jnp.einsum('bsd,bse->bde', k, v)
            num = jnp.einsum('bsd,bde->bse', q, kv)
            denom = jnp.einsum('bsd,bd->bs', q, k.sum(axis=1))
            return num / (denom[..., None] + 1e-06)

        def _window_attention(q, k, v, rel_bias):
            B, S, _ = q.shape
            qh = q.reshape(B, S, N_HEADS, HEAD_DIM).transpose(0, 2, 1, 3)
            kh = k.reshape(B, S, N_HEADS, HEAD_DIM).transpose(0, 2, 1, 3)
            vh = v.reshape(B, S, N_HEADS, HEAD_DIM).transpose(0, 2, 1, 3)
            kp = jnp.pad(kh, ((0, 0), (0, 0), (HALF, HALF), (0, 0)))
            vp = jnp.pad(vh, ((0, 0), (0, 0), (HALF, HALF), (0, 0)))
            pos = jnp.arange(S)
            scale = np.float32(1.0 / np.sqrt(HEAD_DIM))

            def score_step(_, w):
                off = w - HALF
                ks = jax.lax.dynamic_slice_in_dim(kp, w, S, axis=2)
                s = jnp.einsum('bhsd,bhsd->bhs', qh, ks) * scale
                s = s + rel_bias[off + WINDOW][None, :, None]
                valid = (pos + off >= 0) & (pos + off < S)
                s = jnp.where(valid[None, None, :], s, -jnp.inf)
                return (None, s)
            _, scores = jax.lax.scan(score_step, None, jnp.arange(NWIN))
            attn = jax.nn.softmax(scores, axis=0)

            def out_step(acc, aw):
                a, w = aw
                vs = jax.lax.dynamic_slice_in_dim(vp, w, S, axis=2)
                return (acc + a[..., None] * vs, None)
            out, _ = jax.lax.scan(out_step, jnp.zeros_like(qh), (attn, jnp.arange(NWIN)))
            return out.transpose(0, 2, 1, 3).reshape(B, S, D_MODEL)
        h = _layernorm(x, ln_g, ln_b)
        lin_out = _linear_attention(h @ wq_lin + bq_lin, h @ wk_lin + bk_lin, h @ wv_lin + bv_lin)
        win_out = _window_attention(h @ wq_loc + bq_loc, h @ wk_loc + bk_loc, h @ wv_loc + bv_loc, rel_bias)
        gate_in = jnp.concatenate([lin_out, win_out, h], axis=-1)
        gate = jax.nn.sigmoid(jnp.maximum(gate_in @ wg1 + bg1, 0.0) @ wg2 + bg2)
        out = gate * lin_out + (1.0 - gate) * win_out
        return out @ wo + bo + x

    def _L0_ffn_ref(x, ln_g, ln_b, abel_w, abel_b, gate_w_moe, gate_b_moe, w1, b1, w2, b2, gens, mix_w, mix_b):
        import jax, jax.numpy as jnp
        import numpy as np
        from jax.scipy.linalg import expm
        B, S, D, E, K, NROT = (2, 256, 128, 8, 2, 3)
        DF = 4 * D
        EPS = 1e-05
        residual = x
        mu = jnp.mean(x, axis=-1, keepdims=True)
        var = jnp.mean((x - mu) ** 2, axis=-1, keepdims=True)
        xn = (x - mu) * jax.lax.rsqrt(var + EPS) * ln_g + ln_b
        abel = jax.nn.gelu(xn @ abel_w + abel_b, approximate=False)
        logits = xn @ gate_w_moe + gate_b_moe
        tw, ti = jax.lax.top_k(logits, K)
        tw = jax.nn.softmax(tw, axis=-1)
        onehot = (ti[..., None] == jnp.arange(E)).astype(tw.dtype)
        wdense = jnp.sum(tw[..., None] * onehot, axis=2)
        h = jax.nn.gelu(jnp.einsum('bsd,edf->besf', xn, w1) + b1[None, :, None, :], approximate=False)
        eo = jnp.einsum('besf,efd->besd', h, w2) + b2[None, :, None, :]
        moe = jnp.einsum('besd,bse->bsd', eo, wdense)
        rot = expm(gens[0])
        for i in range(1, NROT):
            rot = rot @ expm(gens[i])
        nonabel = moe @ rot
        combined = jnp.concatenate([abel, nonabel], axis=-1)
        g = jax.nn.sigmoid(combined @ mix_w + mix_b)
        return residual + abel * (1.0 - g) + nonabel * g
    x = L0_attn_x
    xn = _layernorm(x, axis=-1)
    x = x + _L0_attn_ref(xn, L0_attn_wq_lin, L0_attn_bq_lin, L0_attn_wk_lin, L0_attn_bk_lin, L0_attn_wv_lin, L0_attn_bv_lin, L0_attn_wq_loc, L0_attn_bq_loc, L0_attn_wk_loc, L0_attn_bk_loc, L0_attn_wv_loc, L0_attn_bv_loc, L0_attn_wo, L0_attn_bo, L0_attn_wg1, L0_attn_bg1, L0_attn_wg2, L0_attn_bg2, L0_attn_rel_bias, L0_attn_ln_g, L0_attn_ln_b) + _L0_ffn_ref(xn, L0_ffn_ln_g, L0_ffn_ln_b, L0_ffn_abel_w, L0_ffn_abel_b, L0_ffn_gate_w_moe, L0_ffn_gate_b_moe, L0_ffn_w1, L0_ffn_b1, L0_ffn_w2, L0_ffn_b2, L0_ffn_gens, L0_ffn_mix_w, L0_ffn_mix_b)
    return x

_drawn_inputs = setup_inputs


def setup_inputs(seed=0):
    import zlib

    import numpy as np

    out = dict(_drawn_inputs(seed))
    spreads = {'L0_attn_bq_lin': (0.0, 2.0),
     'L0_attn_bk_lin': (0.0, 2.0),
     'L0_attn_bv_lin': (0.0, 0.5),
     'L0_attn_bq_loc': (0.0, 0.8),
     'L0_attn_bk_loc': (0.0, 2.0),
     'L0_attn_bv_loc': (0.0, 0.469),
     'L0_attn_bo': (0.0, 0.1),
     'L0_attn_bg1': (0.0, 0.8),
     'L0_attn_bg2': (0.0, 2.0),
     'L0_attn_ln_g': (1.0, 0.6),
     'L0_attn_ln_b': (0.0, 0.305),
     'L0_ffn_ln_g': (1.0, 0.2),
     'L0_ffn_ln_b': (0.0, 0.1),
     'L0_ffn_abel_b': (0.0, 0.785),
     'L0_ffn_gate_b_moe': (0.0, 0.283),
     'L0_ffn_b1': (0.0, 0.726),
     'L0_ffn_b2': (0.0, 0.538)}
    factors = {'L0_attn_wq_lin': 8.0,
     'L0_attn_wk_lin': 8.0,
     'L0_attn_wv_lin': 3.056,
     'L0_attn_wg1': 5.102,
     'L0_attn_wg2': 4.435}
    for name, (base, spread) in spreads.items():
        noise = np.random.default_rng([zlib.crc32(name.encode()), seed]).standard_normal(out[name].shape)
        drawn = base * np.exp(spread * noise) if base else spread * noise
        out[name] = jnp.asarray(drawn.astype(out[name].dtype))
    for name, factor in factors.items():
        out[name] = (out[name] * factor).astype(out[name].dtype)
    return out
```

```python
import concourse.bass as bass
from concourse import mybir
from contextlib import ExitStack


def attention_and_moe_block(nc, x, vecs, rows, w_loc, w_more, rel_t, b1_cols, b2, w1, w2,
                            qk_scratch, out):
    f32, f32r, bf16, f16 = mybir.dt.float32, mybir.dt.float32r, mybir.dt.bfloat16, mybir.dt.float16
    ALU, ACT, AX = mybir.AluOpType, mybir.ActivationFunctionType, mybir.AxisListType

    P = 128
    NB, S, D = x.shape
    TB = S // P
    NT = NB * TB
    TOK = NB * S
    E, _, DF = w1.shape
    NC = DF // P
    NHEAD, HD = 16, 8
    NPAIR = NHEAD // 2
    HALF = 32
    BQ = 64
    NBLK = S // BQ
    SP = S + 2 * HALF
    QK = S + SP
    SPLITS = 3
    QTERM = [0, 0, 0, 1, 1, 2]
    KTERM = [0, 1, 2, 0, 1, 0]
    NTERM = len(QTERM)
    VG = HD + 1
    VW = SPLITS * 2 * VG
    NEG = -1e30
    EPS = 1e-5
    SCALE = float(HD) ** -0.5
    P_SHIFT = 12 * 0.6931471805599453
    EXPM_SQUARINGS, EXPM_DEGREE = 4, 8
    NG = 3

    (V_BQLIN, V_BQLOC, V_BKLOC, V_BV0, V_BV1, V_BG1, V_BG2, V_G, V_B, V_FG, V_FB, V_ABEL,
     V_MIX1, V_MIX2, V_MIXB, V_GATEB) = range(16)
    (M_QLIN, M_KLIN, M_VLIN, M_WO, M_G1LIN, M_G1WIN, M_G1H, M_WG2, M_ABEL, M_GEN) = range(10)
    M_GATE = (M_GEN + NG) * P

    ctx = ExitStack()
    with ctx:
        def sb(name, shape, dt, c=ctx):
            return c.enter_context(nc.sbuf_tensor(name, shape, dt))

        def sem(name):
            return ctx.enter_context(nc.semaphore(name))

        xs = sb("xs", [P, NT, P], f32)
        hA = sb("hA", [P, NB, SP], f32)
        hF = sb("hF", [P, TOK], f32)
        lin_t = sb("lin_t", [P, TOK], f32)
        win_t = sb("win_t", [P, TOK], f32)
        vec = sb("vec", [P, 16], f32)
        wloc = sb("wloc", [P, 3 * P], f32)
        wm = sb("wm", [P, M_GATE + E], f32)
        rowb = sb("rowb", [P, 3, P], f32)
        row1 = sb("row1", [1, 3 * P], f32)
        ident = sb("ident", [P, P], f32)
        identh = sb("identh", [P, P], bf16)
        id64 = sb("id64", [P, 4, BQ], bf16)
        ones1 = sb("ones1", [1, P], f32)
        sel24 = sb("sel24", [SPLITS * 8, 8, P], bf16)
        st = sb("st", [P, NT, 16], f32)
        logit = sb("logit", [P, NT, E], f32)
        rt = sb("rt", [P, 7, NT, E], f32)
        r1 = sb("r1", [P, 8, NT], f32)
        wds = sb("wds", [P, NT, SPLITS * E], bf16)
        b1c = sb("b1c", [P, E * NC], f32)
        b2s = sb("b2s", [E, P], f32)
        small = sb("small", [P, 8], f32)

        win_ctx = ExitStack()
        def sw(name, shape, dt):
            return sb(name, shape, dt, win_ctx)
        xn = sw("xn", [P, 2, P], f32)
        z = sw("z", [P, 2, P], f32)
        part_ctx = ExitStack()
        qk32 = sb("qk32", [P, QK], f32, part_ctx)
        qks = sb("qks", [P, 2, SPLITS, QK], bf16, part_ctx)
        part_ctx.close()
        prob_ctx = ExitStack()
        pe = sb("pe", [P, 2, 1024], f32, prob_ctx)
        p1 = sb("p1", [P, 2, 1024], f16, prob_ctx)
        p2 = sb("p2", [P, 2, 1024], f16, prob_ctx)
        prob_ctx.close()
        part_room = sw("part_room", [P, QK + SPLITS * QK], f32)
        vres = sw("vres", [P, 512], f32)
        vaug = sw("vaug", [P, NB, NBLK, NPAIR, VW], bf16)
        qin = sw("qin", [P, NPAIR, S], bf16)
        qst = sw("qst", [P, 2, NPAIR, NBLK, 2 * BQ], bf16)
        kst = sw("kst", [P, 2, NPAIR, SP], bf16)
        bhm = sw("bhm", [P, NHEAD, P], bf16)
        blo = sw("blo", [88, NHEAD, P], bf16)
        bs = sw("bs", [P, NPAIR, P], bf16)
        mv = sw("mv", [88, 2, TOK], bf16)
        nm = sw("nm", [P, NBLK, NPAIR], f32)
        nmr = sw("nmr", [P, NBLK, NPAIR], f32)
        nms = sw("nms", [P, NBLK, SPLITS, NPAIR], bf16)
        ot = sw("ot", [P, NBLK, NPAIR, VG], f32)
        orec = sw("orec", [P, NBLK, NPAIR], f32)
        on = sw("on", [P, 2, NBLK, NPAIR * HD], f32)
        tab_ctx = ExitStack()
        tb = sb("tb", [P, NHEAD, P], f32, tab_ctx)
        tbr = lin_t[:, :].rearrange("p (h c) -> p h c", c=P)
        thi = sb("thi", [P, NHEAD, P], bf16, tab_ctx)
        tab_ctx.close()
        lin_ctx = ExitStack()
        lt = win_t[:, :].rearrange("p (k c) -> p k c", c=S)
        qlT = sb("qlT", [P, S], f32, lin_ctx)
        kl = sb("kl", [P, TB, P], f32, lin_ctx)
        vl = sb("vl", [P, TB, P + 1], f32, lin_ctx)
        kvs = sb("kvs", [P, P + 1], f32, lin_ctx)
        lrec = sb("lrec", [P, TB], f32, lin_ctx)
        ln_ = sb("ln_", [P, TB, P], f32, lin_ctx)
        lin_ctx.close()
        lgT = sw("lgT", [E, TOK], f32)
        win_ctx.close()

        gate_ctx = ExitStack()
        def sg(name, shape, dt):
            return sb(name, shape, dt, gate_ctx)
        wdT = sg("wdT", [SPLITS * E, TOK], bf16)
        wdTf = sg("wdTf", [E, TOK], f32)
        mix_ctx = ExitStack()
        gh = sb("gh", [P, 2, S], f32, mix_ctx)
        gg = sb("gg", [P, 2, S], f32, mix_ctx)
        gd = sb("gd", [P, 2, S], f32, mix_ctx)
        go = sb("go", [P, 2, S], f32, mix_ctx)
        mix_ctx.close()
        hid = sg("hid", [P, 2, NC, S], f32)
        hidh = sg("hidh", [P, 2, NC, S], f32r)
        hidl = sg("hidl", [P, 2, NC, S], f32r)
        w1r = sg("w1r", [P, 2, DF], f32)
        w2r = sg("w2r", [P, 2, NC, P], f32)
        w1h = sg("w1h", [P, 2, DF], f32r)
        w1l = sg("w1l", [P, 2, DF], f32r)
        w2h = sg("w2h", [P, 2, NC, P], f32r)
        w2l = sg("w2l", [P, 2, NC, P], f32r)
        ab = sg("ab", [P, 2, S], f32)
        abn = sg("abn", [P, NT, P + 1], f32)
        imix = sg("imix", [P, P + 1], f32)
        acc = sg("acc", [P, TOK], f32)
        hFh = sg("hFh", [P, TOK], f32r)
        hFl = sg("hFl", [P, TOK], f32r)
        wb = sg("wb", [P, 2, S], f32)
        ysc = sg("ysc", [P, 2, S], f32)
        bt = sg("bt", [P, NG, P], f32)
        pw = sg("pw", [P, 2, NG, P], f32)
        pwt = sg("pwt", [P, 2, NG, P], f32)
        mt = sg("mt", [P, 2, P], f32)
        rr = sg("rr", [P, P + 1], f32)
        dif = sg("dif", [P, 2, 2, P], f32)
        gl = sg("gl", [P, NT], f32)
        gs = sg("gs", [P, NT], f32)
        yo = sg("yo", [P, 2, 2, P], f32)
        gate_ctx.close()

        ps = ctx.enter_context(nc.psum_tensor("ps", [P, 8, 512], f32))

        names = """vecs_in wloc_in wmore_in rows_in rel_in b1_in
            consts_made ones_made rows_ps rowb_made dve_step act_step sqrt_done z_ready z_used zT_done hA_done hF_done
            pads_set stacks_set qk_ps qk32_done part1_done res1_done part2_done part3_done
            v_ps v1_done vres_done v2_done v3_done vaug_set
            lin_in_ps lin_q_made lin_kmin lin_exp lin_tiles_made kv_ps kv_made num_ps lin_nat_made lin_t_ps lin_t_made
            logit_ps logit_copied logitT_ps logit_made wds_made wdT_ps wdT_made
            band_masked thi_done tmid_done tables_made mv_set sel_made
            s_ps max_taken negmax_split negmaxT_ps negmaxT_done rel_turned
            st_ps p_done p1_done p2_done pv_ps pv_taken o_normed oT_ps oT_done
            gh_ps gh_done gate_ps gate_done mixed proj_ps proj_added
            abel_ps abel_done abn_ps abn_done base_made acc_ps acc_made
            w_split h_ps hid_done hidh_done hidl_done wb_ps wb_copied y_ps y_scaled y_added
            ex_ps ex_done non_ps dif_done gl_done gs_done yo_done imix_made expm_seed bank_free b1s small_made q_spread""".split()
        s = {n: sem(n) for n in names}
        x_in = [sem(f"x_in{b}") for b in range(NB)]
        scratch_out = [sem(f"scratch_out{b}") for b in range(NB)]
        stacks_in = [sem(f"stacks_in{i}") for i in range(2)]
        out_written = [sem(f"out_written{k}") for k in range(2)]
        w_in = [sem(f"w_in{i}") for i in range(2)]

        vcol = lambda i: vec[:, i:i + 1]
        wmat = lambda i: wm[:, i * P:(i + 1) * P]
        LN_GROUPS = [(0, TB), (TB, NT)]
        NU = E * NB

        block = ctx.enter_context(nc.Block())

        @block.sync
        def _(sp):
            for b in range(NB):
                sp.dma_start(xs[:, b * TB:(b + 1) * TB, :], x[b].rearrange("(t p) d -> p t d", p=P)).then_inc(x_in[b], 16)
                if b == 0:
                    sp.dma_start(vec[:, :], vecs).then_inc(s["vecs_in"], 16)
                    sp.dma_start(wloc[:, :], w_loc).then_inc(s["wloc_in"], 16)
            sp.dma_start(wm[:, :], w_more).then_inc(s["wmore_in"], 16)
            sp.dma_start(b1c[:, :], b1_cols).then_inc(s["b1_in"], 16)
            sp.dma_start(b2s[:, :], b2).then_inc(s["b1_in"], 16)
            sp.wait_ge(s["stacks_set"], 3)
            def parts_out(b):
                sp.wait_ge(s["part3_done"], b + 1)
                sp.dma_start(qk_scratch[b], qks[:, b % 2, :, :]).then_inc(scratch_out[b], 16)

            def stacks_back(b):
                sp.wait_ge(scratch_out[b], 16)
                if b >= 1:
                    sp.wait_ge(s["q_spread"], 2 * b)
                if b >= 2:
                    sp.wait_ge(s["st_ps"], 2 * NPAIR * (b - 1))
                for half in range(2):
                    for t in range(NTERM):
                        r0 = half * 64 + 8 * t
                        rows_of = qk_scratch[b][half * 64:(half + 1) * 64]
                        q_src = rows_of[:, QTERM[t], 0:S].rearrange("(p d) n -> d p n", d=HD)
                        k_src = rows_of[:, KTERM[t], S:QK].rearrange("(p d) n -> d p n", d=HD)
                        sp.dma_start(qin[r0:r0 + HD, :, :], q_src).then_inc(stacks_in[b % 2], 16)
                        sp.dma_start(kst[r0:r0 + HD, b % 2, :, :], k_src).then_inc(stacks_in[b % 2], 16)

            parts_out(0)
            stacks_back(0)
            for b in range(1, NB):
                parts_out(b)
            for b in range(1, NB):
                stacks_back(b)
            sp.wait_ge(s["oT_done"], 2 * NB)
            sp.wait_ge(s["p2_done"], 8 * NB)
            sp.wait_ge(s["pv_ps"], 8 * NB)
            for e in range(E):
                if e >= 2:
                    sp.wait_ge(s["w_split"], 4 * (e - 1))
                sp.dma_start(w1r[:, e % 2, :], w1[e]).then_inc(w_in[e % 2], 16)
                sp.dma_start(w2r[:, e % 2, :, :], w2[e].rearrange("(c p) d -> p c d", p=P)).then_inc(w_in[e % 2], 16)
            for i in range(NT // 2):
                sp.wait_ge(s["yo_done"], i + 1)
                b, t = divmod(2 * i, TB)
                sp.dma_start(out[b, t * P:(t + 2) * P, :].rearrange("(t p) d -> p t d", p=P),
                             yo[:, i % 2, :, :]).then_inc(out_written[i % 2], 16)
            for k in range(2):
                sp.wait_ge(out_written[k], 16 * (NT // 4))

        @block.gpsimd
        def _(pool):
            nc.gpsimd.memset(ident[:, :], 0.0).then_inc(s["consts_made"], 1)
            nc.gpsimd.memset(hA[:, :, 0:HALF], 0.0).then_inc(s["pads_set"], 1)
            nc.gpsimd.memset(hA[:, :, HALF + S:SP], 0.0).then_inc(s["pads_set"], 1)
            pool.wait_ge(s["consts_made"], 1)
            nc.gpsimd.affine_select(out=ident[:, :], in_=ident[:, :], compare_op=ALU.not_equal, fill=1.0,
                                    base=0, pattern=[[-1, P]], channel_multiplier=1).then_inc(s["consts_made"], 1)
            pool.dma_start(row1[:, :], rows).then_inc(s["rows_in"], 16)
            for half in range(2):
                src = bass.AP(tensor=rel_t.tensor, offset=0, ap=[[1, BQ], [rel_t.shape[1], NHEAD], [1, P]])
                pool.dma_start(tbr[half * 64:half * 64 + 64, :, :], src).then_inc(s["rel_in"], 16)
            nc.gpsimd.memset(sel24[:, :, :], 0.0).then_inc(s["sel_made"], 1)
            for k in range(SPLITS):
                pool.wait_ge(s["sel_made"], k + 1)
                nc.gpsimd.affine_select(out=sel24[:, :, :], in_=sel24[:, :, :], compare_op=ALU.not_equal, fill=1.0,
                                        base=-8 * k, pattern=[[-1, 8], [0, P]],
                                        channel_multiplier=1).then_inc(s["sel_made"], 1)
            pool.wait_ge(s["rel_turned"], 1)
            for half in range(2):
                t = tb[half * 64:half * 64 + 64, :, :]
                nc.gpsimd.affine_select(out=t, in_=t, compare_op=ALU.is_ge, fill=NEG, base=0,
                                        pattern=[[0, NHEAD], [1, P]], channel_multiplier=-1).then_inc(s["band_masked"], 1)
            for half in range(2):
                t = tb[half * 64:half * 64 + 64, :, :]
                pool.wait_ge(s["band_masked"], 2)
                nc.gpsimd.affine_select(out=t, in_=t, compare_op=ALU.is_ge, fill=NEG, base=2 * HALF,
                                        pattern=[[0, NHEAD], [-1, P]], channel_multiplier=1).then_inc(s["band_masked"], 1)

        @block.tensor
        def _(te):
            mm = nc.tensor.matmul

            te.wait_ge(s["rows_in"], 16)
            te.wait_ge(s["ones_made"], 1)
            mm(ps[:, 7, 0:3 * P], ones1[:, :], row1[:, :], start=True, stop=True).then_inc(s["rows_ps"], 1)
            te.wait_ge(s["consts_made"], 2)
            for b in range(NB):
                for t in range(TB):
                    te.wait_ge(s["z_ready"], b * TB + t + 1)
                    last = nc.tensor.transpose(ps[:, b, t * P:(t + 1) * P], z[:, (b * TB + t) % 2, :], ident[:, :])
                    last.then_inc(s["zT_done"], 1)

            te.wait_ge(s["wloc_in"], 16)
            te.wait_ge(s["pads_set"], 2)
            for b in range(NB):
                te.wait_ge(s["hA_done"], b + 1)
                if b >= 1:
                    te.wait_ge(s["qk32_done"], 2 * b)
                mm(ps[:, 4, :], wloc[:, 0:P], hA[:, b, HALF:HALF + S], start=True, stop=True)
                mm(ps[:, 5, 0:SP // 2], wloc[:, P:2 * P], hA[:, b, 0:SP // 2], start=True, stop=True)
                mm(ps[:, 6, 0:SP // 2], wloc[:, P:2 * P], hA[:, b, SP // 2:SP], start=True, stop=True).then_inc(s["qk_ps"], 1)
            te.wait_ge(s["rowb_made"], 1)
            te.wait_ge(s["hF_done"], 1)
            for j in range(2 * NB):
                b, g = divmod(j, 2)
                if j >= 2:
                    te.wait_ge(s["vres_done"], j - 1)
                bank = 7 if j % 2 == 0 else 0
                for i in range(4):
                    k0 = (4 * g + i) * BQ
                    last = mm(ps[:, bank, i * P:(i + 1) * P], hA[:, b, k0:k0 + P], wloc[:, 2 * P:3 * P], start=True, stop=True)
                last.then_inc(s["v_ps"], 1)

            te.wait_ge(s["wmore_in"], 16)
            te.wait_ge(s["qk32_done"], 2 * NB)
            te.wait_ge(s["hF_done"], NB)
            te.wait_ge(s["vres_done"], 2 * NB)
            for b in range(NB):
                if b >= 1:
                    te.wait_ge(s["lin_q_made"], b)
                    te.wait_ge(s["lin_kmin"], 2 * b)
                    te.wait_ge(s["lin_tiles_made"], b)
                mm(ps[:, 4, :], wmat(M_QLIN), hA[:, b, HALF:HALF + S], start=True, stop=True)
                for t in range(TB):
                    tok = hA[:, b, HALF + t * P:HALF + (t + 1) * P]
                    mm(ps[:, 5, t * P:(t + 1) * P], tok, wmat(M_KLIN), start=True, stop=True)
                    last = mm(ps[:, 6, t * P:(t + 1) * P], tok, wmat(M_VLIN), start=True, stop=True)
                last.then_inc(s["lin_in_ps"], 1)
                te.wait_ge(s["lin_tiles_made"], b + 1)
                if b >= 1:
                    te.wait_ge(s["kv_made"], b)
                for t in range(TB):
                    last = mm(ps[:, 7, 0:P + 1], kl[:, t, :], vl[:, t, :], start=(t == 0), stop=(t == TB - 1))
                last.then_inc(s["kv_ps"], 1)
                te.wait_ge(s["kv_made"], b + 1)
                if b >= 1:
                    te.wait_ge(s["lin_nat_made"], b)
                for t in range(TB):
                    last = mm(ps[:, t // 2, (t % 2) * (P + 1):(t % 2 + 1) * (P + 1)], qlT[:, t * P:(t + 1) * P],
                              kvs[:, :], start=True, stop=True)
                last.then_inc(s["num_ps"], 1)
                te.wait_ge(s["lin_nat_made"], b + 1)
                if b >= 1:
                    te.wait_ge(s["lin_t_made"], b)
                for t in range(TB):
                    last = nc.tensor.transpose(ps[:, 2, t * P:(t + 1) * P], ln_[:, t, :], ident[:, :])
                last.then_inc(s["lin_t_ps"], 1)
            for b in range(NB):
                if b >= 1:
                    te.wait_ge(s["logit_copied"], b)
                mm(ps[0:E, 3, :], wm[:, M_GATE:M_GATE + E], hF[:, b * S:(b + 1) * S],
                   start=True, stop=True).then_inc(s["logit_ps"], 1)
            te.wait_ge(s["logit_copied"], NB)
            for t in range(NT):
                last = nc.tensor.transpose(ps[:, 3, t * E:(t + 1) * E], lgT[:, t * P:(t + 1) * P], ident[0:E, 0:E])
            last.then_inc(s["logitT_ps"], 1)

            def scores_for_max(b):
                te.wait_ge(stacks_in[b % 2], 16 * 2 * 2 * NTERM * (b // 2 + 1))
                for p in range(NPAIR):
                    for g in range(2):
                        n = (b * NPAIR + p) * 2 + g
                        if n >= 2:
                            te.wait_ge(s["max_taken"], n - 1)
                        te.wait_ge(s["q_spread"], 2 * (b + 1))
                        mm(ps[:, g, :], identh[:, :], bs[:, p:p + 1, :].broadcast_to((P, 4, P)), start=True, stop=False)
                        for i in range(4):
                            k0 = (4 * g + i) * BQ
                            last = mm(ps[:, g, i * P:(i + 1) * P], qst[:, b % 2, p, 4 * g + i, :],
                                      kst[:, b % 2, p, k0:k0 + P], start=False, stop=(i == 3))
                        last.then_inc(s["s_ps"], 1)

            def negmax_rows(b):
                te.wait_ge(s["negmax_split"], b + 1)
                if b >= 1:
                    te.wait_ge(s["pv_taken"], NPAIR * b)
                tv = ps[:, 6, :].bitcast(bf16).rearrange("p (i c) -> p i c", c=P)
                for i in range(NBLK):
                    last = nc.tensor.transpose(tv[0:24, i, :], nms[:, i, :, :].rearrange("p a c -> p (a c)"), identh[:, :])
                last.then_inc(s["negmaxT_ps"], 1)

            def probabilities_and_values(b):
                for p in range(NPAIR):
                    n = b * NPAIR + p
                    k = 2 + 2 * (n % 2)
                    if n >= 2:
                        te.wait_ge(s["p1_done"], n - 1)
                    if p == 0:
                        te.wait_ge(s["negmaxT_done"], b + 1)
                    for g in range(2):
                        bank = ps[:, k + g, :]
                        for half in range(2):
                            h = 2 * p + half
                            o = bank[:, half * 256:(half + 1) * 256]
                            cols = b * S + g * 256
                            mm(o, bhm[:, h, :], id64[:, :, :].rearrange("p a c -> p (a c)"), start=(half == 0), stop=False)
                            mm(o, blo[:, h, :], mv[:, half, cols:cols + 256], start=False, stop=False)
                        ob = bank.rearrange("p (a i c) -> p a i c", a=2, c=BQ)
                        for i in range(4):
                            k0 = (4 * g + i) * BQ
                            last = mm(ob[:, :, i, :], kst[:, b % 2, p, k0:k0 + P], qst[:, b % 2, p, 4 * g + i, :],
                                      start=False, stop=(i == 3))
                        last.then_inc(s["st_ps"], 1)
                    if p >= 1:
                        values(b, p - 1)
                values(b, NPAIR - 1)

            def values(b, p):
                n = b * NPAIR + p
                if n >= 2:
                    te.wait_ge(s["pv_taken"], n - 1)
                if b >= 1 and p == 0:
                    te.wait_ge(s["oT_done"], 2 * b)
                te.wait_ge(s["p2_done"], n + 1)
                if p == 0:
                    te.wait_ge(s["v3_done"], 2 * (b + 1))
                    if b == 0:
                        te.wait_ge(s["vaug_set"], 1)
                for i in range(NBLK):
                    o = ps[:, 6 + p % 2, i * VW:(i + 1) * VW]
                    c = slice(i * P, (i + 1) * P)
                    mm(o, p1[:, n % 2, c], vaug[:, b, i, p, :], start=True, stop=False)
                    last = mm(o, p2[:, n % 2, c], vaug[:, b, i, p, :], start=False, stop=True)
                last.then_inc(s["pv_ps"], 1)

            def outputs_transposed(b):
                te.wait_ge(s["o_normed"], b + 1)
                if b + 1 < NB:
                    te.wait_ge(s["negmaxT_done"], b + 2)
                for j in range(2):
                    for i in range(4):
                        last = nc.tensor.transpose(ps[0:64, 6 + j, i * P:(i + 1) * P], on[:, b % 2, 4 * j + i, :], ident[:, :])
                    last.then_inc(s["oT_ps"], 1)

            te.wait_ge(s["lin_t_made"], NB)
            te.wait_ge(s["lin_nat_made"], NB)
            te.wait_ge(s["tables_made"], 4)
            te.wait_ge(s["mv_set"], 2)
            scores_for_max(0)
            negmax_rows(0)
            scores_for_max(1)
            for b in range(NB):
                probabilities_and_values(b)
                if b + 1 < NB:
                    negmax_rows(b + 1)
                if b + 2 < NB:
                    scores_for_max(b + 2)
                outputs_transposed(b)

            te.wait_ge(s["wds_made"], 1)
            te.wait_ge(s["max_taken"], 2 * NPAIR * NB)
            for b in range(NB):
                if b >= 1:
                    te.wait_ge(s["wdT_made"], 2 * b)
                for t in range(TB):
                    i = b * TB + t
                    nc.tensor.transpose(ps[:, 0, :].bitcast(bf16)[0:SPLITS * E, t * P:(t + 1) * P], wds[:, i, :], identh[:, :])
                    last = nc.tensor.transpose(ps[0:E, 1, t * P:(t + 1) * P], rt[:, 6, i, :], ident[:, :])
                last.then_inc(s["wdT_ps"], 1)

            te.wait_ge(s["oT_done"], 2 * NB)

            def gate_hidden(b):
                if b >= 2:
                    te.wait_ge(s["gh_done"], b - 1)
                c = slice(b * S, (b + 1) * S)
                o = ps[:, 2 + b % 2, :]
                mm(o, wmat(M_G1H), hA[:, b, HALF:HALF + S], start=True, stop=False)
                mm(o, wmat(M_G1LIN), lin_t[:, c], start=False, stop=False)
                mm(o, wmat(M_G1WIN), win_t[:, c], start=False, stop=True).then_inc(s["gh_ps"], 1)

            te.wait_ge(s["p1_done"], 8 * NB)
            gate_hidden(0)
            for b in range(NB):
                if b + 1 < NB:
                    gate_hidden(b + 1)
                te.wait_ge(s["gh_done"], b + 1)
                if b >= 2:
                    te.wait_ge(s["gate_done"], b - 1)
                mm(ps[:, 4 + b % 2, :], wmat(M_WG2), gh[:, b % 2, :], start=True, stop=True).then_inc(s["gate_ps"], 1)

            def project(b):
                te.wait_ge(s["mixed"], b + 1)
                if b >= 2:
                    te.wait_ge(s["proj_added"], b - 1)
                for t in range(TB):
                    last = mm(ps[:, 6 + b % 2, t * P:(t + 1) * P], go[:, b % 2, t * P:(t + 1) * P], wmat(M_WO), start=True, stop=True)
                last.then_inc(s["proj_ps"], 1)
            for b in range(NB):
                project(b)

            te.wait_ge(s["gh_done"], NB)
            te.wait_ge(s["gate_done"], NB)
            te.wait_ge(s["wdT_made"], 2 * NB)
            te.wait_ge(s["b1_in"], 32)
            te.wait_ge(s["imix_made"], 1)
            for b in range(NB):
                if b >= 2:
                    te.wait_ge(s["abel_done"], b - 1)
                    te.wait_ge(s["acc_made"], b - 1)
                c = slice(b * S, (b + 1) * S)
                mm(ps[:, 0 + b % 2, :], wmat(M_ABEL), hF[:, c], start=True, stop=True).then_inc(s["abel_ps"], 1)
                mm(ps[:, 2 + b % 2, :], b2s[:, :], wdTf[:, c], start=True, stop=True).then_inc(s["acc_ps"], 1)
                te.wait_ge(s["abel_done"], b + 1)
                for j in range(2):
                    n = 2 * b + j
                    if n >= 2:
                        te.wait_ge(s["abn_done"], n - 1)
                    for i in range(2):
                        t = 2 * j + i
                        last = mm(ps[:, 4 + j, i * (P + 1):(i + 1) * (P + 1)], ab[:, b % 2, t * P:(t + 1) * P],
                                  imix[:, :], start=True, stop=True)
                    last.then_inc(s["abn_ps"], 1)
            te.wait_ge(s["abn_done"], 2 * NB)
            te.wait_ge(s["acc_made"], NB)
            te.wait_ge(s["proj_added"], NB)

            def first_layer(u):
                e, g = divmod(u, NB)
                c = slice(g * S, (g + 1) * S)
                te.wait_ge(s["w_split"], 4 * (e + 1))
                for j in range(2):
                    if u >= 1:
                        te.wait_ge(s["hid_done"], 4 * (u - 1) + 2 * j + 2)
                    for ch in (2 * j, 2 * j + 1):
                        o = ps[:, ch, :]
                        w = slice(ch * P, (ch + 1) * P)
                        mm(o, w1h[:, e % 2, w], hFh[:, c], start=True, stop=False)
                        mm(o, w1h[:, e % 2, w], hFl[:, c], start=False, stop=False)
                        mm(o, w1l[:, e % 2, w], hFh[:, c], start=False, stop=True).then_inc(s["h_ps"], 1)
                if u >= 1:
                    te.wait_ge(s["wb_copied"], u)
                mm(ps[:, 7, :], sel24[:, e, :], wdT[:, c], start=True, stop=True).then_inc(s["wb_ps"], 1)

            def second_layer(u):
                e = u // NB
                if u >= 2:
                    te.wait_ge(s["y_scaled"], u - 1)
                o = ps[:, 4 + u % 2, :]
                for ch in range(NC):
                    if ch % 2 == 0:
                        te.wait_ge(s["hidl_done"], 2 * u + ch // 2 + 1)
                        te.wait_ge(s["hidh_done"], 2 * u + ch // 2 + 1)
                    mm(o, w2h[:, e % 2, ch, :], hidh[:, u % 2, ch, :], start=(ch == 0), stop=False)
                    mm(o, w2h[:, e % 2, ch, :], hidl[:, u % 2, ch, :], start=False, stop=False)
                    last = mm(o, w2l[:, e % 2, ch, :], hidh[:, u % 2, ch, :], start=False, stop=(ch == NC - 1))
                last.then_inc(s["y_ps"], 1)

            def expm_steps():
                gen = wm[:, M_GEN * P:(M_GEN + NG) * P].rearrange("p (i c) -> p i c", c=P)
                o = ps[:, 6, 0:NG * P].rearrange("p (i c) -> p i c", c=P)
                for i in range(NG):
                    yield_last = nc.tensor.transpose(o[:, i, :], gen[:, i, :], ident[:, :])
                yield yield_last
                k = 0
                for _ in range(EXPM_DEGREE - 1):
                    for i in range(NG):
                        last = mm(o[:, i, :], bt[:, i, :], pw[:, k % 2, i, :], start=True, stop=True)
                    yield last
                    k += 1
                for i in range(NG):
                    last = nc.tensor.transpose(o[:, i, :], pw[:, k % 2, i, :], ident[:, :])
                yield last
                kt = 0
                for _ in range(EXPM_SQUARINGS):
                    for i in range(NG):
                        last = mm(o[:, i, :], pwt[:, kt % 2, i, :], pw[:, k % 2, i, :], start=True, stop=True)
                    yield last
                    for i in range(NG):
                        last = mm(o[:, i, :], pw[:, k % 2, i, :], pwt[:, kt % 2, i, :], start=True, stop=True)
                    yield last
                    k += 1
                    kt += 1
                yield mm(o[:, 0, :], pw[:, k % 2, 1, :], pwt[:, kt % 2, 0, :], start=True, stop=True)
                mm(o[:, 0, :], mt[:, 0, :], pw[:, k % 2, 2, :], start=True, stop=True)
                yield mm(o[:, 1, :], pw[:, k % 2, 2, :], mt[:, 0, :], start=True, stop=True)
                yield mm(o[:, 0, 0:1], mt[:, 1, :], vcol(V_MIX2), start=True, stop=True)

            steps = expm_steps()
            n_ex = 0
            te.wait_ge(s["expm_seed"], 1)
            for u in range(NU + 1):
                if u < NU:
                    first_layer(u)
                if u >= 1:
                    second_layer(u - 1)
                if n_ex >= 1:
                    te.wait_ge(s["ex_done"], n_ex)
                step = next(steps, None)
                if step is not None:
                    step.then_inc(s["ex_ps"], 1)
                    n_ex += 1
            assert next(steps, None) is None

            te.wait_ge(s["ex_done"], n_ex)
            for i in range(NT // 2):
                te.wait_ge(s["y_added"], NU - NB + (2 * i) // TB + 1)
                if i >= 2:
                    te.wait_ge(s["yo_done"], i - 1)
                for j in range(2):
                    t = 2 * i + j
                    last = mm(ps[:, 0 + i % 2, j * (P + 1):(j + 1) * (P + 1)], acc[:, t * P:(t + 1) * P], rr[:, :],
                              start=True, stop=True)
                last.then_inc(s["non_ps"], 1)

        @block.scalar
        def _(act):
            A = nc.scalar.activation
            steps = [0]

            def link(ins):
                steps[0] += 1
                ins.then_inc(s["act_step"], 1)
                act.wait_ge(s["act_step"], steps[0])

            def roots(g):
                t0, t1 = LN_GROUPS[g]
                for n in range(2):
                    act.wait_ge(s["z_used"], 2 * g + n + 1)
                    A(st[:, t0:t1, 9], st[:, t0:t1, 8], ACT.Sqrt).then_inc(s["sqrt_done"], 1)

            def attention_input(b):
                act.wait_ge(s["zT_done"], TB * (b + 1))
                A(hA[:, b, HALF:HALF + S], ps[:, b, :], ACT.Identity, bias=vcol(V_B), scale=vcol(V_G)).then_inc(s["hA_done"], 1)

            roots(0)
            act.wait_ge(s["vecs_in"], 16)
            act.wait_ge(s["rows_ps"], 1)
            A(rowb[:, :, :].rearrange("p a c -> p (a c)"), ps[:, 7, 0:3 * P], ACT.Copy).then_inc(s["rowb_made"], 1)
            attention_input(0)
            roots(1)
            for b in range(1, NB):
                attention_input(b)
            act.wait_ge(s["small_made"], 1)
            for b in range(NB):
                act.wait_ge(s["qk_ps"], b + 1)
                if b >= 1:
                    act.wait_ge(s["res1_done"], b)
                A(qk32[:, 0:S], ps[:, 4, :], ACT.Identity, bias=small[:, 0:1], scale=SCALE).then_inc(s["qk32_done"], 1)
                A(qk32[:, S:QK].rearrange("p (a c) -> p a c", a=2), ps[:, 5:7, 0:SP // 2], ACT.Identity,
                  bias=vcol(V_BKLOC)).then_inc(s["qk32_done"], 1)
                act.wait_ge(s["qk32_done"], 2 * (b + 1))
                if b >= 2:
                    act.wait_ge(scratch_out[b - 2], 16)
                A(qks[:, b % 2, 0, :], qk32[:, :], ACT.Copy).then_inc(s["part1_done"], 1)
                act.wait_ge(s["res1_done"], b + 1)
                A(qks[:, b % 2, 1, :], qk32[:, :], ACT.Copy).then_inc(s["part2_done"], 1)
                if b + 1 < NB:
                    act.wait_ge(s["part3_done"], b + 1)
            act.wait_ge(s["vaug_set"], 1)
            for j in range(2 * NB):
                b, g = divmod(j, 2)
                bank = 7 if j % 2 == 0 else 0
                act.wait_ge(s["v_ps"], j + 1)
                va = vaug[:, b, 4 * g:4 * g + 4, :, :].rearrange("p i n c -> p (i n) c")
                part = lambda k: va[:, :, k * 2 * VG:(k + 1) * 2 * VG].rearrange("p n (h d) -> p n h d", h=2)[:, :, :, 0:HD]
                A(part(0), ps[:, bank, :].rearrange("p (n h d) -> p n h d", h=2, d=HD), ACT.Copy).then_inc(s["v1_done"], 1)
                act.wait_ge(s["vres_done"], j + 1)
                A(part(1), vres[:, :].rearrange("p (n h d) -> p n h d", h=2, d=HD), ACT.Copy).then_inc(s["v2_done"], 1)
            act.wait_ge(s["band_masked"], 4)
            A(thi[:, :, :], tb[:, :, :], ACT.Copy).then_inc(s["thi_done"], 1)
            act.wait_ge(s["tmid_done"], 1)
            A(thi[:, :, :], tbr[:, :, :], ACT.Copy).then_inc(s["thi_done"], 1)
            act.wait_ge(s["tables_made"], 4)
            for b in range(NB):
                act.wait_ge(s["lin_in_ps"], b + 1)
                if b >= 1:
                    act.wait_ge(s["num_ps"], b)
                A(lt[:, 0, :], ps[:, 4, :], ACT.Identity, bias=vcol(V_BQLIN)).then_inc(s["lin_q_made"], 1)
                act.wait_ge(s["lin_kmin"], 2 * b + 2)
                A(lt[:, 2:4, :], lt[:, 2:4, :], ACT.Exp).then_inc(s["lin_exp"], 1)
                act.wait_ge(s["kv_ps"], b + 1)
                A(kvs[:, :], ps[:, 7, 0:P + 1], ACT.Copy).then_inc(s["kv_made"], 1)
                act.wait_ge(s["lin_t_ps"], b + 1)
                A(lin_t[:, b * S:(b + 1) * S], ps[:, 2, :], ACT.Copy).then_inc(s["lin_t_made"], 1)
            for b in range(NB):
                act.wait_ge(s["logit_ps"], b + 1)
                A(lgT[:, b * S:(b + 1) * S], ps[0:E, 3, :], ACT.Identity, bias=vec[0:E, V_GATEB:V_GATEB + 1]).then_inc(s["logit_copied"], 1)
            act.wait_ge(s["b1s"], 1)
            A(r1[:, 4, :], r1[:, 3, :], ACT.Exp).then_inc(s["b1s"], 1)
            act.wait_ge(s["part3_done"], NB)
            for b in range(NB):
                act.wait_ge(scratch_out[b], 16)
            for n in range(NPAIR * NB):
                k = 2 + 2 * (n % 2)
                act.wait_ge(s["st_ps"], 2 * (n + 1))
                if n >= 2:
                    act.wait_ge(s["p2_done"], n - 1)
                    act.wait_ge(s["pv_ps"], n - 1)
                src = ps[:, k:k + 2, :].rearrange("p g (a i c) -> p g i a c", a=2, c=BQ)
                for buf, done in ((pe, "p_done"), (p1, "p1_done")):
                    for g in range(2):
                        last = A(buf[:, n % 2, g * 512:(g + 1) * 512].rearrange("p (i a c) -> p i a c", a=2, c=BQ),
                                 src[:, g], ACT.Exp, bias=small[:, 1:2])
                    last.then_inc(s[done], 1)
            for b in range(NB):
                act.wait_ge(s["wdT_ps"], b + 1)
                A(wdT[:, b * S:(b + 1) * S], ps[:, 0, :].bitcast(bf16)[0:SPLITS * E, 0:S], ACT.Copy).then_inc(s["wdT_made"], 1)
                A(wdTf[:, b * S:(b + 1) * S], ps[0:E, 1, :], ACT.Copy).then_inc(s["wdT_made"], 1)
            def gate_relu(b):
                act.wait_ge(s["gh_ps"], b + 1)
                if b >= 2:
                    act.wait_ge(s["gate_ps"], b - 1)
                A(gh[:, b % 2, :], ps[:, 2 + b % 2, :], ACT.Relu, bias=vcol(V_BG1)).then_inc(s["gh_done"], 1)
            gate_relu(0)
            for b in range(NB):
                if b + 1 < NB:
                    gate_relu(b + 1)
                act.wait_ge(s["gate_ps"], b + 1)
                if b >= 2:
                    act.wait_ge(s["mixed"], b - 1)
                A(gg[:, b % 2, :], ps[:, 4 + b % 2, :], ACT.Sigmoid, bias=vcol(V_BG2)).then_inc(s["gate_done"], 1)
            for b in range(NB):
                act.wait_ge(s["acc_ps"], b + 1)
                A(acc[:, b * S:(b + 1) * S], ps[:, 2 + b % 2, :], ACT.Copy).then_inc(s["acc_made"], 1)
                if b >= 2:
                    act.wait_ge(s["abn_ps"], 2 * (b - 1))
                A(ab[:, b % 2, :], ps[:, 0 + b % 2, :], ACT.Gelu, bias=vcol(V_ABEL)).then_inc(s["abel_done"], 1)
                for j in range(2):
                    n = 2 * b + j
                    act.wait_ge(s["abn_ps"], n + 1)
                    A(abn[:, 2 * n:2 * n + 2, :].rearrange("p t c -> p (t c)"), ps[:, 4 + j, 0:2 * (P + 1)], ACT.Copy).then_inc(s["abn_done"], 1)
            for u in range(NU):
                e = u // NB
                if u >= 2:
                    act.wait_ge(s["y_ps"], u - 1)
                    act.wait_ge(s["hidl_done"], 2 * (u - 1))
                for j in range(2):
                    for ch in (2 * j, 2 * j + 1):
                        act.wait_ge(s["h_ps"], NC * u + ch + 1)
                        A(hid[:, u % 2, ch, :], ps[:, ch, :], ACT.Gelu, bias=b1c[:, e * NC + ch:e * NC + ch + 1]).then_inc(s["hid_done"], 1)
                    act.wait_ge(s["hid_done"], NC * u + 2 * j + 2)
                    c = slice(2 * j, 2 * j + 2)
                    A(hidh[:, u % 2, c, :], hid[:, u % 2, c, :], ACT.Copy).then_inc(s["hidh_done"], 1)
                act.wait_ge(s["wb_ps"], u + 1)
                if u >= 2:
                    act.wait_ge(s["y_scaled"], u - 1)
                A(wb[:, u % 2, :], ps[:, 7, :], ACT.Copy).then_inc(s["wb_copied"], 1)
            for i in range(NT // 2):
                act.wait_ge(s["gl_done"], i + 1)
                A(gs[:, 2 * i:2 * i + 2], gl[:, 2 * i:2 * i + 2], ACT.Sigmoid, bias=vcol(V_MIXB)).then_inc(s["gs_done"], 1)

        @block.vector
        def _(dve):
            V = nc.vector
            steps = [0]

            def link(ins):
                steps[0] += 1
                ins.then_inc(s["dve_step"], 1)
                dve.wait_ge(s["dve_step"], steps[0])

            def rsqrt(v, root, r, t, n, g):
                dve.wait_ge(s["sqrt_done"], 2 * g + n + 1)
                link(V.reciprocal(r, root))
                link(V.tensor_tensor(t, r, r, ALU.mult))
                link(V.tensor_tensor(t, t, v, ALU.mult))
                link(V.tensor_scalar(t, t, -0.5, 1.5, ALU.mult, ALU.add))
                link(V.tensor_tensor(r, r, t, ALU.mult))

            V.memset(ones1[:, :], 1.0).then_inc(s["ones_made"], 1)
            for g, (t0, t1) in enumerate(LN_GROUPS):
                for t in range(t0, t1):
                    if t % TB == 0:
                        dve.wait_ge(x_in[t // TB], 16)
                    link(V.bn_stats(st[:, t, 0:6], xs[:, t, :]))
                    link(V.bn_aggr(st[:, t, 6:8], st[:, t, 0:6]))
                mean, var, ve, root = (st[:, t0:t1, i] for i in (6, 7, 8, 9))
                ra, rb, tmp, w2_ = (st[:, t0:t1, i] for i in (10, 11, 12, 13))
                V.tensor_scalar(ve, var, EPS, None, ALU.add).then_inc(s["z_used"], 1)
                dve.wait_ge(s["z_used"], 2 * g + 1)
                rsqrt(ve, root, ra, tmp, 0, g)
                link(V.tensor_tensor(tmp, ra, ra, ALU.mult))
                link(V.tensor_tensor(tmp, tmp, var, ALU.mult))
                V.tensor_scalar(ve, tmp, EPS, None, ALU.add).then_inc(s["z_used"], 1)
                dve.wait_ge(s["z_used"], 2 * g + 2)
                rsqrt(ve, root, rb, tmp, 1, g)
                for t in range(t0, t1):
                    if t >= 2:
                        dve.wait_ge(s["zT_done"], t - 1)
                    link(V.tensor_scalar(xn[:, t % 2, :], xs[:, t, :], st[:, t, 6:7], st[:, t, 10:11], ALU.subtract, ALU.mult))
                    V.tensor_scalar(z[:, t % 2, :], xn[:, t % 2, :], st[:, t, 11:12], None, ALU.mult).then_inc(s["z_ready"], 1)
                    link(V.scalar_tensor_tensor(xs[:, t, :], xn[:, t % 2, :], 2.0, xs[:, t, :], ALU.mult, ALU.add))
                    if t % TB == TB - 1:
                        b = t // TB
                        if b == 0:
                            dve.wait_ge(s["vecs_in"], 16)
                            V.memset(small[:, 1:2], P_SHIFT)
                            V.tensor_scalar(small[:, 0:1], vcol(V_BQLOC), SCALE, None, ALU.mult).then_inc(s["small_made"], 1)
                        dve.wait_ge(s["hA_done"], b + 1)
                        V.tensor_scalar(hF[:, b * S:(b + 1) * S], ps[:, b, :], vcol(V_FG), vcol(V_FB), ALU.mult, ALU.add).then_inc(s["hF_done"], 1)
            V.memset(qst[:, :, :, :, :], 0.0)
            for half in range(2):
                o = 64 * half
                V.memset(qin[o + 32:o + 64, :, :], 1.0)
                link(V.memset(kst[o + 32:o + 64, :, :, :], 0.0))
                V.memset(kst[o + 32:o + 64, :, :, 0:HALF], NEG / 16)
                V.memset(kst[o + 32:o + 64, :, :, HALF + S:SP], NEG / 16).then_inc(s["stacks_set"], 1)
            link(V.memset(vaug[:, :, :, :, :], 0.0))
            va = vaug[:, :, :, :, :].rearrange("p b i n c -> p (b i n) c")
            V.memset(va[:, :, HD:2 * VG:VG], 1.0).then_inc(s["vaug_set"], 1)
            V.tensor_copy(identh[:, :], ident[:, :]).then_inc(s["stacks_set"], 1)
            dve.wait_ge(s["rel_in"], 32)
            turned = bass.AP(tensor=lin_t, offset=P - 1, ap=[[TOK, P], [P, NHEAD], [-1, P]])
            V.tensor_copy(tb[:, :, :], turned).then_inc(s["rel_turned"], 1)
            for b in range(NB):
                dve.wait_ge(s["part1_done"], b + 1)
                V.tensor_tensor(qk32[:, :], qk32[:, :], qks[:, b % 2, 0, :], ALU.subtract).then_inc(s["res1_done"], 1)
                dve.wait_ge(s["part2_done"], b + 1)
                V.tensor_tensor(qks[:, b % 2, 2, :], qk32[:, :], qks[:, b % 2, 1, :], ALU.subtract).then_inc(s["part3_done"], 1)
            for j in range(2 * NB):
                b, g = divmod(j, 2)
                bank = 7 if j % 2 == 0 else 0
                va = vaug[:, b, 4 * g:4 * g + 4, :, :].rearrange("p i n c -> p (i n) c")
                part = lambda k: va[:, :, k * 2 * VG:(k + 1) * 2 * VG].rearrange("p n (h d) -> p n h d", h=2)[:, :, :, 0:HD]
                r4 = vres[:, :].rearrange("p (n h d) -> p n h d", h=2, d=HD)
                dve.wait_ge(s["v1_done"], j + 1)
                if j >= 1:
                    dve.wait_ge(s["v3_done"], j)
                V.tensor_tensor(r4, ps[:, bank, :].rearrange("p (n h d) -> p n h d", h=2, d=HD), part(0), ALU.subtract).then_inc(s["vres_done"], 1)
                dve.wait_ge(s["v2_done"], j + 1)
                V.tensor_tensor(part(2), r4, part(1), ALU.subtract).then_inc(s["v3_done"], 1)
            dve.wait_ge(s["thi_done"], 1)
            V.tensor_copy(bhm[0:64, :, :], thi[0:64, :, :])
            th = thi[:, :, :].rearrange("p (n a) c -> p n a c", a=2)
            for half in range(2):
                V.tensor_copy(bs[64 * half:64 * half + 64, :, :], th[64 * half:64 * half + 64, :, half, :])
            V.tensor_tensor(tbr[:, :, :], tb[:, :, :], thi[:, :, :], ALU.subtract).then_inc(s["tmid_done"], 1)
            dve.wait_ge(s["thi_done"], 2)
            V.tensor_copy(bhm[64:128, :, :], thi[64:128, :, :]).then_inc(s["tables_made"], 1)
            V.tensor_tensor(blo[0:64, :, :], tbr[0:64, :, :], thi[0:64, :, :], ALU.subtract).then_inc(s["tables_made"], 1)
            dve.wait_ge(s["sel_made"], 1 + SPLITS)
            for half in range(2):
                V.tensor_copy(blo[64:88, :, :].rearrange("p (n a) c -> p n a c", a=2)[:, :, half, :], sel24[:, :, :]).then_inc(s["tables_made"], 1)
            for half in range(2):
                o = 64 * half
                link(V.tensor_copy(id64[o:o + 64, :, :], ident[o:o + 64, o:o + 64].rearrange("p (a c) -> p a c", a=1).broadcast_to((64, 4, BQ))))
            for half in range(2):
                V.tensor_copy(mv[0:64, half, :].rearrange("p (n c) -> p n c", c=BQ),
                              ident[0:64, 0:BQ].rearrange("p (a c) -> p a c", a=1).broadcast_to((64, TOK // BQ, BQ))).then_inc(s["mv_set"], 1)
            for b in range(NB):
                dve.wait_ge(s["lin_in_ps"], b + 1)
                if b >= 1:
                    dve.wait_ge(s["num_ps"], b)
                bc = lambda i: rowb[:, i:i + 1, :].broadcast_to((P, TB, P))
                link(V.tensor_tensor(lt[:, 1, :].rearrange("p (t c) -> p t c", c=P), ps[:, 5, :].rearrange("p (t c) -> p t c", c=P), bc(0), ALU.add))
                V.tensor_tensor(vl[:, :, 0:P], ps[:, 6, :].rearrange("p (t c) -> p t c", c=P), bc(1), ALU.add)
                V.memset(vl[:, :, P:P + 1], 1.0)
                V.tensor_scalar(lt[:, 2, :], lt[:, 1, :], 0.0, None, ALU.min).then_inc(s["lin_kmin"], 1)
                dve.wait_ge(s["lin_q_made"], b + 1)
                V.tensor_scalar(lt[:, 3, :], lt[:, 0, :], 0.0, None, ALU.min).then_inc(s["lin_kmin"], 1)
                dve.wait_ge(s["lin_exp"], b + 1)
                V.scalar_tensor_tensor(qlT[:, :], lt[:, 0, :], 0.0, lt[:, 3, :], ALU.max, ALU.add)
                V.scalar_tensor_tensor(kl[:, :, :].rearrange("p t c -> p (t c)"), lt[:, 1, :], 0.0, lt[:, 2, :], ALU.max, ALU.add).then_inc(s["lin_tiles_made"], 1)
                dve.wait_ge(s["num_ps"], b + 1)
                nat = ps[:, 0:2, 0:2 * (P + 1)].rearrange("p g (t c) -> p g t c", c=P + 1)
                l4 = ln_[:, :, :].rearrange("p (g t) c -> p g t c", g=2)
                link(V.tensor_scalar(lrec[:, :].rearrange("p (g t) -> p g t", g=2), nat[:, :, :, P], 1e-6, None, ALU.add))
                link(V.reciprocal(lrec[:, :], lrec[:, :]))
                if b >= 1:
                    dve.wait_ge(s["lin_t_ps"], b)
                for t in range(TB):
                    last = V.tensor_scalar(ln_[:, t, :], nat[:, t // 2, t % 2, 0:P], lrec[:, t:t + 1], None, ALU.mult)
                last.then_inc(s["lin_nat_made"], 1)
            dve.wait_ge(s["logitT_ps"], 1)
            L = lambda i: rt[:, i, :, :]
            R = lambda i: r1[:, i, :]
            col = lambda a: a.rearrange("p (t c) -> p t c", c=1).broadcast_to((P, NT, E))
            link(V.tensor_copy(logit[:, :, :].rearrange("p t e -> p (t e)"), ps[:, 3, 0:NT * E]))
            for e in range(E):
                last = V.memset(rt[:, 0, :, e], float(e) - 100.0)
            link(last)
            src = logit[:, :, :]
            for k in range(2):
                m, first = R(k), L(1 + k)
                link(V.tensor_reduce(m, src, AX.X, ALU.max))
                link(V.tensor_tensor(L(3), src, col(m), ALU.is_equal))
                link(V.tensor_tensor(L(4), L(3), L(0), ALU.mult))
                link(V.tensor_reduce(R(2), L(4), AX.X, ALU.min))
                link(V.tensor_tensor(first, L(4), col(R(2)), ALU.is_equal))
                if k == 0:
                    link(V.tensor_scalar(L(3), first, -3e38, None, ALU.mult))
                    link(V.tensor_tensor(L(5), src, L(3), ALU.add))
                    src = L(5)
            V.tensor_tensor(R(3), R(1), R(0), ALU.subtract).then_inc(s["b1s"], 1)
            dve.wait_ge(s["b1s"], 2)
            link(V.tensor_scalar(R(5), R(4), 1.0, None, ALU.add))
            link(V.reciprocal(R(6), R(5)))
            link(V.tensor_tensor(R(7), R(4), R(6), ALU.mult))
            link(V.tensor_tensor(L(3), L(1), col(R(6)), ALU.mult))
            link(V.tensor_tensor(L(4), L(2), col(R(7)), ALU.mult))
            link(V.tensor_tensor(L(6), L(3), L(4), ALU.add))
            link(V.tensor_copy(wds[:, :, 0:E], L(6)))
            link(V.tensor_tensor(L(5), L(6), wds[:, :, 0:E], ALU.subtract))
            link(V.tensor_copy(wds[:, :, E:2 * E], L(5)))
            V.tensor_tensor(wds[:, :, 2 * E:3 * E], L(5), wds[:, :, E:2 * E], ALU.subtract).then_inc(s["wds_made"], 1)

            def take_max(b, p):
                for g in range(2):
                    n = (b * NPAIR + p) * 2 + g
                    dve.wait_ge(s["s_ps"], n + 1)
                    if b >= 1 and p == 0 and g == 0:
                        dve.wait_ge(s["negmax_split"], b)
                    V.tensor_reduce(nm[:, 4 * g:4 * g + 4, p], ps[:, g, :].rearrange("p (i c) -> p i c", c=P),
                                    AX.X, ALU.max, negate=True).then_inc(s["max_taken"], 1)

            def split_max(b):
                dve.wait_ge(s["max_taken"], 2 * NPAIR * (b + 1))
                if b >= 1:
                    dve.wait_ge(s["negmaxT_ps"], b)
                link(V.tensor_copy(nms[:, :, 0, :], nm[:, :, :]))
                link(V.tensor_tensor(nmr[:, :, :], nm[:, :, :], nms[:, :, 0, :], ALU.subtract))
                link(V.tensor_copy(nms[:, :, 1, :], nmr[:, :, :]))
                V.tensor_tensor(nms[:, :, 2, :], nmr[:, :, :], nms[:, :, 1, :], ALU.subtract).then_inc(s["negmax_split"], 1)

            def negmax_rows(b):
                dve.wait_ge(s["negmaxT_ps"], b + 1)
                tv = ps[:, 6, :].bitcast(bf16).rearrange("p (i a c) -> p i a c", a=2, c=BQ)
                for half in range(2):
                    last = V.tensor_copy(mv[64:88, half, b * S:(b + 1) * S].rearrange("p (i c) -> p i c", c=BQ), tv[0:24, :, half, :])
                last.then_inc(s["negmaxT_done"], 1)

            def take_values(n):
                b, p = divmod(n, NPAIR)
                dve.wait_ge(s["pv_ps"], n + 1)
                if p == 0 and b >= 1:
                    dve.wait_ge(s["o_normed"], b)
                for half in range(2):
                    o = 64 * half
                    src = ps[o:o + 64, 6 + p % 2, 0:NBLK * VW].rearrange("p (i k a c) -> p i a c k", i=NBLK, k=SPLITS, a=2)
                    last = V.tensor_reduce(ot[o:o + 64, :, p, :], src[:, :, half, :, :], AX.X, ALU.add)
                last.then_inc(s["pv_taken"], 1)

            def normalise(b):
                dve.wait_ge(s["pv_taken"], NPAIR * (b + 1))
                o3 = ot[:, :, :, :].rearrange("p i n c -> p (i n) c")
                link(V.reciprocal(orec[:, :, :].rearrange("p i n -> p (i n)"), o3[:, :, HD]))
                if b >= 2:
                    dve.wait_ge(s["oT_ps"], 2 * (b - 1))
                V.tensor_tensor(on[:, b % 2, :, :].rearrange("p i (n c) -> p (i n) c", c=HD), o3[:, :, 0:HD],
                                orec[:, :, :].rearrange("p i (n c) -> p (i n) c", c=1).broadcast_to((P, NBLK * NPAIR, HD)),
                                ALU.mult).then_inc(s["o_normed"], 1)

            def outputs_transposed(b):
                for j in range(2):
                    dve.wait_ge(s["oT_ps"], 2 * b + j + 1)
                    src = ps[0:64, 6 + j, :].rearrange("p (i a c) -> p i a c", a=2, c=BQ)
                    for half in range(2):
                        dst = win_t[64 * half:64 * half + 64, b * S + 256 * j:b * S + 256 * (j + 1)].rearrange("p (i c) -> p i c", c=BQ)
                        last = V.tensor_scalar(dst, src[:, :, half, :], vec[0:64, V_BV0 + half:V_BV0 + half + 1], None, ALU.add)
                    last.then_inc(s["oT_done"], 1)

            def spread(b):
                dve.wait_ge(stacks_in[b % 2], 16 * 2 * 2 * NTERM * (b // 2 + 1))
                if b >= 2:
                    dve.wait_ge(s["st_ps"], 8 * 2 * (b - 1))
                for half in range(2):
                    o = 64 * half
                    V.tensor_copy(qst[o:o + 64, b % 2, :, :, o:o + BQ].rearrange("p n i c -> p (n i) c"),
                                  qin[o:o + 64, :, :].rearrange("p n (i c) -> p (n i) c", c=BQ)).then_inc(s["q_spread"], 1)

            spread(0)
            for p in range(NPAIR):
                take_max(0, p)
            split_max(0)
            negmax_rows(0)
            spread(1)
            for p in range(NPAIR):
                take_max(1, p)
            split_max(1)
            for b in range(NB):
                for p in range(NPAIR):
                    n = b * NPAIR + p
                    dve.wait_ge(s["p_done"], n + 1)
                    dve.wait_ge(s["p1_done"], n + 1)
                    if n >= 2:
                        dve.wait_ge(s["pv_ps"], n - 1)
                    V.tensor_tensor(p2[:, n % 2, :], pe[:, n % 2, :], p1[:, n % 2, :], ALU.subtract).then_inc(s["p2_done"], 1)
                    if p >= 1:
                        take_values(n - 1)
                take_values(b * NPAIR + NPAIR - 1)
                normalise(b)
                if b + 1 < NB:
                    negmax_rows(b + 1)
                if b + 2 < NB:
                    spread(b + 2)
                    for p in range(NPAIR):
                        take_max(b + 2, p)
                    split_max(b + 2)
                outputs_transposed(b)

            dve.wait_ge(s["oT_done"], 2 * NB)
            for b in range(NB):
                c = slice(b * S, (b + 1) * S)
                if b >= 2:
                    dve.wait_ge(s["proj_ps"], b - 1)
                link(V.tensor_tensor(gd[:, b % 2, :], lin_t[:, c], win_t[:, c], ALU.subtract))
                dve.wait_ge(s["gate_done"], b + 1)
                link(V.tensor_tensor(gd[:, b % 2, :], gd[:, b % 2, :], gg[:, b % 2, :], ALU.mult))
                V.tensor_tensor(go[:, b % 2, :], gd[:, b % 2, :], win_t[:, c], ALU.add).then_inc(s["mixed"], 1)
            for b in range(NB):
                t = slice(b * TB, (b + 1) * TB)
                dve.wait_ge(s["proj_ps"], b + 1)
                link(V.tensor_tensor(xs[:, t, :], xs[:, t, :], ps[:, 6 + b % 2, :].rearrange("p (t c) -> p t c", c=P), ALU.add))
                V.tensor_tensor(xs[:, t, :], xs[:, t, :], rowb[:, 2:3, :].broadcast_to((P, TB, P)), ALU.add).then_inc(s["proj_added"], 1)
            V.tensor_copy(imix[:, 0:P], ident[:, :])
            V.tensor_copy(imix[:, P:P + 1], vcol(V_MIX1)).then_inc(s["imix_made"], 1)

            link(V.tensor_copy(hFh[:, :], hF[:, :]))
            V.tensor_tensor(hFl[:, :], hF[:, :], hFh[:, :].bitcast(f32), ALU.subtract)

            def split_weights(e):
                k = e % 2
                dve.wait_ge(w_in[k], 32 * (e // 2 + 1))
                if e >= 2:
                    dve.wait_ge(s["y_ps"], NB * (e - 1))
                V.tensor_copy(w1h[:, k, :], w1r[:, k, :]).then_inc(s["w_split"], 1)
                V.tensor_copy(w2h[:, k, :, :], w2r[:, k, :, :]).then_inc(s["w_split"], 1)
                dve.wait_ge(s["w_split"], 4 * e + 2)
                V.tensor_tensor(w1l[:, k, :], w1r[:, k, :], w1h[:, k, :].bitcast(f32), ALU.subtract).then_inc(s["w_split"], 1)
                V.tensor_tensor(w2l[:, k, :, :], w2r[:, k, :, :], w2h[:, k, :, :].bitcast(f32), ALU.subtract).then_inc(s["w_split"], 1)

            split_weights(0)
            for b in range(NB):
                dve.wait_ge(s["abn_done"], 2 * (b + 1))
                if b == 0:
                    dve.wait_ge(s["proj_added"], NB)
                t = slice(b * TB, (b + 1) * TB)
                V.tensor_tensor(xs[:, t, :], xs[:, t, :], abn[:, t, 0:P], ALU.add).then_inc(s["base_made"], 1)

            gen = wm[:, M_GEN * P:(M_GEN + NG) * P].rearrange("p (i c) -> p i c", c=P)
            down = 2.0 ** -EXPM_SQUARINGS
            for i in range(NG):
                last = V.scalar_tensor_tensor(pw[:, 0, i, :], gen[:, i, :], down / EXPM_DEGREE, ident[:, :], ALU.mult, ALU.add)
            last.then_inc(s["expm_seed"], 1)

            def expm_steps():
                o = ps[:, 6, 0:NG * P].rearrange("p (i c) -> p i c", c=P)
                yield V.tensor_scalar(bt[:, :, :], o, down, None, ALU.mult)
                k = 0
                for d in range(EXPM_DEGREE - 1, 0, -1):
                    for i in range(NG):
                        last = V.scalar_tensor_tensor(pw[:, (k + 1) % 2, i, :], o[:, i, :], 1.0 / d, ident[:, :], ALU.mult, ALU.add)
                    yield last
                    k += 1
                yield V.tensor_copy(pwt[:, 0, :, :], o)
                kt = 0
                for _ in range(EXPM_SQUARINGS):
                    yield V.tensor_copy(pw[:, (k + 1) % 2, :, :], o)
                    yield V.tensor_copy(pwt[:, (kt + 1) % 2, :, :], o)
                    k += 1
                    kt += 1
                yield V.tensor_copy(mt[:, 0, :], o[:, 0, :])
                V.tensor_copy(rr[:, 0:P], o[:, 0, :])
                yield V.tensor_copy(mt[:, 1, :], o[:, 1, :])
                yield V.tensor_copy(rr[:, P:P + 1], o[:, 0, 0:1])

            def add_expert(u):
                c = slice((u % NB) * S, (u % NB + 1) * S)
                dve.wait_ge(s["y_ps"], u + 1)
                dve.wait_ge(s["wb_copied"], u + 1)
                if u == 0:
                    dve.wait_ge(s["acc_made"], NB)
                V.tensor_tensor(ysc[:, u % 2, :], ps[:, 4 + u % 2, :], wb[:, u % 2, :], ALU.mult).then_inc(s["y_scaled"], 1)
                dve.wait_ge(s["y_scaled"], u + 1)
                V.tensor_tensor(acc[:, c], acc[:, c], ysc[:, u % 2, :], ALU.add).then_inc(s["y_added"], 1)

            steps_ = expm_steps()
            n_ex = 0
            for u in range(NU):
                for j in range(2):
                    dve.wait_ge(s["hidh_done"], 2 * u + j + 1)
                    c = slice(2 * j, 2 * j + 2)
                    if u >= 2:
                        dve.wait_ge(s["y_ps"], u - 1)
                    V.tensor_tensor(hidl[:, u % 2, c, :], hid[:, u % 2, c, :], hidh[:, u % 2, c, :].bitcast(f32),
                                    ALU.subtract).then_inc(s["hidl_done"], 1)
                if u >= 1:
                    add_expert(u - 1)
                if n_ex < 20:
                    dve.wait_ge(s["ex_ps"], n_ex + 1)
                    step = next(steps_, None)
                    step.then_inc(s["ex_done"], 1)
                    n_ex += 1
                if u % NB == 1 and u // NB + 1 < E:
                    split_weights(u // NB + 1)
            assert next(steps_, None) is None
            add_expert(NU - 1)

            for i in range(NT // 2):
                k = i % 2
                t = slice(2 * i, 2 * i + 2)
                dve.wait_ge(s["non_ps"], i + 1)
                if i == 0:
                    dve.wait_ge(s["base_made"], NB)
                n2 = ps[:, k, 0:2 * (P + 1)].rearrange("p (t c) -> p t c", c=P + 1)
                V.tensor_tensor(gl[:, t], n2[:, :, P], abn[:, t, P], ALU.add).then_inc(s["gl_done"], 1)
                link(V.tensor_tensor(dif[:, k, :, :], n2[:, :, 0:P], abn[:, t, 0:P], ALU.subtract))
                dve.wait_ge(s["gs_done"], i + 1)
                if i >= 2:
                    dve.wait_ge(out_written[k], 16 * (i // 2))
                for j in range(2):
                    last = V.scalar_tensor_tensor(yo[:, k, j, :], dif[:, k, j, :], gs[:, 2 * i + j:2 * i + j + 1],
                                                  xs[:, 2 * i + j, :], ALU.mult, ALU.add)
                last.then_inc(s["yo_done"], 1)


def kernel(**inputs):
    import numpy as np
    import concourse.bacc as bacc
    from concourse import mybir as mb
    from concourse.bass_utils import run_bass_kernel_spmd

    a = {k: np.ascontiguousarray(v) for k, v in inputs.items()}
    at = lambda n: a["L0_attn_" + n]
    ff = lambda n: a["L0_ffn_" + n]
    D, HD, NPAIR = 128, 8, 8
    perm = np.arange(D).reshape(NPAIR, 2, HD).transpose(1, 0, 2).reshape(D)
    bv = at("bv_loc")[perm]
    cols = [at("bq_lin"), at("bq_loc")[perm], at("bk_loc")[perm], bv, np.roll(bv, -64), at("bg1"), at("bg2")[perm],
            at("ln_g"), at("ln_b"), ff("ln_g"), ff("ln_b"), ff("abel_b"), ff("mix_w")[0:D, 0], ff("mix_w")[D:2 * D, 0],
            np.repeat(ff("mix_b"), D), np.pad(ff("gate_b_moe"), (0, D - 8))]
    wg1 = at("wg1")
    rel = at("rel_bias")
    rel_t = np.zeros((rel.shape[1], 192), rel.dtype)
    rel_t[:, 31:31 + rel.shape[0]] = rel.T[:, ::-1]
    gens = ff("gens")
    b1 = ff("b1")
    arrays = {
        "x": a["L0_attn_x"],
        "vecs": np.stack(cols, axis=1),
        "rows": np.concatenate([at("bk_lin"), at("bv_lin")[perm], at("bo")])[None, :],
        "w_loc": np.concatenate([at("wq_loc")[:, perm], at("wk_loc")[:, perm], at("wv_loc")], axis=1),
        "w_more": np.concatenate([at("wq_lin"), at("wk_lin"), at("wv_lin")[:, perm], at("wo")[perm, :],
                                  wg1[0:D][perm, :], wg1[D:2 * D][perm, :], wg1[2 * D:], at("wg2")[:, perm],
                                  ff("abel_w"), gens[0], gens[1], gens[2], ff("gate_w_moe")], axis=1),
        "rel_t": rel_t,
        "b1_cols": b1.reshape(b1.shape[0], -1, D).transpose(2, 0, 1).reshape(D, -1),
        "b2": ff("b2"), "w1": ff("w1"), "w2": ff("w2"),
    }
    arrays = {"in_" + k: np.ascontiguousarray(v) for k, v in arrays.items()}
    nc = bacc.Bacc("TRN2", target_bir_lowering=False, num_devices=1)
    args = {k: nc.dram_tensor(k, v.shape, mb.dt.from_np(v.dtype), kind="ExternalInput").ap() for k, v in arrays.items()}
    g = lambda n: args["in_" + n]
    scratch = nc.dram_tensor("qk_scratch", [4, D, 3, 512 + 576], mb.dt.bfloat16, kind="Internal").ap()
    out = nc.dram_tensor("out_0_dram", (4, 512, D), mb.dt.float32, kind="ExternalOutput").ap()
    attention_and_moe_block(nc, g("x"), g("vecs"), g("rows"), g("w_loc"), g("w_more"), g("rel_t"), g("b1_cols"),
                            g("b2"), g("w1"), g("w2"), scratch, out)
    r = run_bass_kernel_spmd(nc, [arrays], core_ids=[0])
    return r.results[0]["out_0_dram"]
```

```python
import concourse.bass as bass
from concourse import mybir
from contextlib import ExitStack


def attention_and_moe_block(nc, x, vecs, rows, w_loc, w_more, rel_t, b1_cols, b2, w1, w2,
                            qk_scratch, out):
    f32, f32r, bf16, f16 = mybir.dt.float32, mybir.dt.float32r, mybir.dt.bfloat16, mybir.dt.float16
    ALU, ACT, AX = mybir.AluOpType, mybir.ActivationFunctionType, mybir.AxisListType

    P = 128
    NB, S, D = x.shape
    TB = S // P
    NT = NB * TB
    TOK = NB * S
    E, _, DF = w1.shape
    NC = DF // P
    NHEAD, HD = 16, 8
    NPAIR = NHEAD // 2
    HALF = 32
    BQ = 64
    NBLK = S // BQ
    SP = S + 2 * HALF
    QK = S + SP
    SPLITS = 3
    QTERM = [0, 0, 0, 1, 1, 2]
    KTERM = [0, 1, 2, 0, 1, 0]
    NTERM = len(QTERM)
    VG = HD + 1
    VW = SPLITS * 2 * VG
    NEG = -1e30
    EPS = 1e-5
    SCALE = float(HD) ** -0.5
    P_SHIFT = 12 * 0.6931471805599453
    EXPM_SQUARINGS, EXPM_DEGREE = 4, 8
    NG = 3

    (V_BQLIN, V_BQLOC, V_BKLOC, V_BV0, V_BV1, V_BG1, V_BG2, V_G, V_B, V_FG, V_FB, V_ABEL,
     V_MIX1, V_MIX2, V_MIXB, V_GATEB) = range(16)
    (M_QLIN, M_KLIN, M_VLIN, M_WO, M_G1LIN, M_G1WIN, M_G1H, M_WG2, M_ABEL, M_GEN) = range(10)
    M_GATE = (M_GEN + NG) * P

    ctx = ExitStack()
    with ctx:
        def sb(name, shape, dt, c=ctx):
            return c.enter_context(nc.sbuf_tensor(name, shape, dt))

        def sem(name):
            return ctx.enter_context(nc.semaphore(name))

        xs = sb("xs", [P, NT, P], f32)
        hA = sb("hA", [P, NB, SP], f32)
        hF = sb("hF", [P, TOK], f32)
        lin_t = sb("lin_t", [P, TOK], f32)
        win_t = sb("win_t", [P, TOK], f32)
        vec = sb("vec", [P, 16], f32)
        wloc = sb("wloc", [P, 3 * P], f32)
        wm = sb("wm", [P, M_GATE + E], f32)
        rowb = sb("rowb", [P, 3, P], f32)
        row1 = sb("row1", [1, 3 * P], f32)
        ident = sb("ident", [P, P], f32)
        identh = sb("identh", [P, P], bf16)
        id64 = sb("id64", [P, 4, BQ], bf16)
        ones1 = sb("ones1", [1, P], f32)
        sel24 = sb("sel24", [SPLITS * 8, 8, P], bf16)
        st = sb("st", [P, NT, 16], f32)
        logit = sb("logit", [P, NT, E], f32)
        rt = sb("rt", [P, 7, NT, E], f32)
        r1 = sb("r1", [P, 8, NT], f32)
        wds = sb("wds", [P, NT, SPLITS * E], bf16)
        b1c = sb("b1c", [P, E * NC], f32)
        b2s = sb("b2s", [E, P], f32)
        small = sb("small", [P, 8], f32)

        win_ctx = ExitStack()
        def sw(name, shape, dt):
            return sb(name, shape, dt, win_ctx)
        on = sw("on", [P, NBLK, NPAIR * HD], f32)
        z = on[:, :, :].rearrange("p i c -> p (i c)").rearrange("p (t c) -> p t c", c=P)
        part_ctx = ExitStack()
        qk32 = sb("qk32", [P, QK], f32, part_ctx)
        qks = sb("qks", [P, 2, SPLITS, QK], bf16, part_ctx)
        part_ctx.close()
        prob_ctx = ExitStack()
        pe = sb("pe", [P, 2, 1024], f32, prob_ctx)
        p1 = sb("p1", [P, 2, 1024], f16, prob_ctx)
        p2 = sb("p2", [P, 2, 1024], f16, prob_ctx)
        prob_ctx.close()
        part_room = sw("part_room", [P, QK + SPLITS * QK], f32)
        vaug = sw("vaug", [P, NB, NBLK, NPAIR, VW], bf16)
        qin = sw("qin", [P, NPAIR, S], bf16)
        qst = sw("qst", [P, 2, NPAIR, NBLK, 2 * BQ], bf16)
        kst = sw("kst", [P, 3, NPAIR, SP], bf16)
        bhm = sw("bhm", [P, NHEAD, P], bf16)
        blo = sw("blo", [88, NHEAD, P], bf16)
        bs = sw("bs", [P, NPAIR, P], bf16)
        mv = sw("mv", [88, 2, TOK], bf16)
        nm = sw("nm", [P, NBLK, NPAIR], f32)
        nmr = sw("nmr", [P, NBLK, NPAIR], f32)
        nms = sw("nms", [P, NBLK, SPLITS, NPAIR], bf16)
        ot = sw("ot", [P, NBLK, NPAIR, VG], f32)
        vres = ot[:, :, :, :].rearrange("p i n c -> p (i n c)")[:, 0:4 * P]
        orec = sw("orec", [P, NBLK, NPAIR], f32)
        tab_ctx = ExitStack()
        thi = sb("thi", [P, NHEAD, P], bf16, tab_ctx)
        tb = win_t[:, :].rearrange("p (h c) -> p h c", c=P)
        tbr = lin_t[:, :].rearrange("p (h c) -> p h c", c=P)
        tab_ctx.close()
        lgT_ctx = ExitStack()
        lgT = sb("lgT", [E, TOK], f32, lgT_ctx)
        lgT_ctx.close()
        lt = sw("lt", [P, 2, S], f32)
        ln_ = lt[:, 0, :].rearrange("p (t c) -> p t c", c=P)
        qlT = sw("qlT", [P, S], f32)
        kl = sw("kl", [P, TB, P], f32)
        vl = sw("vl", [P, TB, P + 1], f32)
        kvs = sw("kvs", [P, P + 1], f32)
        lrec = sw("lrec", [P, TB], f32)
        win_ctx.close()

        gate_ctx = ExitStack()
        def sg(name, shape, dt):
            return sb(name, shape, dt, gate_ctx)
        wdT = sg("wdT", [SPLITS * E, TOK], bf16)
        wdTf = sg("wdTf", [E, TOK], f32)
        mix_ctx = ExitStack()
        gh = sb("gh", [P, 2, S], f32, mix_ctx)
        gg = sb("gg", [P, 2, S], f32, mix_ctx)
        gd = sb("gd", [P, 2, S], f32, mix_ctx)
        go = sb("go", [P, 2, S], f32, mix_ctx)
        mix_ctx.close()
        hid = sg("hid", [P, 2, NC, S], f32)
        hidh = sg("hidh", [P, 2, NC, S], f32r)
        hidl = sg("hidl", [P, 2, NC, S], f32r)
        w1r = sg("w1r", [P, 2, DF], f32)
        w2r = sg("w2r", [P, 2, NC, P], f32)
        w1h = sg("w1h", [P, 2, DF], f32r)
        w1l = sg("w1l", [P, 2, DF], f32r)
        w2h = sg("w2h", [P, 2, NC, P], f32r)
        w2l = sg("w2l", [P, 2, NC, P], f32r)
        ab = sg("ab", [P, 2, S], f32)
        abn = sg("abn", [P, NT, P + 1], f32)
        imix = sg("imix", [P, P + 1], f32)
        acc = sg("acc", [P, TOK], f32)
        hFh = sg("hFh", [P, TOK], f32r)
        hFl = sg("hFl", [P, TOK], f32r)
        wb = sg("wb", [P, 2, S], f32)
        ysc = sg("ysc", [P, 2, S], f32)
        bt = sg("bt", [P, NG, P], f32)
        pw = sg("pw", [P, 2, NG, P], f32)
        pwt = sg("pwt", [P, 2, NG, P], f32)
        mt = sg("mt", [P, 2, P], f32)
        rr = sg("rr", [P, P + 1], f32)
        dif = sg("dif", [P, 2, 2, P], f32)
        gl = sg("gl", [P, NT], f32)
        gs = sg("gs", [P, NT], f32)
        yo = sg("yo", [P, 2, 2, P], f32)
        gate_ctx.close()

        ps = ctx.enter_context(nc.psum_tensor("ps", [P, 8, 512], f32))

        names = """vecs_in wloc_in wmore_in rows_in rel_in b1_in
            consts_made ones_made rows_ps rowb_made dve_step act_step sqrt_done z_ready z_used zT_done hA_done hF_done
            pads_set stacks_set qk_ps qk32_done part1_done res1_done part2_done part3_done
            v_ps v1_done vres_done v2_done v3_done vaug_set
            lin_ps lin_free lin_min lin_exp lin_q_made lin_k_made vl_ones
            logit_ps logit_copied logitT_ps logit_made wds_made wdT_ps wdT_made
            band_masked thi_done tmid_done tables_made mv_set sel_made
            s_ps max_taken negmax_split negmaxT_ps negmaxT_done rel_turned
            st_ps p_done p1_done p2_done pv_ps pv_taken o_normed oT_ps oT_done
            gh_ps gh_done gate_ps gate_done mixed proj_ps proj_added
            abel_ps abel_done abn_ps abn_done base_made acc_ps acc_made
            w_split h_ps hid_done hidh_done hidl_done wb_ps wb_copied y_ps y_scaled y_added
            ex_ps ex_done non_ps dif_done gl_done gs_done yo_done imix_made expm_seed bank_free b1s small_made q_spread identh_made""".split()
        s = {n: sem(n) for n in names}
        x_in = [sem(f"x_in{b}") for b in range(NB)]
        scratch_out = [sem(f"scratch_out{b}") for b in range(NB)]
        q_in = [sem(f"q_in{b}") for b in range(NB)]
        k_in = [sem(f"k_in{b}") for b in range(NB)]
        out_written = [sem(f"out_written{k}") for k in range(2)]
        w_in = [sem(f"w_in{i}") for i in range(2)]

        vcol = lambda i: vec[:, i:i + 1]
        wmat = lambda i: wm[:, i * P:(i + 1) * P]
        AHEAD = [[0, 1], [2], [3], [4], [5], [6], [7], []]
        LIN_STEPS = 7

        LN_GROUPS = [(0, TB), (TB, NT)]
        NU = E * NB

        block = ctx.enter_context(nc.Block())

        @block.sync
        def _(sp):
            for b in range(NB):
                sp.dma_start(xs[:, b * TB:(b + 1) * TB, :], x[b].rearrange("(t p) d -> p t d", p=P)).then_inc(x_in[b], 16)
                if b == 0:
                    sp.dma_start(vec[:, :], vecs).then_inc(s["vecs_in"], 16)
                    sp.dma_start(wloc[:, :], w_loc).then_inc(s["wloc_in"], 16)
            sp.dma_start(wm[:, :], w_more).then_inc(s["wmore_in"], 16)
            sp.dma_start(b1c[:, :], b1_cols).then_inc(s["b1_in"], 16)
            sp.dma_start(b2s[:, :], b2).then_inc(s["b1_in"], 16)
            sp.wait_ge(s["stacks_set"], 7)
            def parts_out(b):
                sp.wait_ge(s["part3_done"], b + 1)
                sp.dma_start(qk_scratch[b], qks[:, b % 2, :, :]).then_inc(scratch_out[b], 16)

            def rows_back(b, terms, c0, c1, dst, done):
                for half in range(2):
                    for t in range(NTERM):
                        r0 = half * 64 + 8 * t
                        src = qk_scratch[b][half * 64:(half + 1) * 64, terms[t], c0:c1].rearrange("(p d) n -> d p n", d=HD)
                        sp.dma_start(dst[r0:r0 + HD], src).then_inc(done[b], 16)

            def q_back(b):
                sp.wait_ge(scratch_out[b], 16)
                if b >= 1:
                    sp.wait_ge(s["q_spread"], 8 * b)
                rows_back(b, QTERM, 0, S, qin, q_in)

            def k_back(b):
                sp.wait_ge(scratch_out[b], 16)
                if b >= 3:
                    sp.wait_ge(s["st_ps"], 2 * NPAIR * (b - 2))
                rows_back(b, KTERM, S, QK, kst[:, b % 3], k_in)

            parts_out(0)
            q_back(0)
            k_back(0)
            for b in range(1, 3):
                parts_out(b)
                k_back(b)
            parts_out(3)
            q_back(1)
            q_back(2)
            k_back(3)
            q_back(3)
            sp.wait_ge(s["oT_done"], 2 * NB)
            sp.wait_ge(s["p2_done"], 8 * NB)
            sp.wait_ge(s["pv_ps"], 8 * NB)
            for e in range(E):
                if e >= 2:
                    sp.wait_ge(s["w_split"], 4 * (e - 1))
                sp.dma_start(w1r[:, e % 2, :], w1[e]).then_inc(w_in[e % 2], 16)
                sp.dma_start(w2r[:, e % 2, :, :], w2[e].rearrange("(c p) d -> p c d", p=P)).then_inc(w_in[e % 2], 16)
            for i in range(NT // 2):
                sp.wait_ge(s["yo_done"], i + 1)
                b, t = divmod(2 * i, TB)
                sp.dma_start(out[b, t * P:(t + 2) * P, :].rearrange("(t p) d -> p t d", p=P),
                             yo[:, i % 2, :, :]).then_inc(out_written[i % 2], 16)
            for k in range(2):
                sp.wait_ge(out_written[k], 16 * (NT // 4))

        @block.gpsimd
        def _(pool):
            nc.gpsimd.memset(ident[:, :], 0.0).then_inc(s["consts_made"], 1)
            nc.gpsimd.memset(hA[:, :, 0:HALF], 0.0).then_inc(s["pads_set"], 1)
            nc.gpsimd.memset(hA[:, :, HALF + S:SP], 0.0).then_inc(s["pads_set"], 1)
            pool.wait_ge(s["consts_made"], 1)
            nc.gpsimd.affine_select(out=ident[:, :], in_=ident[:, :], compare_op=ALU.not_equal, fill=1.0,
                                    base=0, pattern=[[-1, P]], channel_multiplier=1).then_inc(s["consts_made"], 1)
            nc.gpsimd.memset(kst[:, :, :, :], 0.0).then_inc(s["pads_set"], 1)
            pool.wait_ge(s["pads_set"], 3)
            for half in range(2):
                o = 64 * half
                nc.gpsimd.memset(kst[o + 32:o + 64, :, :, 0:HALF], NEG / 16).then_inc(s["stacks_set"], 1)
                nc.gpsimd.memset(kst[o + 32:o + 64, :, :, HALF + S:SP], NEG / 16).then_inc(s["stacks_set"], 1)
                nc.gpsimd.memset(qin[o + 32:o + 64, :, :], 1.0).then_inc(s["stacks_set"], 1)
            pool.wait_ge(s["stacks_set"], 6)
            nc.gpsimd.memset(qst[:, :, :, :, :], 0.0).then_inc(s["stacks_set"], 1)
            pool.wait_ge(s["stacks_set"], 7)
            pool.dma_start(row1[:, :], rows).then_inc(s["rows_in"], 16)
            for half in range(2):
                src = bass.AP(tensor=rel_t.tensor, offset=0, ap=[[1, BQ], [rel_t.shape[1], NHEAD], [1, P]])
                pool.dma_start(tbr[half * 64:half * 64 + 64, :, :], src).then_inc(s["rel_in"], 16)
            nc.gpsimd.memset(sel24[:, :, :], 0.0).then_inc(s["sel_made"], 1)
            for k in range(SPLITS):
                pool.wait_ge(s["sel_made"], k + 1)
                nc.gpsimd.affine_select(out=sel24[:, :, :], in_=sel24[:, :, :], compare_op=ALU.not_equal, fill=1.0,
                                        base=-8 * k, pattern=[[-1, 8], [0, P]],
                                        channel_multiplier=1).then_inc(s["sel_made"], 1)
            pool.wait_ge(s["rel_turned"], 1)
            for half in range(2):
                t = tb[half * 64:half * 64 + 64, :, :]
                nc.gpsimd.affine_select(out=t, in_=t, compare_op=ALU.is_ge, fill=NEG, base=0,
                                        pattern=[[0, NHEAD], [1, P]], channel_multiplier=-1).then_inc(s["band_masked"], 1)
            for half in range(2):
                t = tb[half * 64:half * 64 + 64, :, :]
                pool.wait_ge(s["band_masked"], 2)
                nc.gpsimd.affine_select(out=t, in_=t, compare_op=ALU.is_ge, fill=NEG, base=2 * HALF,
                                        pattern=[[0, NHEAD], [-1, P]], channel_multiplier=1).then_inc(s["band_masked"], 1)

        @block.tensor
        def _(te):
            mm = nc.tensor.matmul

            te.wait_ge(s["rows_in"], 16)
            te.wait_ge(s["ones_made"], 1)
            mm(ps[:, 7, 0:3 * P], ones1[:, :], row1[:, :], start=True, stop=True).then_inc(s["rows_ps"], 1)
            te.wait_ge(s["consts_made"], 2)
            for b in range(NB):
                for t in range(TB):
                    te.wait_ge(s["z_ready"], b * TB + t + 1)
                    last = nc.tensor.transpose(ps[:, b, t * P:(t + 1) * P], z[:, t, :], ident[:, :])
                    last.then_inc(s["zT_done"], 1)

            te.wait_ge(s["wloc_in"], 16)
            te.wait_ge(s["pads_set"], 2)
            te.wait_ge(s["rowb_made"], 1)
            te.wait_ge(s["hF_done"], 1)
            for b in range(NB):
                te.wait_ge(s["hA_done"], b + 1)
                if b >= 1:
                    te.wait_ge(s["qk32_done"], 2 * b)
                mm(ps[:, 4, :], wloc[:, 0:P], hA[:, b, HALF:HALF + S], start=True, stop=True)
                mm(ps[:, 5, 0:SP // 2], wloc[:, P:2 * P], hA[:, b, 0:SP // 2], start=True, stop=True)
                mm(ps[:, 6, 0:SP // 2], wloc[:, P:2 * P], hA[:, b, SP // 2:SP], start=True, stop=True).then_inc(s["qk_ps"], 1)
                for g in range(2):
                    j = 2 * b + g
                    if j >= 2:
                        te.wait_ge(s["vres_done"], j - 1)
                    for i in range(4):
                        k0 = (4 * g + i) * BQ
                        last = mm(ps[:, 7 * (1 - g), i * P:(i + 1) * P], hA[:, b, k0:k0 + P], wloc[:, 2 * P:3 * P], start=True, stop=True)
                    last.then_inc(s["v_ps"], 1)

            te.wait_ge(s["wmore_in"], 16)
            te.wait_ge(s["hF_done"], NB)
            for b in range(NB):
                if b >= 1:
                    te.wait_ge(s["logit_copied"], b)
                mm(ps[0:E, 3, :], wm[:, M_GATE:M_GATE + E], hF[:, b * S:(b + 1) * S],
                   start=True, stop=True).then_inc(s["logit_ps"], 1)
            te.wait_ge(s["logit_copied"], NB)
            for t in range(NT):
                last = nc.tensor.transpose(ps[:, 3, t * E:(t + 1) * E], lgT[:, t * P:(t + 1) * P], ident[0:E, 0:E])
            last.then_inc(s["logitT_ps"], 1)

            def scores_for_max(b, p):
                if p % 2 == 0:
                    te.wait_ge(s["q_spread"], 8 * b + p + 2)
                if p == 0:
                    te.wait_ge(k_in[b], 16 * 2 * NTERM)
                    if b >= 1:
                        te.wait_ge(s["negmaxT_done"], b)
                for g in range(2):
                    n = (b * NPAIR + p) * 2 + g
                    if n >= 2:
                        te.wait_ge(s["max_taken"], n - 1)
                    mm(ps[:, g, :], identh[:, :], bs[:, p:p + 1, :].broadcast_to((P, 4, P)), start=True, stop=False)
                    for i in range(4):
                        k0 = (4 * g + i) * BQ
                        last = mm(ps[:, g, i * P:(i + 1) * P], qst[:, b % 2, p, 4 * g + i, :],
                                  kst[:, b % 3, p, k0:k0 + P], start=False, stop=(i == 3))
                    last.then_inc(s["s_ps"], 1)

            def negmax_rows(b):
                te.wait_ge(s["negmax_split"], b + 1)
                tv = ps[:, 0, :].bitcast(bf16).rearrange("p (i c) -> p i c", c=P)
                for i in range(NBLK):
                    last = nc.tensor.transpose(tv[0:24, i, :], nms[:, i, :, :].rearrange("p a c -> p (a c)"), identh[:, :])
                last.then_inc(s["negmaxT_ps"], 1)

            def scores_for_exp(b, p):
                for g in range(2):
                    m = 2 * (b * NPAIR + p) + g
                    if m >= 3:
                        te.wait_ge(s["p1_done"], m - 2)
                    bank = ps[:, 2 + m % 3, :]
                    for half in range(2):
                        h = 2 * p + half
                        o = bank[:, half * 256:(half + 1) * 256]
                        cols = b * S + g * 256
                        mm(o, bhm[:, h, :], id64[:, :, :].rearrange("p a c -> p (a c)"), start=(half == 0), stop=False)
                        mm(o, blo[:, h, :], mv[:, half, cols:cols + 256], start=False, stop=False)
                    ob = bank.rearrange("p (a i c) -> p a i c", a=2, c=BQ)
                    for i in range(4):
                        k0 = (4 * g + i) * BQ
                        last = mm(ob[:, :, i, :], kst[:, b % 3, p, k0:k0 + P], qst[:, b % 2, p, 4 * g + i, :],
                                  start=False, stop=(i == 3))
                    last.then_inc(s["st_ps"], 1)

            def values(b, p):
                n = b * NPAIR + p
                if n >= 2:
                    te.wait_ge(s["pv_taken"], n - 1)
                if b >= 1 and p == 0:
                    te.wait_ge(s["oT_done"], 2 * b)
                te.wait_ge(s["p2_done"], n + 1)
                for i in range(NBLK):
                    o = ps[:, 6 + p % 2, i * VW:(i + 1) * VW]
                    c = slice(i * P, (i + 1) * P)
                    mm(o, p1[:, n % 2, c], vaug[:, b, i, p, :], start=True, stop=False)
                    last = mm(o, p2[:, n % 2, c], vaug[:, b, i, p, :], start=False, stop=True)
                last.then_inc(s["pv_ps"], 1)

            def outputs_transposed(b):
                te.wait_ge(s["o_normed"], b + 1)
                for j in range(2):
                    for i in range(4):
                        last = nc.tensor.transpose(ps[0:64, 6 + j, i * P:(i + 1) * P], on[:, 4 * j + i, :], ident[:, :])
                    last.then_inc(s["oT_ps"], 1)

            def linear(k):
                b, j = divmod(k, LIN_STEPS)
                if b >= NB:
                    return
                if k >= 1:
                    te.wait_ge(s["lin_free"], k)
                tok = lambda t: hA[:, b, HALF + t * P:HALF + (t + 1) * P]
                o = ps[:, 5, :]
                if j == 0:
                    last = mm(o, wmat(M_QLIN), hA[:, b, HALF:HALF + S], start=True, stop=True)
                elif j in (1, 2):
                    for t in range(TB):
                        last = mm(o[:, t * P:(t + 1) * P], tok(t), wmat(M_KLIN if j == 1 else M_VLIN), start=True, stop=True)
                elif j == 3:
                    te.wait_ge(s["lin_k_made"], b + 1)
                    for t in range(TB):
                        last = mm(o[:, 0:P + 1], kl[:, t, :], vl[:, t, :], start=(t == 0), stop=(t == TB - 1))
                elif j in (4, 5):
                    te.wait_ge(s["lin_q_made"], b + 1)
                    for i in range(2):
                        t = 2 * (j - 4) + i
                        last = mm(o[:, i * (P + 1):(i + 1) * (P + 1)], qlT[:, t * P:(t + 1) * P], kvs[:, :], start=True, stop=True)
                else:
                    for t in range(TB):
                        last = nc.tensor.transpose(o[:, t * P:(t + 1) * P], ln_[:, t, :], ident[:, :])
                last.then_inc(s["lin_ps"], 1)

            te.wait_ge(s["tables_made"], 4)
            te.wait_ge(s["mv_set"], 2)
            te.wait_ge(s["stacks_set"], 7)
            te.wait_ge(s["identh_made"], 1)
            te.wait_ge(s["vl_ones"], 1)
            te.wait_ge(s["vres_done"], 2 * NB)
            te.wait_ge(s["v3_done"], 2 * NB)
            te.wait_ge(s["vaug_set"], 1)
            te.wait_ge(s["qk32_done"], 2 * NB)
            for p in range(NPAIR):
                scores_for_max(0, p)
            negmax_rows(0)
            for b in range(NB):
                for p in range(NPAIR):
                    if p == 0:
                        te.wait_ge(s["negmaxT_done"], b + 1)
                    scores_for_exp(b, p)
                    if b + 1 < NB:
                        for q in AHEAD[p]:
                            scores_for_max(b + 1, q)
                        if p == NPAIR - 1:
                            negmax_rows(b + 1)
                    if p >= 1:
                        values(b, p - 1)
                    elif b >= 1:
                        outputs_transposed(b - 1)
                    linear(b * NPAIR + p)
                values(b, NPAIR - 1)
            outputs_transposed(NB - 1)

            te.wait_ge(s["wds_made"], 1)
            te.wait_ge(s["max_taken"], 2 * NPAIR * NB)
            for b in range(NB):
                if b >= 1:
                    te.wait_ge(s["wdT_made"], 2 * b)
                for t in range(TB):
                    i = b * TB + t
                    nc.tensor.transpose(ps[:, 0, :].bitcast(bf16)[0:SPLITS * E, t * P:(t + 1) * P], wds[:, i, :], identh[:, :])
                    last = nc.tensor.transpose(ps[0:E, 1, t * P:(t + 1) * P], rt[:, 6, i, :], ident[:, :])
                last.then_inc(s["wdT_ps"], 1)

            te.wait_ge(s["oT_done"], 2 * NB)

            def gate_hidden(b):
                if b >= 2:
                    te.wait_ge(s["gh_done"], b - 1)
                c = slice(b * S, (b + 1) * S)
                o = ps[:, 2 + b % 2, :]
                mm(o, wmat(M_G1H), hA[:, b, HALF:HALF + S], start=True, stop=False)
                mm(o, wmat(M_G1LIN), lin_t[:, c], start=False, stop=False)
                mm(o, wmat(M_G1WIN), win_t[:, c], start=False, stop=True).then_inc(s["gh_ps"], 1)

            te.wait_ge(s["p1_done"], 2 * NPAIR * NB)
            te.wait_ge(s["lin_free"], LIN_STEPS * NB)
            gate_hidden(0)
            for b in range(NB):
                if b + 1 < NB:
                    gate_hidden(b + 1)
                te.wait_ge(s["gh_done"], b + 1)
                if b >= 2:
                    te.wait_ge(s["gate_done"], b - 1)
                mm(ps[:, 4 + b % 2, :], wmat(M_WG2), gh[:, b % 2, :], start=True, stop=True).then_inc(s["gate_ps"], 1)

            def project(b):
                te.wait_ge(s["mixed"], b + 1)
                if b >= 2:
                    te.wait_ge(s["proj_added"], b - 1)
                for t in range(TB):
                    last = mm(ps[:, 6 + b % 2, t * P:(t + 1) * P], go[:, b % 2, t * P:(t + 1) * P], wmat(M_WO), start=True, stop=True)
                last.then_inc(s["proj_ps"], 1)
            for b in range(NB):
                project(b)

            te.wait_ge(s["gh_done"], NB)
            te.wait_ge(s["gate_done"], NB)
            te.wait_ge(s["wdT_made"], 2 * NB)
            te.wait_ge(s["b1_in"], 32)
            te.wait_ge(s["imix_made"], 1)
            for b in range(NB):
                if b >= 2:
                    te.wait_ge(s["abel_done"], b - 1)
                    te.wait_ge(s["acc_made"], b - 1)
                c = slice(b * S, (b + 1) * S)
                mm(ps[:, 0 + b % 2, :], wmat(M_ABEL), hF[:, c], start=True, stop=True).then_inc(s["abel_ps"], 1)
                mm(ps[:, 2 + b % 2, :], b2s[:, :], wdTf[:, c], start=True, stop=True).then_inc(s["acc_ps"], 1)
                te.wait_ge(s["abel_done"], b + 1)
                for j in range(2):
                    n = 2 * b + j
                    if n >= 2:
                        te.wait_ge(s["abn_done"], n - 1)
                    for i in range(2):
                        t = 2 * j + i
                        last = mm(ps[:, 4 + j, i * (P + 1):(i + 1) * (P + 1)], ab[:, b % 2, t * P:(t + 1) * P],
                                  imix[:, :], start=True, stop=True)
                    last.then_inc(s["abn_ps"], 1)
            te.wait_ge(s["abn_done"], 2 * NB)
            te.wait_ge(s["acc_made"], NB)
            te.wait_ge(s["proj_added"], NB)

            def first_layer(u):
                e, g = divmod(u, NB)
                c = slice(g * S, (g + 1) * S)
                te.wait_ge(s["w_split"], 4 * (e + 1))
                for j in range(2):
                    if u >= 1:
                        te.wait_ge(s["hid_done"], 4 * (u - 1) + 2 * j + 2)
                    for ch in (2 * j, 2 * j + 1):
                        o = ps[:, ch, :]
                        w = slice(ch * P, (ch + 1) * P)
                        mm(o, w1h[:, e % 2, w], hFh[:, c], start=True, stop=False)
                        mm(o, w1h[:, e % 2, w], hFl[:, c], start=False, stop=False)
                        mm(o, w1l[:, e % 2, w], hFh[:, c], start=False, stop=True).then_inc(s["h_ps"], 1)
                if u >= 1:
                    te.wait_ge(s["wb_copied"], u)
                mm(ps[:, 7, :], sel24[:, e, :], wdT[:, c], start=True, stop=True).then_inc(s["wb_ps"], 1)

            def second_layer(u):
                e = u // NB
                if u >= 2:
                    te.wait_ge(s["y_scaled"], u - 1)
                o = ps[:, 4 + u % 2, :]
                for ch in range(NC):
                    if ch % 2 == 0:
                        te.wait_ge(s["hidl_done"], 2 * u + ch // 2 + 1)
                        te.wait_ge(s["hidh_done"], 2 * u + ch // 2 + 1)
                    mm(o, w2h[:, e % 2, ch, :], hidh[:, u % 2, ch, :], start=(ch == 0), stop=False)
                    mm(o, w2h[:, e % 2, ch, :], hidl[:, u % 2, ch, :], start=False, stop=False)
                    last = mm(o, w2l[:, e % 2, ch, :], hidh[:, u % 2, ch, :], start=False, stop=(ch == NC - 1))
                last.then_inc(s["y_ps"], 1)

            def expm_steps():
                gen = wm[:, M_GEN * P:(M_GEN + NG) * P].rearrange("p (i c) -> p i c", c=P)
                o = ps[:, 6, 0:NG * P].rearrange("p (i c) -> p i c", c=P)
                for i in range(NG):
                    yield_last = nc.tensor.transpose(o[:, i, :], gen[:, i, :], ident[:, :])
                yield yield_last
                k = 0
                for _ in range(EXPM_DEGREE - 1):
                    for i in range(NG):
                        last = mm(o[:, i, :], bt[:, i, :], pw[:, k % 2, i, :], start=True, stop=True)
                    yield last
                    k += 1
                for i in range(NG):
                    last = nc.tensor.transpose(o[:, i, :], pw[:, k % 2, i, :], ident[:, :])
                yield last
                kt = 0
                for _ in range(EXPM_SQUARINGS):
                    for i in range(NG):
                        last = mm(o[:, i, :], pwt[:, kt % 2, i, :], pw[:, k % 2, i, :], start=True, stop=True)
                    yield last
                    for i in range(NG):
                        last = mm(o[:, i, :], pw[:, k % 2, i, :], pwt[:, kt % 2, i, :], start=True, stop=True)
                    yield last
                    k += 1
                    kt += 1
                yield mm(o[:, 0, :], pw[:, k % 2, 1, :], pwt[:, kt % 2, 0, :], start=True, stop=True)
                mm(o[:, 0, :], mt[:, 0, :], pw[:, k % 2, 2, :], start=True, stop=True)
                yield mm(o[:, 1, :], pw[:, k % 2, 2, :], mt[:, 0, :], start=True, stop=True)
                yield mm(o[:, 0, 0:1], mt[:, 1, :], vcol(V_MIX2), start=True, stop=True)

            steps = expm_steps()
            n_ex = 0
            te.wait_ge(s["expm_seed"], 1)
            for u in range(NU + 1):
                if u < NU:
                    first_layer(u)
                if u >= 1:
                    second_layer(u - 1)
                if n_ex >= 1:
                    te.wait_ge(s["ex_done"], n_ex)
                step = next(steps, None)
                if step is not None:
                    step.then_inc(s["ex_ps"], 1)
                    n_ex += 1
            assert next(steps, None) is None

            te.wait_ge(s["ex_done"], n_ex)
            for i in range(NT // 2):
                te.wait_ge(s["y_added"], NU - NB + (2 * i) // TB + 1)
                if i >= 2:
                    te.wait_ge(s["yo_done"], i - 1)
                for j in range(2):
                    t = 2 * i + j
                    last = mm(ps[:, 0 + i % 2, j * (P + 1):(j + 1) * (P + 1)], acc[:, t * P:(t + 1) * P], rr[:, :],
                              start=True, stop=True)
                last.then_inc(s["non_ps"], 1)

        @block.scalar
        def _(act):
            A = nc.scalar.activation
            steps = [0]

            def link(ins):
                steps[0] += 1
                ins.then_inc(s["act_step"], 1)
                act.wait_ge(s["act_step"], steps[0])

            def roots(g):
                t0, t1 = LN_GROUPS[g]
                for n in range(2):
                    act.wait_ge(s["z_used"], 2 * g + n + 1)
                    A(st[:, t0:t1, 9], st[:, t0:t1, 8], ACT.Sqrt).then_inc(s["sqrt_done"], 1)

            def attention_input(b):
                act.wait_ge(s["zT_done"], TB * (b + 1))
                A(hA[:, b, HALF:HALF + S], ps[:, b, :], ACT.Identity, bias=vcol(V_B), scale=vcol(V_G)).then_inc(s["hA_done"], 1)

            roots(0)
            act.wait_ge(s["vecs_in"], 16)
            act.wait_ge(s["rows_ps"], 1)
            A(rowb[:, :, :].rearrange("p a c -> p (a c)"), ps[:, 7, 0:3 * P], ACT.Copy).then_inc(s["rowb_made"], 1)
            attention_input(0)
            roots(1)
            for b in range(1, NB):
                attention_input(b)
            act.wait_ge(s["small_made"], 1)
            act.wait_ge(s["vaug_set"], 1)
            for b in range(NB):
                act.wait_ge(s["qk_ps"], b + 1)
                if b >= 1:
                    act.wait_ge(s["part3_done"], b)
                A(qk32[:, 0:S], ps[:, 4, :], ACT.Identity, bias=small[:, 0:1], scale=SCALE).then_inc(s["qk32_done"], 1)
                A(qk32[:, S:QK].rearrange("p (a c) -> p a c", a=2), ps[:, 5:7, 0:SP // 2], ACT.Identity,
                  bias=vcol(V_BKLOC)).then_inc(s["qk32_done"], 1)
                act.wait_ge(s["qk32_done"], 2 * (b + 1))
                if b >= 2:
                    act.wait_ge(scratch_out[b - 2], 16)
                A(qks[:, b % 2, 0, :], qk32[:, :], ACT.Copy).then_inc(s["part1_done"], 1)
                for g in range(2):
                    j = 2 * b + g
                    act.wait_ge(s["v_ps"], j + 1)
                    va = vaug[:, b, 4 * g:4 * g + 4, :, :].rearrange("p i n c -> p (i n) c")
                    part = lambda k: va[:, :, k * 2 * VG:(k + 1) * 2 * VG].rearrange("p n (h d) -> p n h d", h=2)[:, :, :, 0:HD]
                    A(part(0), ps[:, 7 * (1 - g), :].rearrange("p (n h d) -> p n h d", h=2, d=HD), ACT.Copy).then_inc(s["v1_done"], 1)
                    act.wait_ge(s["vres_done"], j + 1)
                    A(part(1), vres.rearrange("p (n h d) -> p n h d", h=2, d=HD), ACT.Copy).then_inc(s["v2_done"], 1)
            act.wait_ge(s["band_masked"], 4)
            A(thi[:, :, :], tb[:, :, :], ACT.Copy).then_inc(s["thi_done"], 1)
            act.wait_ge(s["tmid_done"], 1)
            A(thi[:, :, :], tbr[:, :, :], ACT.Copy).then_inc(s["thi_done"], 1)
            act.wait_ge(s["tables_made"], 4)
            for b in range(NB):
                act.wait_ge(s["logit_ps"], b + 1)
                A(lgT[:, b * S:(b + 1) * S], ps[0:E, 3, :], ACT.Identity, bias=vec[0:E, V_GATEB:V_GATEB + 1]).then_inc(s["logit_copied"], 1)
            act.wait_ge(s["b1s"], 1)
            A(r1[:, 4, :], r1[:, 3, :], ACT.Exp).then_inc(s["b1s"], 1)
            act.wait_ge(s["part3_done"], NB)
            for b in range(NB):
                act.wait_ge(scratch_out[b], 16)
            def linear(k):
                b, j = divmod(k, LIN_STEPS)
                if b >= NB:
                    return
                if j in (1, 2):
                    act.wait_ge(s["lin_min"], 2 * b + j)
                    A(lt[:, 1, :], lt[:, 1, :], ACT.Exp).then_inc(s["lin_exp"], 1)
                if j in (0, 3, 6):
                    act.wait_ge(s["lin_ps"], k + 1)
                if j == 0:
                    A(lt[:, 0, :], ps[:, 5, :], ACT.Identity, bias=vcol(V_BQLIN)).then_inc(s["lin_free"], 1)
                elif j == 3:
                    A(kvs[:, :], ps[:, 5, 0:P + 1], ACT.Copy).then_inc(s["lin_free"], 1)
                elif j == 6:
                    A(lin_t[:, b * S:(b + 1) * S], ps[:, 5, :], ACT.Copy).then_inc(s["lin_free"], 1)

            for n in range(NPAIR * NB):
                for g in range(2):
                    m = 2 * n + g
                    act.wait_ge(s["st_ps"], m + 1)
                    if n >= 2 and g == 0:
                        act.wait_ge(s["p2_done"], n - 1)
                        act.wait_ge(s["pv_ps"], n - 1)
                    src = ps[:, 2 + m % 3, :].rearrange("p (a i c) -> p i a c", a=2, c=BQ)
                    for buf, done in ((pe, "p_done"), (p1, "p1_done")):
                        A(buf[:, n % 2, g * 512:(g + 1) * 512].rearrange("p (i a c) -> p i a c", a=2, c=BQ),
                          src, ACT.Exp, bias=small[:, 1:2]).then_inc(s[done], 1)
                linear(n)
            for b in range(NB):
                act.wait_ge(s["wdT_ps"], b + 1)
                A(wdT[:, b * S:(b + 1) * S], ps[:, 0, :].bitcast(bf16)[0:SPLITS * E, 0:S], ACT.Copy).then_inc(s["wdT_made"], 1)
                A(wdTf[:, b * S:(b + 1) * S], ps[0:E, 1, :], ACT.Copy).then_inc(s["wdT_made"], 1)
            def gate_relu(b):
                act.wait_ge(s["gh_ps"], b + 1)
                if b >= 2:
                    act.wait_ge(s["gate_ps"], b - 1)
                A(gh[:, b % 2, :], ps[:, 2 + b % 2, :], ACT.Relu, bias=vcol(V_BG1)).then_inc(s["gh_done"], 1)
            gate_relu(0)
            for b in range(NB):
                if b + 1 < NB:
                    gate_relu(b + 1)
                act.wait_ge(s["gate_ps"], b + 1)
                if b >= 2:
                    act.wait_ge(s["mixed"], b - 1)
                A(gg[:, b % 2, :], ps[:, 4 + b % 2, :], ACT.Sigmoid, bias=vcol(V_BG2)).then_inc(s["gate_done"], 1)
            for b in range(NB):
                act.wait_ge(s["acc_ps"], b + 1)
                A(acc[:, b * S:(b + 1) * S], ps[:, 2 + b % 2, :], ACT.Copy).then_inc(s["acc_made"], 1)
                if b >= 2:
                    act.wait_ge(s["abn_ps"], 2 * (b - 1))
                A(ab[:, b % 2, :], ps[:, 0 + b % 2, :], ACT.Gelu, bias=vcol(V_ABEL)).then_inc(s["abel_done"], 1)
                for j in range(2):
                    n = 2 * b + j
                    act.wait_ge(s["abn_ps"], n + 1)
                    A(abn[:, 2 * n:2 * n + 2, :].rearrange("p t c -> p (t c)"), ps[:, 4 + j, 0:2 * (P + 1)], ACT.Copy).then_inc(s["abn_done"], 1)
            for u in range(NU):
                e = u // NB
                if u >= 2:
                    act.wait_ge(s["y_ps"], u - 1)
                    act.wait_ge(s["hidl_done"], 2 * (u - 1))
                for j in range(2):
                    for ch in (2 * j, 2 * j + 1):
                        act.wait_ge(s["h_ps"], NC * u + ch + 1)
                        A(hid[:, u % 2, ch, :], ps[:, ch, :], ACT.Gelu, bias=b1c[:, e * NC + ch:e * NC + ch + 1]).then_inc(s["hid_done"], 1)
                    act.wait_ge(s["hid_done"], NC * u + 2 * j + 2)
                    c = slice(2 * j, 2 * j + 2)
                    A(hidh[:, u % 2, c, :], hid[:, u % 2, c, :], ACT.Copy).then_inc(s["hidh_done"], 1)
                act.wait_ge(s["wb_ps"], u + 1)
                if u >= 2:
                    act.wait_ge(s["y_scaled"], u - 1)
                A(wb[:, u % 2, :], ps[:, 7, :], ACT.Copy).then_inc(s["wb_copied"], 1)
            for i in range(NT // 2):
                act.wait_ge(s["gl_done"], i + 1)
                A(gs[:, 2 * i:2 * i + 2], gl[:, 2 * i:2 * i + 2], ACT.Sigmoid, bias=vcol(V_MIXB)).then_inc(s["gs_done"], 1)

        @block.vector
        def _(dve):
            V = nc.vector
            steps = [0]

            def link(ins):
                steps[0] += 1
                ins.then_inc(s["dve_step"], 1)
                dve.wait_ge(s["dve_step"], steps[0])

            def rsqrt(v, root, r, t, n, g):
                dve.wait_ge(s["sqrt_done"], 2 * g + n + 1)
                link(V.reciprocal(r, root))
                link(V.tensor_tensor(t, r, r, ALU.mult))
                link(V.tensor_tensor(t, t, v, ALU.mult))
                link(V.tensor_scalar(t, t, -0.5, 1.5, ALU.mult, ALU.add))
                link(V.tensor_tensor(r, r, t, ALU.mult))

            def ffn_input(b):
                dve.wait_ge(s["hA_done"], b + 1)
                V.tensor_scalar(hF[:, b * S:(b + 1) * S], ps[:, b, :], vcol(V_FG), vcol(V_FB), ALU.mult, ALU.add).then_inc(s["hF_done"], 1)

            V.memset(ones1[:, :], 1.0).then_inc(s["ones_made"], 1)
            V.memset(vl[:, :, P:P + 1], 1.0).then_inc(s["vl_ones"], 1)
            V.memset(small[:, 1:2], P_SHIFT)
            va = vaug[:, :, :, :, :].rearrange("p b i n c -> p (b i n) c")
            for k in range(SPLITS):
                for h in range(2):
                    c = (2 * k + h) * VG + HD
                    last = V.memset(va[:, :, c:c + 1], 1.0 if k == 0 else 0.0)
            last.then_inc(s["vaug_set"], 1)
            dve.wait_ge(s["vecs_in"], 16)
            V.tensor_scalar(small[:, 0:1], vcol(V_BQLOC), SCALE, None, ALU.mult).then_inc(s["small_made"], 1)
            for g, (t0, t1) in enumerate(LN_GROUPS):
                for t in range(t0, t1):
                    if t % TB == 0:
                        dve.wait_ge(x_in[t // TB], 16)
                    last = V.bn_stats(st[:, t, 0:6], xs[:, t, :])
                link(last)
                for t in range(t0, t1):
                    last = V.bn_aggr(st[:, t, 6:8], st[:, t, 0:6])
                link(last)
                mean, var, ve, root = (st[:, t0:t1, i] for i in (6, 7, 8, 9))
                ra, rb, tmp = (st[:, t0:t1, i] for i in (10, 11, 12))
                V.tensor_scalar(ve, var, EPS, None, ALU.add).then_inc(s["z_used"], 1)
                dve.wait_ge(s["z_used"], 2 * g + 1)
                rsqrt(ve, root, ra, tmp, 0, g)
                link(V.tensor_tensor(tmp, ra, ra, ALU.mult))
                link(V.tensor_tensor(tmp, tmp, var, ALU.mult))
                V.tensor_scalar(ve, tmp, EPS, None, ALU.add).then_inc(s["z_used"], 1)
                dve.wait_ge(s["z_used"], 2 * g + 2)
                rsqrt(ve, root, rb, tmp, 1, g)
                link(V.tensor_tensor(rb, ra, rb, ALU.mult))
                for b in range(t0 // TB, t1 // TB):
                    for t in range(b * TB, (b + 1) * TB):
                        if b >= 1:
                            dve.wait_ge(s["zT_done"], t - TB + 1)
                        V.tensor_scalar(z[:, t % TB, :], xs[:, t, :], st[:, t, 6:7], st[:, t, 11:12], ALU.subtract, ALU.mult).then_inc(s["z_ready"], 1)
                    if b >= 1:
                        ffn_input(b - 1)
            ffn_input(NB - 1)
            V.tensor_copy(identh[:, :], ident[:, :]).then_inc(s["identh_made"], 1)
            dve.wait_ge(s["rel_in"], 32)
            turned = bass.AP(tensor=lin_t, offset=P - 1, ap=[[TOK, P], [P, NHEAD], [-1, P]])
            V.tensor_copy(tb[:, :, :], turned).then_inc(s["rel_turned"], 1)
            for b in range(NB):
                dve.wait_ge(s["part1_done"], b + 1)
                V.tensor_tensor(qk32[:, :], qk32[:, :], qks[:, b % 2, 0, :], ALU.subtract).then_inc(s["res1_done"], 1)
                dve.wait_ge(s["res1_done"], b + 1)
                V.tensor_copy(qks[:, b % 2, 1, :], qk32[:, :]).then_inc(s["part2_done"], 1)
                dve.wait_ge(s["part2_done"], b + 1)
                V.tensor_tensor(qks[:, b % 2, 2, :], qk32[:, :], qks[:, b % 2, 1, :], ALU.subtract).then_inc(s["part3_done"], 1)
                for g in range(2):
                    j = 2 * b + g
                    va = vaug[:, b, 4 * g:4 * g + 4, :, :].rearrange("p i n c -> p (i n) c")
                    part = lambda k: va[:, :, k * 2 * VG:(k + 1) * 2 * VG].rearrange("p n (h d) -> p n h d", h=2)[:, :, :, 0:HD]
                    r4 = vres.rearrange("p (n h d) -> p n h d", h=2, d=HD)
                    dve.wait_ge(s["v1_done"], j + 1)
                    if j >= 1:
                        dve.wait_ge(s["v3_done"], j)
                    V.tensor_tensor(r4, ps[:, 7 * (1 - g), :].rearrange("p (n h d) -> p n h d", h=2, d=HD), part(0), ALU.subtract).then_inc(s["vres_done"], 1)
                    dve.wait_ge(s["v2_done"], j + 1)
                    V.tensor_tensor(part(2), r4, part(1), ALU.subtract).then_inc(s["v3_done"], 1)
            dve.wait_ge(s["thi_done"], 1)
            V.tensor_copy(bhm[0:64, :, :], thi[0:64, :, :])
            th = thi[:, :, :].rearrange("p (n a) c -> p n a c", a=2)
            for half in range(2):
                V.tensor_copy(bs[64 * half:64 * half + 64, :, :], th[64 * half:64 * half + 64, :, half, :])
            V.tensor_tensor(tbr[:, :, :], tb[:, :, :], thi[:, :, :], ALU.subtract).then_inc(s["tmid_done"], 1)
            dve.wait_ge(s["thi_done"], 2)
            V.tensor_copy(bhm[64:128, :, :], thi[64:128, :, :]).then_inc(s["tables_made"], 1)
            V.tensor_tensor(blo[0:64, :, :], tbr[0:64, :, :], thi[0:64, :, :], ALU.subtract).then_inc(s["tables_made"], 1)
            dve.wait_ge(s["sel_made"], 1 + SPLITS)
            for half in range(2):
                V.tensor_copy(blo[64:88, :, :].rearrange("p (n a) c -> p n a c", a=2)[:, :, half, :], sel24[:, :, :]).then_inc(s["tables_made"], 1)
            for half in range(2):
                o = 64 * half
                link(V.tensor_copy(id64[o:o + 64, :, :], ident[o:o + 64, o:o + 64].rearrange("p (a c) -> p a c", a=1).broadcast_to((64, 4, BQ))))
            for half in range(2):
                V.tensor_copy(mv[0:64, half, :].rearrange("p (n c) -> p n c", c=BQ),
                              ident[0:64, 0:BQ].rearrange("p (a c) -> p a c", a=1).broadcast_to((64, TOK // BQ, BQ))).then_inc(s["mv_set"], 1)
            link(V.tensor_scalar(st[:, :, 13], st[:, :, 10], 2.0, 1.0, ALU.mult, ALU.add))
            link(V.tensor_tensor(st[:, :, 14], st[:, :, 6], st[:, :, 10], ALU.mult))
            link(V.tensor_scalar(st[:, :, 15], st[:, :, 14], -2.0, None, ALU.mult))
            for t in range(NT):
                last = V.tensor_scalar(xs[:, t, :], xs[:, t, :], st[:, t, 13:14], st[:, t, 15:16], ALU.mult, ALU.add)
            link(last)
            dve.wait_ge(s["logitT_ps"], 1)
            L = lambda i: rt[:, i, :, :]
            R = lambda i: r1[:, i, :]
            col = lambda a: a.rearrange("p (t c) -> p t c", c=1).broadcast_to((P, NT, E))
            link(V.tensor_copy(logit[:, :, :].rearrange("p t e -> p (t e)"), ps[:, 3, 0:NT * E]))
            for e in range(E):
                last = V.memset(rt[:, 0, :, e], float(e) - 100.0)
            link(last)
            src = logit[:, :, :]
            for k in range(2):
                m, first = R(k), L(1 + k)
                link(V.tensor_reduce(m, src, AX.X, ALU.max))
                link(V.tensor_tensor(L(3), src, col(m), ALU.is_equal))
                link(V.tensor_tensor(L(4), L(3), L(0), ALU.mult))
                link(V.tensor_reduce(R(2), L(4), AX.X, ALU.min))
                link(V.tensor_tensor(first, L(4), col(R(2)), ALU.is_equal))
                if k == 0:
                    link(V.tensor_scalar(L(3), first, -3e38, None, ALU.mult))
                    link(V.tensor_tensor(L(5), src, L(3), ALU.add))
                    src = L(5)
            V.tensor_tensor(R(3), R(1), R(0), ALU.subtract).then_inc(s["b1s"], 1)
            dve.wait_ge(s["b1s"], 2)
            link(V.tensor_scalar(R(5), R(4), 1.0, None, ALU.add))
            link(V.reciprocal(R(6), R(5)))
            link(V.tensor_tensor(R(7), R(4), R(6), ALU.mult))
            link(V.tensor_tensor(L(3), L(1), col(R(6)), ALU.mult))
            link(V.tensor_tensor(L(4), L(2), col(R(7)), ALU.mult))
            link(V.tensor_tensor(L(6), L(3), L(4), ALU.add))
            link(V.tensor_copy(wds[:, :, 0:E], L(6)))
            link(V.tensor_tensor(L(5), L(6), wds[:, :, 0:E], ALU.subtract))
            link(V.tensor_copy(wds[:, :, E:2 * E], L(5)))
            V.tensor_tensor(wds[:, :, 2 * E:3 * E], L(5), wds[:, :, E:2 * E], ALU.subtract).then_inc(s["wds_made"], 1)

            def take_max(b, p):
                for g in range(2):
                    n = (b * NPAIR + p) * 2 + g
                    dve.wait_ge(s["s_ps"], n + 1)
                    if b >= 1 and p == 0 and g == 0:
                        dve.wait_ge(s["negmax_split"], b)
                    V.tensor_reduce(nm[:, 4 * g:4 * g + 4, p], ps[:, g, :].rearrange("p (i c) -> p i c", c=P),
                                    AX.X, ALU.max, negate=True).then_inc(s["max_taken"], 1)

            def split_max(b):
                dve.wait_ge(s["max_taken"], 2 * NPAIR * (b + 1))
                if b >= 1:
                    dve.wait_ge(s["negmaxT_ps"], b)
                link(V.tensor_copy(nms[:, :, 0, :], nm[:, :, :]))
                link(V.tensor_tensor(nmr[:, :, :], nm[:, :, :], nms[:, :, 0, :], ALU.subtract))
                link(V.tensor_copy(nms[:, :, 1, :], nmr[:, :, :]))
                V.tensor_tensor(nms[:, :, 2, :], nmr[:, :, :], nms[:, :, 1, :], ALU.subtract).then_inc(s["negmax_split"], 1)

            def negmax_rows(b):
                dve.wait_ge(s["negmaxT_ps"], b + 1)
                tv = ps[:, 0, :].bitcast(bf16).rearrange("p (i a c) -> p i a c", a=2, c=BQ)
                for half in range(2):
                    last = V.tensor_copy(mv[64:88, half, b * S:(b + 1) * S].rearrange("p (i c) -> p i c", c=BQ), tv[0:24, :, half, :])
                last.then_inc(s["negmaxT_done"], 1)

            def linear(k):
                b, j = divmod(k, LIN_STEPS)
                if b >= NB:
                    return
                bank = ps[:, 5, :].rearrange("p (t c) -> p t c", c=P)
                raw, low = lt[:, 0, :], lt[:, 1, :]
                rows = lambda a: a.rearrange("p (t c) -> p t c", c=P)
                bias = lambda i: rowb[:, i:i + 1, :].broadcast_to((P, TB, P))
                if j == 0:
                    dve.wait_ge(s["lin_free"], k + 1)
                    V.tensor_scalar(low, raw, 0.0, None, ALU.min).then_inc(s["lin_min"], 1)
                elif j == 1:
                    dve.wait_ge(s["lin_exp"], 2 * b + 1)
                    V.scalar_tensor_tensor(qlT[:, :], raw, 0.0, low, ALU.max, ALU.add).then_inc(s["lin_q_made"], 1)
                    dve.wait_ge(s["lin_ps"], k + 1)
                    dve.wait_ge(s["lin_q_made"], b + 1)
                    V.tensor_tensor(rows(raw), bank, bias(0), ALU.add).then_inc(s["lin_free"], 1)
                    dve.wait_ge(s["lin_free"], k + 1)
                    V.tensor_scalar(low, raw, 0.0, None, ALU.min).then_inc(s["lin_min"], 1)
                elif j == 2:
                    dve.wait_ge(s["lin_exp"], 2 * b + 2)
                    V.scalar_tensor_tensor(kl[:, :, :].rearrange("p t c -> p (t c)"), raw, 0.0, low, ALU.max, ALU.add).then_inc(s["lin_k_made"], 1)
                    dve.wait_ge(s["lin_ps"], k + 1)
                    V.tensor_tensor(vl[:, :, 0:P], bank, bias(1), ALU.add).then_inc(s["lin_free"], 1)
                elif j in (4, 5):
                    g = j - 4
                    dve.wait_ge(s["lin_ps"], k + 1)
                    dve.wait_ge(s["lin_k_made"], b + 1)
                    if b >= 1:
                        dve.wait_ge(s["lin_free"], LIN_STEPS * b)
                    nat = ps[:, 5, 0:2 * (P + 1)].rearrange("p (t c) -> p t c", c=P + 1)
                    rec = lrec[:, 2 * g:2 * g + 2]
                    link(V.tensor_scalar(rec, nat[:, :, P], 1e-6, None, ALU.add))
                    link(V.reciprocal(rec, rec))
                    for i in range(2):
                        last = V.tensor_scalar(ln_[:, 2 * g + i, :], nat[:, i, 0:P], rec[:, i:i + 1], None, ALU.mult)
                    last.then_inc(s["lin_free"], 1)

            def take_values(n):
                b, p = divmod(n, NPAIR)
                dve.wait_ge(s["pv_ps"], n + 1)
                if p == 0 and b >= 1:
                    dve.wait_ge(s["o_normed"], b)
                for half in range(2):
                    o = 64 * half
                    src = ps[o:o + 64, 6 + p % 2, 0:NBLK * VW].rearrange("p (i k a c) -> p i a c k", i=NBLK, k=SPLITS, a=2)
                    last = V.tensor_reduce(ot[o:o + 64, :, p, :], src[:, :, half, :, :], AX.X, ALU.add)
                last.then_inc(s["pv_taken"], 1)

            def normalise(b):
                dve.wait_ge(s["pv_taken"], NPAIR * (b + 1))
                o3 = ot[:, :, :, :].rearrange("p i n c -> p (i n) c")
                link(V.reciprocal(orec[:, :, :].rearrange("p i n -> p (i n)"), o3[:, :, HD]))
                if b >= 1:
                    dve.wait_ge(s["oT_ps"], 2 * b)
                V.tensor_tensor(on[:, :, :].rearrange("p i (n c) -> p (i n) c", c=HD), o3[:, :, 0:HD],
                                orec[:, :, :].rearrange("p i (n c) -> p (i n) c", c=1).broadcast_to((P, NBLK * NPAIR, HD)),
                                ALU.mult).then_inc(s["o_normed"], 1)

            def outputs_transposed(b):
                for j in range(2):
                    dve.wait_ge(s["oT_ps"], 2 * b + j + 1)
                    src = ps[0:64, 6 + j, :].rearrange("p (i a c) -> p i a c", a=2, c=BQ)
                    for half in range(2):
                        dst = win_t[64 * half:64 * half + 64, b * S + 256 * j:b * S + 256 * (j + 1)].rearrange("p (i c) -> p i c", c=BQ)
                        last = V.tensor_scalar(dst, src[:, :, half, :], vec[0:64, V_BV0 + half:V_BV0 + half + 1], None, ALU.add)
                    last.then_inc(s["oT_done"], 1)

            def spread(b, c):
                if c == 0:
                    dve.wait_ge(q_in[b], 16 * 2 * NTERM)
                    if b >= 2:
                        dve.wait_ge(s["st_ps"], 2 * NPAIR * (b - 1))
                for half in range(2):
                    o = 64 * half
                    V.tensor_copy(qst[o:o + 64, b % 2, 2 * c:2 * c + 2, :, o:o + BQ].rearrange("p n i c -> p (n i) c"),
                                  qin[o:o + 64, 2 * c:2 * c + 2, :].rearrange("p n (i c) -> p (n i) c", c=BQ)).then_inc(s["q_spread"], 1)

            dve.wait_ge(s["stacks_set"], 7)
            for c in range(4):
                spread(0, c)
            for p in range(NPAIR):
                take_max(0, p)
            split_max(0)
            negmax_rows(0)
            for c in range(4):
                spread(1, c)
            for b in range(NB):
                for p in range(NPAIR):
                    n = b * NPAIR + p
                    if b + 1 < NB:
                        for q in AHEAD[p]:
                            if b >= 1 and q % 2 == 0:
                                spread(b + 1, q // 2)
                            take_max(b + 1, q)
                        if p == 6:
                            split_max(b + 1)
                        if p == 7:
                            negmax_rows(b + 1)
                    dve.wait_ge(s["p_done"], 2 * n + 2)
                    dve.wait_ge(s["p1_done"], 2 * n + 2)
                    if n >= 2:
                        dve.wait_ge(s["pv_ps"], n - 1)
                    V.tensor_tensor(p2[:, n % 2, :], pe[:, n % 2, :], p1[:, n % 2, :], ALU.subtract).then_inc(s["p2_done"], 1)
                    linear(n)
                    if p >= 1:
                        take_values(n - 1)
                    elif b >= 1:
                        outputs_transposed(b - 1)
                take_values(b * NPAIR + NPAIR - 1)
                normalise(b)
            outputs_transposed(NB - 1)

            dve.wait_ge(s["oT_done"], 2 * NB)
            for b in range(NB):
                c = slice(b * S, (b + 1) * S)
                if b >= 2:
                    dve.wait_ge(s["proj_ps"], b - 1)
                link(V.tensor_tensor(gd[:, b % 2, :], lin_t[:, c], win_t[:, c], ALU.subtract))
                dve.wait_ge(s["gate_done"], b + 1)
                link(V.tensor_tensor(gd[:, b % 2, :], gd[:, b % 2, :], gg[:, b % 2, :], ALU.mult))
                V.tensor_tensor(go[:, b % 2, :], gd[:, b % 2, :], win_t[:, c], ALU.add).then_inc(s["mixed"], 1)
            for b in range(NB):
                t = slice(b * TB, (b + 1) * TB)
                dve.wait_ge(s["proj_ps"], b + 1)
                link(V.tensor_tensor(xs[:, t, :], xs[:, t, :], ps[:, 6 + b % 2, :].rearrange("p (t c) -> p t c", c=P), ALU.add))
                V.tensor_tensor(xs[:, t, :], xs[:, t, :], rowb[:, 2:3, :].broadcast_to((P, TB, P)), ALU.add).then_inc(s["proj_added"], 1)
            V.tensor_copy(imix[:, 0:P], ident[:, :])
            V.tensor_copy(imix[:, P:P + 1], vcol(V_MIX1)).then_inc(s["imix_made"], 1)

            link(V.tensor_copy(hFh[:, :], hF[:, :]))
            V.tensor_tensor(hFl[:, :], hF[:, :], hFh[:, :].bitcast(f32), ALU.subtract)

            def split_weights(e):
                k = e % 2
                dve.wait_ge(w_in[k], 32 * (e // 2 + 1))
                if e >= 2:
                    dve.wait_ge(s["y_ps"], NB * (e - 1))
                V.tensor_copy(w1h[:, k, :], w1r[:, k, :]).then_inc(s["w_split"], 1)
                V.tensor_copy(w2h[:, k, :, :], w2r[:, k, :, :]).then_inc(s["w_split"], 1)
                dve.wait_ge(s["w_split"], 4 * e + 2)
                V.tensor_tensor(w1l[:, k, :], w1r[:, k, :], w1h[:, k, :].bitcast(f32), ALU.subtract).then_inc(s["w_split"], 1)
                V.tensor_tensor(w2l[:, k, :, :], w2r[:, k, :, :], w2h[:, k, :, :].bitcast(f32), ALU.subtract).then_inc(s["w_split"], 1)

            split_weights(0)
            for b in range(NB):
                dve.wait_ge(s["abn_done"], 2 * (b + 1))
                if b == 0:
                    dve.wait_ge(s["proj_added"], NB)
                t = slice(b * TB, (b + 1) * TB)
                V.tensor_tensor(xs[:, t, :], xs[:, t, :], abn[:, t, 0:P], ALU.add).then_inc(s["base_made"], 1)

            gen = wm[:, M_GEN * P:(M_GEN + NG) * P].rearrange("p (i c) -> p i c", c=P)
            down = 2.0 ** -EXPM_SQUARINGS
            for i in range(NG):
                last = V.scalar_tensor_tensor(pw[:, 0, i, :], gen[:, i, :], down / EXPM_DEGREE, ident[:, :], ALU.mult, ALU.add)
            last.then_inc(s["expm_seed"], 1)

            def expm_steps():
                o = ps[:, 6, 0:NG * P].rearrange("p (i c) -> p i c", c=P)
                yield V.tensor_scalar(bt[:, :, :], o, down, None, ALU.mult)
                k = 0
                for d in range(EXPM_DEGREE - 1, 0, -1):
                    for i in range(NG):
                        last = V.scalar_tensor_tensor(pw[:, (k + 1) % 2, i, :], o[:, i, :], 1.0 / d, ident[:, :], ALU.mult, ALU.add)
                    yield last
                    k += 1
                yield V.tensor_copy(pwt[:, 0, :, :], o)
                kt = 0
                for _ in range(EXPM_SQUARINGS):
                    yield V.tensor_copy(pw[:, (k + 1) % 2, :, :], o)
                    yield V.tensor_copy(pwt[:, (kt + 1) % 2, :, :], o)
                    k += 1
                    kt += 1
                yield V.tensor_copy(mt[:, 0, :], o[:, 0, :])
                V.tensor_copy(rr[:, 0:P], o[:, 0, :])
                yield V.tensor_copy(mt[:, 1, :], o[:, 1, :])
                yield V.tensor_copy(rr[:, P:P + 1], o[:, 0, 0:1])

            def add_expert(u):
                c = slice((u % NB) * S, (u % NB + 1) * S)
                dve.wait_ge(s["y_ps"], u + 1)
                dve.wait_ge(s["wb_copied"], u + 1)
                if u == 0:
                    dve.wait_ge(s["acc_made"], NB)
                V.tensor_tensor(ysc[:, u % 2, :], ps[:, 4 + u % 2, :], wb[:, u % 2, :], ALU.mult).then_inc(s["y_scaled"], 1)
                dve.wait_ge(s["y_scaled"], u + 1)
                V.tensor_tensor(acc[:, c], acc[:, c], ysc[:, u % 2, :], ALU.add).then_inc(s["y_added"], 1)

            steps_ = expm_steps()
            n_ex = 0
            for u in range(NU):
                for j in range(2):
                    dve.wait_ge(s["hidh_done"], 2 * u + j + 1)
                    c = slice(2 * j, 2 * j + 2)
                    if u >= 2:
                        dve.wait_ge(s["y_ps"], u - 1)
                    V.tensor_tensor(hidl[:, u % 2, c, :], hid[:, u % 2, c, :], hidh[:, u % 2, c, :].bitcast(f32),
                                    ALU.subtract).then_inc(s["hidl_done"], 1)
                if u >= 1:
                    add_expert(u - 1)
                if n_ex < 20:
                    dve.wait_ge(s["ex_ps"], n_ex + 1)
                    step = next(steps_, None)
                    step.then_inc(s["ex_done"], 1)
                    n_ex += 1
                if u % NB == 1 and u // NB + 1 < E:
                    split_weights(u // NB + 1)
            assert next(steps_, None) is None
            add_expert(NU - 1)

            for i in range(NT // 2):
                k = i % 2
                t = slice(2 * i, 2 * i + 2)
                dve.wait_ge(s["non_ps"], i + 1)
                if i == 0:
                    dve.wait_ge(s["base_made"], NB)
                n2 = ps[:, k, 0:2 * (P + 1)].rearrange("p (t c) -> p t c", c=P + 1)
                V.tensor_tensor(gl[:, t], n2[:, :, P], abn[:, t, P], ALU.add).then_inc(s["gl_done"], 1)
                link(V.tensor_tensor(dif[:, k, :, :], n2[:, :, 0:P], abn[:, t, 0:P], ALU.subtract))
                dve.wait_ge(s["gs_done"], i + 1)
                if i >= 2:
                    dve.wait_ge(out_written[k], 16 * (i // 2))
                for j in range(2):
                    last = V.scalar_tensor_tensor(yo[:, k, j, :], dif[:, k, j, :], gs[:, 2 * i + j:2 * i + j + 1],
                                                  xs[:, 2 * i + j, :], ALU.mult, ALU.add)
                last.then_inc(s["yo_done"], 1)


def kernel(**inputs):
    import numpy as np
    import concourse.bacc as bacc
    from concourse import mybir as mb
    from concourse.bass_utils import run_bass_kernel_spmd

    a = {k: np.ascontiguousarray(v) for k, v in inputs.items()}
    at = lambda n: a["L0_attn_" + n]
    ff = lambda n: a["L0_ffn_" + n]
    D, HD, NPAIR = 128, 8, 8
    perm = np.arange(D).reshape(NPAIR, 2, HD).transpose(1, 0, 2).reshape(D)
    bv = at("bv_loc")[perm]
    cols = [at("bq_lin"), at("bq_loc")[perm], at("bk_loc")[perm], bv, np.roll(bv, -64), at("bg1"), at("bg2")[perm],
            at("ln_g"), at("ln_b"), ff("ln_g"), ff("ln_b"), ff("abel_b"), ff("mix_w")[0:D, 0], ff("mix_w")[D:2 * D, 0],
            np.repeat(ff("mix_b"), D), np.pad(ff("gate_b_moe"), (0, D - 8))]
    wg1 = at("wg1")
    rel = at("rel_bias")
    rel_t = np.zeros((rel.shape[1], 192), rel.dtype)
    rel_t[:, 31:31 + rel.shape[0]] = rel.T[:, ::-1]
    gens = ff("gens")
    b1 = ff("b1")
    arrays = {
        "x": a["L0_attn_x"],
        "vecs": np.stack(cols, axis=1),
        "rows": np.concatenate([at("bk_lin"), at("bv_lin")[perm], at("bo")])[None, :],
        "w_loc": np.concatenate([at("wq_loc")[:, perm], at("wk_loc")[:, perm], at("wv_loc")], axis=1),
        "w_more": np.concatenate([at("wq_lin"), at("wk_lin"), at("wv_lin")[:, perm], at("wo")[perm, :],
                                  wg1[0:D][perm, :], wg1[D:2 * D][perm, :], wg1[2 * D:], at("wg2")[:, perm],
                                  ff("abel_w"), gens[0], gens[1], gens[2], ff("gate_w_moe")], axis=1),
        "rel_t": rel_t,
        "b1_cols": b1.reshape(b1.shape[0], -1, D).transpose(2, 0, 1).reshape(D, -1),
        "b2": ff("b2"), "w1": ff("w1"), "w2": ff("w2"),
    }
    arrays = {"in_" + k: np.ascontiguousarray(v) for k, v in arrays.items()}
    nc = bacc.Bacc("TRN2", target_bir_lowering=False, num_devices=1)
    args = {k: nc.dram_tensor(k, v.shape, mb.dt.from_np(v.dtype), kind="ExternalInput").ap() for k, v in arrays.items()}
    g = lambda n: args["in_" + n]
    scratch = nc.dram_tensor("qk_scratch", [4, D, 3, 512 + 576], mb.dt.bfloat16, kind="Internal").ap()
    out = nc.dram_tensor("out_0_dram", (4, 512, D), mb.dt.float32, kind="ExternalOutput").ap()
    attention_and_moe_block(nc, g("x"), g("vecs"), g("rows"), g("w_loc"), g("w_more"), g("rel_t"), g("b1_cols"),
                            g("b2"), g("w1"), g("w2"), scratch, out)
    r = run_bass_kernel_spmd(nc, [arrays], core_ids=[0])
    return r.results[0]["out_0_dram"]
```

```python
import concourse.bass as bass
from concourse import mybir
from contextlib import ExitStack


def attention_and_moe_block(nc, x, vecs, rows, w_loc, w_more, rel_t, b1_cols, b2, w1, w2,
                            q_scratch, k_scratch, routing_scratch, out):
    f32, f32r, bf16, f16 = mybir.dt.float32, mybir.dt.float32r, mybir.dt.bfloat16, mybir.dt.float16
    ALU, ACT, AX = mybir.AluOpType, mybir.ActivationFunctionType, mybir.AxisListType

    P = 128
    NB, S, D = x.shape
    TB = S // P
    NT = NB * TB
    TOK = NB * S
    E, _, DF = w1.shape
    NC = DF // P
    NHEAD, HD = 16, 8
    NPAIR = NHEAD // 2
    HALF = 32
    BQ = 64
    NBLK = S // BQ
    SP = S + 2 * HALF
    QK = S + SP
    SPLITS = 3
    QTERM = [(0, 0, 0, 3), (3, 1, 0, 2), (5, 2, 0, 1)]
    KTERM = [(0, 0, 1, 3), (3, 0, 1, 2), (5, 0, 0, 1)]
    NTERM = len(QTERM)
    VG = HD + 1
    VW = SPLITS * 2 * VG
    NEG = -1e30
    BF16_ONES = 1.0 + 0x3f80 / 2 ** 23
    EPS = 1e-5
    SCALE = float(HD) ** -0.5
    P_SHIFT = 12 * 0.6931471805599453
    EXPM_SQUARINGS, EXPM_DEGREE = 4, 8
    WB = 4
    NG = 3

    (V_BQLIN, V_BQLOC, V_BKLOC, V_BV0, V_BV1, V_BG1, V_BG2, V_G, V_B, V_FG, V_FB, V_ABEL,
     V_MIX1, V_MIX2, V_MIXB) = range(15)
    (M_QLIN, M_KLIN, M_VLIN, M_WO, M_G1LIN, M_G1WIN, M_G1H, M_WG2, M_ABEL, M_GEN) = range(10)
    M_GATE = (M_GEN + NG) * P

    ctx = ExitStack()
    with ctx:
        def sb(name, shape, dt, c=ctx):
            return c.enter_context(nc.sbuf_tensor(name, shape, dt))

        def sem(name):
            return ctx.enter_context(nc.semaphore(name))

        xs = sb("xs", [P, NT, P], f32)
        hA = sb("hA", [P, NB, SP], f32)
        hF = sb("hF", [P, TOK], f32)
        lin_t = sb("lin_t", [P, TOK], f32)
        win_t = sb("win_t", [P, TOK], f32)
        vec = sb("vec", [P, 15], f32)
        wloc = sb("wloc", [P, 3 * P], f32)
        wm = sb("wm", [P, M_GATE + E], f32)
        rowb = sb("rowb", [P, 3 * P + E], f32)
        ident = sb("ident", [P, P], f32)
        identh = sb("identh", [P, P], bf16)
        id64 = sb("id64", [P, 4, BQ], bf16)
        ones1 = sb("ones1", [1, P], f32)
        st = sb("st", [P, NT, 16], f32)
        logit = sb("logit", [P, NT, E], f32)
        rt = sb("rt", [P, 7, NT, E], f32)
        row1 = rt[0:1, :, :, :].rearrange("p a t e -> p (a t e)")[:, 0:3 * P + E]
        r1 = sb("r1", [P, 8, NT], f32)
        b1c = sb("b1c", [P, E * NC], f32)
        b2s = sb("b2s", [E, P], f32)
        small = sb("small", [P, 8], f32)

        win_ctx = ExitStack()
        def sw(name, shape, dt):
            return sb(name, shape, dt, win_ctx)
        on = sw("on", [P, NBLK, NPAIR * HD], f32)
        z = on[:, :, :].rearrange("p i c -> p (i c)").rearrange("p (t c) -> p t c", c=P)
        part_ctx = ExitStack()
        qk32 = sb("qk32", [P, 2, QK], f32, part_ctx)
        qks = sb("qks", [P, 2, SPLITS, QK], bf16, part_ctx)
        part_ctx.close()
        prob_ctx = ExitStack()
        pe = sb("pe", [P, 2, 1024], f32, prob_ctx)
        p1 = sb("p1", [P, 2, 1024], f16, prob_ctx)
        p2 = sb("p2", [P, 2, 1024], f16, prob_ctx)
        prob_ctx.close()
        part_room = sw("part_room", [P, 2 * QK + SPLITS * QK], f32)
        vaug = sw("vaug", [P, NB, NBLK, NPAIR, VW], bf16)
        qin = sw("qin", [P, NPAIR, S], bf16)
        qst = sw("qst", [P, 2, NPAIR, NBLK, 2 * BQ], bf16)
        kst = sw("kst", [P, 3, NPAIR, SP], bf16)
        bhm = sw("bhm", [P, NHEAD, P], bf16)
        blo = sw("blo", [88, NHEAD, P], bf16)
        bs = sw("bs", [P, NPAIR, P], bf16)
        mv = sw("mv", [88, 2, TOK], bf16)
        nm = sw("nm", [P, NBLK, NPAIR], f32)
        nmr = sw("nmr", [P, NBLK, NPAIR], f32)
        nms = sw("nms", [P, NBLK, SPLITS, NPAIR], bf16)
        ot = sw("ot", [P, NBLK, NPAIR, VG], f32)
        orec = sw("orec", [P, NBLK, NPAIR], f32)
        tab_ctx = ExitStack()
        thi = sb("thi", [P, NHEAD, P], bf16, tab_ctx)
        vres = sb("vres", [P, NBLK * P], f32, tab_ctx)
        tb = win_t[:, :].rearrange("p (h c) -> p h c", c=P)
        tbr = lin_t[:, :].rearrange("p (h c) -> p h c", c=P)
        tab_ctx.close()
        lt = sw("lt", [P, 2, S], f32)
        ln_ = lt[:, 0, :].rearrange("p (t c) -> p t c", c=P)
        qlT = sw("qlT", [P, S], f32)
        kl = sw("kl", [P, TB, P], f32)
        vl = sw("vl", [P, TB, P + 1], f32)
        kvs = sw("kvs", [P, P + 1], f32)
        lrec = sw("lrec", [P, TB], f32)
        win_ctx.close()

        gate_ctx = ExitStack()
        def sg(name, shape, dt):
            return sb(name, shape, dt, gate_ctx)
        hid = sg("hid", [P, 2, NC, S], f32)
        hidh = sg("hidh", [P, 2, NC, S], f32r)
        pw = sg("pw", [P, 2, NG, P], f32)
        rr = sg("rr", [P, P + 1], f32)
        imix = sg("imix", [P, P + 1], f32)
        gl = sg("gl", [P, NT], f32)
        gs = sg("gs", [P, NT], f32)
        sg("filler", [P, 30], f32)
        w1h = sg("w1h", [P, 2, DF], f32r)
        w1l = sg("w1l", [P, 2, DF], f32r)
        w2h = sg("w2h", [P, 2, NC, P], f32r)
        w2l = sg("w2l", [P, 2, NC, P], f32r)
        w1r = sg("w1r", [P, 2, DF], f32)
        w2r = sg("w2r", [P, 2, NC, P], f32)
        wdT = sg("wdT", [E, TOK], f32)
        wb = sg("wb", [P, WB, S], f32)
        mix_ctx = ExitStack()
        gg = sb("gg", [P, NB, S], f32, mix_ctx)
        gd = sb("gd", [P, NB, S], f32, mix_ctx)
        mix_ctx.close()
        hidl = sg("hidl", [P, 2, NC, S], f32r)
        hFl = sg("hFl", [P, TOK], f32r)
        mt = sg("mt", [P, 2, P], f32)
        hFh = sg("hFh", [P, TOK], f32r)
        gh_ctx = ExitStack()
        gh = sb("gh", [P, NB, S], f32, gh_ctx)
        gh_ctx.close()
        ab = sg("ab", [P, 2, S], f32)
        ysc = sg("ysc", [P, 2, S], f32)
        abn = sg("abn", [P, NT, P + 1], f32)
        acc = sg("acc", [P, TOK], f32)
        bt = sg("bt", [P, NG, P], f32)
        pwt = sg("pwt", [P, 2, NG, P], f32)
        dif = hF[:, :].rearrange("p (t c) -> p t c", c=P)
        gate_ctx.close()

        ps = ctx.enter_context(nc.psum_tensor("ps", [P, 8, 512], f32))

        names = """
            vecs_in wloc_in wmore_in rows_in rel_in b1_in
            consts_made identh_made ones_made small_made pads_set stacks_set qst_set vaug_set vl_ones id_zeros mv_set
            rows_ps rowb_made dve_step
            sqrt_done z_ready z_used zT_done hA_done hF_done residual_cols residual_made residual_biased
            qk_ps qk32_done part1_done res1_done part2_done part3_done
            v_ps v1_done vres_done v2_done v3_done
            rel_turned band_masked thi_done tmid_done tables_made low_made picks_made
            logit_ps logit_made top_gap top_ratio routed wdT_ps wdT_made routing_out
            q_spread s_ps max_taken negmax_split negmaxT_ps negmaxT_done
            st_ps p_done p1_done p2_done pv_ps pv_taken o_normed oT_ps oT_done
            lin_ps lin_free lin_min lin_exp lin_q_made lin_k_made
            gh_ps gh_done gate_ps gate_done diff_made mixed proj_ps proj_added acc_ps acc_made
            gelu_ps gelu_done imix_made base_made
            expm_seed ex_ps ex_done
            ffn_high ffn_split w_split h_ps hid_done hidh_done hidl_done y_ps y_scaled y_added
            rot_ps rot_done gs_done tile_done out_written
            """.split()
        s = {n: sem(n) for n in names}
        x_in = [sem(f"x_in{b}") for b in range(NB)]
        scratch_out = [sem(f"scratch_out{b}") for b in range(NB)]
        q_in = [sem(f"q_in{b}") for b in range(NB)]
        k_in = [sem(f"k_in{b}") for b in range(NB)]
        wb_in = [sem(f"wb_in{i}") for i in range(WB)]
        w_in = [sem(f"w_in{i}") for i in range(2)]

        vcol = lambda i: vec[:, i:i + 1]
        wmat = lambda i: wm[:, i * P:(i + 1) * P]
        AHEAD = [[0, 1], [2], [3], [4], [5], [6], [7], []]
        LIN_STEPS = 7

        heads = lambda a: a.rearrange("p (n h d) -> p n h d", h=2, d=HD)
        v_bank = lambda b: heads(ps[:, 2 * (b % 2):2 * (b % 2) + 2, :].rearrange("p a c -> p (a c)"))
        vpart = lambda b, k: vaug[:, b, :, :, k * 2 * VG:(k + 1) * 2 * VG].rearrange("p i n (h c) -> p (i n) h c", h=2)[:, :, :, 0:HD]

        row_bias = lambda i: rowb[:, i * P:(i + 1) * P].rearrange("p (t c) -> p t c", t=1).broadcast_to((P, TB, P))

        LN_GROUPS = [(0, TB), (TB, NT)]
        NU = E * NB
        OUT_GROUPS = [(b * TB, (b + 1) * TB) for b in range(NB - 1)] + [(NT - TB, NT - TB // 2), (NT - TB // 2, NT)]
        EXPM_STEPS = EXPM_DEGREE + 1 + 2 * EXPM_SQUARINGS + 3

        block = ctx.enter_context(nc.Block())

        @block.sync
        def _(sp):
            for b in range(NB):
                sp.dma_start(xs[:, b * TB:(b + 1) * TB, :], x[b].rearrange("(t p) d -> p t d", p=P)).then_inc(x_in[b], 16)
                if b == 0:
                    sp.dma_start(vec[:, :], vecs).then_inc(s["vecs_in"], 16)
                    sp.dma_start(wloc[:, :], w_loc).then_inc(s["wloc_in"], 16)
            sp.dma_start(wm[:, :], w_more).then_inc(s["wmore_in"], 16)
            sp.dma_start(b1c[:, :], b1_cols).then_inc(s["b1_in"], 16)
            sp.dma_start(b2s[:, :], b2).then_inc(s["b1_in"], 16)
            sp.wait_ge(s["stacks_set"], 4)
            def parts_out(b):
                sp.wait_ge(s["part3_done"], b + 1)
                sp.dma_start(q_scratch[b].rearrange("k r n -> r k n"), qks[:, b % 2, :, 0:S]).then_inc(scratch_out[b], 16)
                sp.dma_start(k_scratch[b].rearrange("k r n -> r k n"), qks[:, b % 2, :, S:QK]).then_inc(scratch_out[b], 16)

            def rows_back(b, terms, scratch, dst, done):
                cols = scratch.shape[3]
                for half in range(2):
                    for t, first, step, count in terms:
                        r0 = half * 64 + HD * t
                        src = bass.AP(tensor=scratch.tensor, offset=((b * SPLITS + first) * P + half * 64) * cols,
                                      ap=[[step * P * cols, count], [NPAIR * cols, HD], [1, NPAIR * cols]])
                        sp.dma_start(dst[r0:r0 + HD * count].rearrange("r n c -> r (n c)"), src).then_inc(done[b], 16)

            def q_back(b):
                sp.wait_ge(scratch_out[b], 32)
                if b >= 1:
                    sp.wait_ge(s["q_spread"], 8 * b)
                rows_back(b, QTERM, q_scratch, qin, q_in)

            def k_back(b):
                sp.wait_ge(scratch_out[b], 32)
                if b >= 3:
                    sp.wait_ge(s["st_ps"], 2 * NPAIR * (b - 2))
                rows_back(b, KTERM, k_scratch, kst[:, b % 3], k_in)

            parts_out(0)
            q_back(0)
            for b in range(1, 4):
                parts_out(b)
                k_back(b - 1)
            q_back(1)
            q_back(2)
            k_back(3)
            q_back(3)
            sp.wait_ge(s["q_spread"], 8 * NB)
            def weights(e):
                if e >= 2:
                    sp.wait_ge(s["w_split"], 4 * (e - 1))
                sp.dma_start(w1r[:, e % 2, :], w1[e]).then_inc(w_in[e % 2], 16)
                sp.dma_start(w2r[:, e % 2, :, :], w2[e].rearrange("(c p) d -> p c d", p=P)).then_inc(w_in[e % 2], 16)
            weights(0)
            weights(1)
            sp.wait_ge(s["wdT_made"], NB)
            sp.dma_start(routing_scratch, wdT[:, :]).then_inc(s["routing_out"], 16)
            sp.wait_ge(s["routing_out"], 16)
            for u in range(NU):
                e, g = divmod(u, NB)
                if u >= WB:
                    sp.wait_ge(s["y_scaled"], u - WB + 1)
                row = bass.AP(tensor=routing_scratch.tensor, offset=e * TOK + g * S, ap=[[0, P], [1, S]])
                sp.dma_start(wb[:, u % WB, :], row).then_inc(wb_in[u % WB], 16)
                if g == NB - 1 and 2 <= e + 1 < E:
                    weights(e + 1)
            for k, (t0, t1) in enumerate(OUT_GROUPS):
                sp.wait_ge(s["tile_done"], t1)
                b, t = divmod(t0, TB)
                sp.dma_start(out[b, t * P:(t + t1 - t0) * P, :].rearrange("(t p) d -> p t d", p=P), xs[:, t0:t1, :]).then_inc(s["out_written"], 16)
            sp.wait_ge(s["out_written"], 16 * len(OUT_GROUPS))

        @block.gpsimd
        def _(pool):
            nc.gpsimd.memset(ident[:, :], 0.0).then_inc(s["consts_made"], 1)
            nc.gpsimd.memset(hA[:, :, 0:HALF], 0.0).then_inc(s["pads_set"], 1)
            nc.gpsimd.memset(hA[:, :, HALF + S:SP], 0.0).then_inc(s["pads_set"], 1)
            pool.wait_ge(s["consts_made"], 1)
            nc.gpsimd.affine_select(out=ident[:, :], in_=ident[:, :], compare_op=ALU.not_equal, fill=1.0,
                                    base=0, pattern=[[-1, P]], channel_multiplier=1).then_inc(s["consts_made"], 1)
            pool.dma_start(row1, rows).then_inc(s["rows_in"], 16)
            for half in range(2):
                src = bass.AP(tensor=rel_t.tensor, offset=0, ap=[[1, BQ], [rel_t.shape[1], NHEAD], [1, P]])
                pool.dma_start(tbr[half * 64:half * 64 + 64, :, :], src).then_inc(s["rel_in"], 16)
            pairs = lambda a: a.bitcast(f32)
            nc.gpsimd.memset(pairs(qin[:, :, :]), BF16_ONES).then_inc(s["stacks_set"], 1)
            nc.gpsimd.memset(kst[:, :, :, 0:HALF], NEG / 16).then_inc(s["stacks_set"], 1)
            nc.gpsimd.memset(kst[:, :, :, HALF + S:SP], NEG / 16).then_inc(s["stacks_set"], 1)
            nc.gpsimd.memset(pairs(kst[:, :, :, :])[:, :, :, HALF // 2:(HALF + S) // 2], 0.0).then_inc(s["stacks_set"], 1)
            pool.wait_ge(s["stacks_set"], 4)
            pool.wait_ge(s["rel_turned"], 1)
            for half in range(2):
                t = tb[half * 64:half * 64 + 64, :, :]
                nc.gpsimd.affine_select(out=t, in_=t, compare_op=ALU.is_ge, fill=NEG, base=0,
                                        pattern=[[0, NHEAD], [1, P]], channel_multiplier=-1).then_inc(s["band_masked"], 1)
            for half in range(2):
                t = tb[half * 64:half * 64 + 64, :, :]
                pool.wait_ge(s["band_masked"], 2)
                nc.gpsimd.affine_select(out=t, in_=t, compare_op=ALU.is_ge, fill=NEG, base=2 * HALF,
                                        pattern=[[0, NHEAD], [-1, P]], channel_multiplier=1).then_inc(s["band_masked"], 1)
            pool.wait_ge(s["band_masked"], 4)
            va = vaug[:, :, :, :, :].rearrange("p b i n c -> p (b i n) c")
            for k in range(SPLITS):
                for h in range(2):
                    c = (2 * k + h) * VG + HD
                    nc.gpsimd.memset(va[:, :, c:c + 1], 1.0 if k == 0 else 0.0).then_inc(s["vaug_set"], 1)
            nc.gpsimd.memset(pairs(qst[:, :, :, :, :]), 0.0).then_inc(s["qst_set"], 1)
            def v_third(b):
                pool.wait_ge(s["v2_done"], b + 1)
                nc.gpsimd.tensor_tensor(vpart(b, 2), heads(vres), vpart(b, 1), ALU.subtract).then_inc(s["v3_done"], 1)

            v_third(0)
            pool.wait_ge(s["v3_done"], 1)
            nc.gpsimd.memset(id64[:, :, :], 0.0).then_inc(s["id_zeros"], 1)
            nc.gpsimd.memset(pairs(mv[0:64, :, :]), 0.0).then_inc(s["id_zeros"], 1)
            pool.wait_ge(s["id_zeros"], 2)
            for half in range(2):
                o = 64 * half
                nc.gpsimd.affine_select(out=id64[o:o + 64, :, :], in_=id64[o:o + 64, :, :], compare_op=ALU.not_equal, fill=1.0,
                                        base=0, pattern=[[0, 4], [-1, BQ]], channel_multiplier=1).then_inc(s["mv_set"], 1)
            pool.wait_ge(s["mv_set"], 2)
            v_third(1)
            pool.wait_ge(s["v3_done"], 2)
            for half in range(2):
                m3 = mv[0:64, half, :].rearrange("p (n c) -> p n c", c=BQ)
                nc.gpsimd.affine_select(out=m3, in_=m3, compare_op=ALU.not_equal, fill=1.0,
                                        base=0, pattern=[[0, TOK // BQ], [-1, BQ]], channel_multiplier=1).then_inc(s["mv_set"], 1)
            pool.wait_ge(s["mv_set"], 4)
            v_third(2)
            pool.wait_ge(s["v3_done"], 3)
            picks = blo[64:88, :, :].rearrange("p (n a) c -> p n a c", a=2)
            nc.gpsimd.memset(pairs(blo[64:88, :, :]), 0.0).then_inc(s["picks_made"], 1)

            def pick(k):
                pool.wait_ge(s["picks_made"], k + 1)
                nc.gpsimd.affine_select(out=picks, in_=picks, compare_op=ALU.not_equal, fill=1.0, base=-8 * k,
                                        pattern=[[-1, NPAIR], [0, 2], [0, P]], channel_multiplier=1).then_inc(s["picks_made"], 1)
            pick(0)
            pool.wait_ge(s["picks_made"], 2)
            v_third(3)
            pool.wait_ge(s["v3_done"], 4)
            pick(1)
            pick(2)
            pool.wait_ge(s["picks_made"], 1 + SPLITS)
            pool.wait_ge(s["residual_cols"], 1)
            pool.wait_ge(s["z_ready"], NT)
            for t in range(NT):
                nc.gpsimd.tensor_scalar(xs[:, t, :], xs[:, t, :], st[:, t, 13:14], st[:, t, 15:16], ALU.mult, ALU.add).then_inc(s["residual_made"], 1)
            for n in range(NPAIR * NB):
                pool.wait_ge(s["p_done"], 2 * n + 2)
                pool.wait_ge(s["p1_done"], 2 * n + 2)
                if n >= 2:
                    pool.wait_ge(s["pv_ps"], n - 1)
                nc.gpsimd.tensor_tensor(p2[:, n % 2, :], pe[:, n % 2, :], p1[:, n % 2, :], ALU.subtract).then_inc(s["p2_done"], 1)
                if n % NPAIR == 2:
                    b = n // NPAIR
                    pool.wait_ge(s["residual_made"], (b + 1) * TB)
                    t = slice(b * TB, (b + 1) * TB)
                    nc.gpsimd.tensor_tensor(xs[:, t, :], xs[:, t, :], row_bias(2), ALU.add).then_inc(s["residual_biased"], 1)
            pool.wait_ge(s["proj_added"], NB)
            for b in range(NB):
                pool.wait_ge(s["gelu_done"], 3 * (b + 1))
                t = slice(b * TB, (b + 1) * TB)
                nc.gpsimd.tensor_tensor(xs[:, t, :], xs[:, t, :], abn[:, t, 0:P], ALU.add).then_inc(s["base_made"], 1)

        @block.tensor
        def _(te):
            mm = nc.tensor.matmul

            te.wait_ge(s["rows_in"], 16)
            te.wait_ge(s["ones_made"], 1)
            mm(ps[:, 7, 0:3 * P + E], ones1[:, :], row1, start=True, stop=True).then_inc(s["rows_ps"], 1)
            te.wait_ge(s["consts_made"], 2)
            for b in range(NB):
                for t in range(TB):
                    te.wait_ge(s["z_ready"], b * TB + t + 1)
                    last = nc.tensor.transpose(ps[:, b, t * P:(t + 1) * P], z[:, t, :], ident[:, :])
                    last.then_inc(s["zT_done"], 1)

            te.wait_ge(s["wloc_in"], 16)
            te.wait_ge(s["pads_set"], 2)
            te.wait_ge(s["rowb_made"], 1)
            te.wait_ge(s["hF_done"], 1)
            for b in range(NB):
                te.wait_ge(s["hA_done"], b + 1)
                if b >= 1:
                    te.wait_ge(s["qk32_done"], 2 * b)
                mm(ps[:, 4, :], wloc[:, 0:P], hA[:, b, HALF:HALF + S], start=True, stop=True)
                mm(ps[:, 5, 0:SP // 2], wloc[:, P:2 * P], hA[:, b, 0:SP // 2], start=True, stop=True)
                mm(ps[:, 6, 0:SP // 2], wloc[:, P:2 * P], hA[:, b, SP // 2:SP], start=True, stop=True).then_inc(s["qk_ps"], 1)
                te.wait_ge(s["hF_done"], 2 if b == 0 else NB)
                if b >= 2:
                    te.wait_ge(s["vres_done"], b - 1)
                for i in range(NBLK):
                    last = mm(ps[:, 2 * (b % 2) + i // 4, (i % 4) * P:(i % 4 + 1) * P], hA[:, b, i * BQ:i * BQ + P],
                              wloc[:, 2 * P:3 * P], start=True, stop=True)
                last.then_inc(s["v_ps"], 1)
                if b == 0:
                    te.wait_ge(s["wmore_in"], 16)
                for t in range(b * TB, (b + 1) * TB):
                    last = mm(ps[:, 7, t * E:(t + 1) * E], hF[:, t * P:(t + 1) * P], wm[:, M_GATE:M_GATE + E], start=True, stop=True)
                last.then_inc(s["logit_ps"], 1)

            def scores_for_max(b, p, g):
                if g == 0:
                    if p % 2 == 0:
                        te.wait_ge(s["q_spread"], 8 * b + p + 2)
                    if p == 0:
                        te.wait_ge(k_in[b], 16 * 2 * NTERM)
                        if b >= 1:
                            te.wait_ge(s["negmaxT_done"], b)
                n = (b * NPAIR + p) * 2 + g
                if n >= 2:
                    te.wait_ge(s["max_taken"], n - 1)
                mm(ps[:, g, :], identh[:, :], bs[:, p:p + 1, :].broadcast_to((P, 4, P)), start=True, stop=False)
                for i in range(4):
                    k0 = (4 * g + i) * BQ
                    last = mm(ps[:, g, i * P:(i + 1) * P], qst[:, b % 2, p, 4 * g + i, :],
                              kst[:, b % 3, p, k0:k0 + P], start=False, stop=(i == 3))
                last.then_inc(s["s_ps"], 1)

            def negmax_rows(b):
                te.wait_ge(s["negmax_split"], b + 1)
                tv = ps[:, 0, :].bitcast(bf16).rearrange("p (i c) -> p i c", c=P)
                for i in range(NBLK):
                    last = nc.tensor.transpose(tv[0:24, i, :], nms[:, i, :, :].rearrange("p a c -> p (a c)"), identh[:, :])
                last.then_inc(s["negmaxT_ps"], 1)

            def scores_for_exp(b, p, g):
                m = 2 * (b * NPAIR + p) + g
                if m >= 3:
                    te.wait_ge(s["p1_done"], m - 2)
                bank = ps[:, 2 + m % 3, :]
                for half in range(2):
                    h = 2 * p + half
                    o = bank[:, half * 256:(half + 1) * 256]
                    cols = b * S + g * 256
                    mm(o, bhm[:, h, :], id64[:, :, :].rearrange("p a c -> p (a c)"), start=(half == 0), stop=False)
                    mm(o, blo[:, h, :], mv[:, half, cols:cols + 256], start=False, stop=False)
                ob = bank.rearrange("p (a i c) -> p a i c", a=2, c=BQ)
                for i in range(4):
                    k0 = (4 * g + i) * BQ
                    last = mm(ob[:, :, i, :], kst[:, b % 3, p, k0:k0 + P], qst[:, b % 2, p, 4 * g + i, :],
                              start=False, stop=(i == 3))
                last.then_inc(s["st_ps"], 1)

            def values(b, p):
                n = b * NPAIR + p
                if n >= 2:
                    te.wait_ge(s["pv_taken"], n - 1)
                te.wait_ge(s["p2_done"], n + 1)
                for i in range(NBLK):
                    o = ps[:, 6 + p % 2, i * VW:(i + 1) * VW]
                    c = slice(i * P, (i + 1) * P)
                    mm(o, p1[:, n % 2, c], vaug[:, b, i, p, :], start=True, stop=False)
                    last = mm(o, p2[:, n % 2, c], vaug[:, b, i, p, :], start=False, stop=True)
                last.then_inc(s["pv_ps"], 1)

            def outputs_transposed(b):
                te.wait_ge(s["o_normed"], b + 1)
                for i in range(NBLK // 2):
                    last = nc.tensor.transpose(ps[:, 5, i * P:(i + 1) * P],
                                               on[:, 2 * i:2 * i + 2, :].rearrange("p a c -> p (a c)"), ident[:, :])
                last.then_inc(s["oT_ps"], 1)

            def linear(k):
                b, j = divmod(k, LIN_STEPS)
                if k >= 1:
                    te.wait_ge(s["lin_free"], k)
                if j == 1 and b >= 1:
                    te.wait_ge(s["oT_done"], b)
                tok = lambda t: hA[:, b, HALF + t * P:HALF + (t + 1) * P]
                o = ps[:, 5, :]
                if j == 0:
                    last = mm(o, wmat(M_QLIN), hA[:, b, HALF:HALF + S], start=True, stop=True)
                elif j in (1, 2):
                    for t in range(TB):
                        last = mm(o[:, t * P:(t + 1) * P], tok(t), wmat(M_KLIN if j == 1 else M_VLIN), start=True, stop=True)
                elif j == 3:
                    te.wait_ge(s["lin_k_made"], b + 1)
                    for t in range(TB):
                        last = mm(o[:, 0:P + 1], kl[:, t, :], vl[:, t, :], start=(t == 0), stop=(t == TB - 1))
                elif j in (4, 5):
                    te.wait_ge(s["lin_q_made"], b + 1)
                    for i in range(2):
                        t = 2 * (j - 4) + i
                        last = mm(o[:, i * (P + 1):(i + 1) * (P + 1)], qlT[:, t * P:(t + 1) * P], kvs[:, :], start=True, stop=True)
                else:
                    for t in range(TB):
                        last = nc.tensor.transpose(o[:, t * P:(t + 1) * P], ln_[:, t, :], ident[:, :])
                last.then_inc(s["lin_ps"], 1)

            def gate_hidden(b, bank):
                c = slice(b * S, (b + 1) * S)
                o = ps[:, bank, :]
                mm(o, wmat(M_G1H), hA[:, b, HALF:HALF + S], start=True, stop=False)
                mm(o, wmat(M_G1LIN), lin_t[:, c], start=False, stop=False)
                mm(o, wmat(M_G1WIN), win_t[:, c], start=False, stop=True).then_inc(s["gh_ps"], 1)

            def routing_transposed(b):
                if b == 0:
                    te.wait_ge(s["routed"], 1)
                    te.wait_ge(s["gh_done"], NB - 1)
                elif b >= 2:
                    te.wait_ge(s["wdT_made"], b - 1)
                for t in range(TB):
                    last = nc.tensor.transpose(ps[0:E, b % 2, t * P:(t + 1) * P], rt[:, 6, b * TB + t, :], ident[:, :])
                last.then_inc(s["wdT_ps"], 1)

            def beside_last_batch(p):
                if 1 <= p <= 3:
                    if p == 1:
                        te.wait_ge(s["oT_done"], NB - 2)
                        te.wait_ge(s["lin_free"], LIN_STEPS * (NB - 1))
                        te.wait_ge(s["max_taken"], 2 * NPAIR * NB)
                        te.wait_ge(s["negmaxT_done"], NB)
                    if p == 3:
                        te.wait_ge(s["oT_done"], NB - 1)
                        te.wait_ge(s["gh_done"], 1)
                    gate_hidden(p - 1, (p - 1) % 2)
                elif p >= 4:
                    routing_transposed(p - 4)

            te.wait_ge(s["low_made"], 1)
            te.wait_ge(s["stacks_set"], 4)
            te.wait_ge(s["qst_set"], 1)
            te.wait_ge(s["identh_made"], 1)
            te.wait_ge(s["vres_done"], NB - 1)
            for p in range(NPAIR):
                for g in range(2):
                    scores_for_max(0, p, g)
            te.wait_ge(s["tables_made"], 2)
            te.wait_ge(s["picks_made"], 1 + SPLITS)
            te.wait_ge(s["mv_set"], 4)
            te.wait_ge(s["vl_ones"], 1)
            te.wait_ge(s["vres_done"], NB)
            te.wait_ge(s["qk32_done"], 2 * NB)
            te.wait_ge(s["logit_made"], 1)
            te.wait_ge(s["v3_done"], NB)
            te.wait_ge(s["vaug_set"], 2 * SPLITS)
            negmax_rows(0)
            for b in range(NB):
                for p in range(NPAIR):
                    if p == 0:
                        te.wait_ge(s["negmaxT_done"], b + 1)
                    ahead = AHEAD[p] if b + 1 < NB else []
                    for g in range(2):
                        scores_for_exp(b, p, g)
                        if ahead:
                            scores_for_max(b + 1, ahead[0], g)
                    if b + 1 < NB and p == NPAIR - 1:
                        negmax_rows(b + 1)
                    n = b * NPAIR + p
                    if n >= 1:
                        values(*divmod(n - 1, NPAIR))
                    if p != 1:
                        linear(b * LIN_STEPS + p - (p > 1))
                    elif b >= 1:
                        te.wait_ge(s["lin_free"], LIN_STEPS * b + 1)
                        outputs_transposed(b - 1)
                    for q in ahead[1:]:
                        for g in range(2):
                            scores_for_max(b + 1, q, g)
                    if b == NB - 1:
                        beside_last_batch(p)

            def gate(b, bank):
                te.wait_ge(s["gh_done"], b + 1)
                mm(ps[:, bank, :], wmat(M_WG2), gh[:, b, :], start=True, stop=True).then_inc(s["gate_ps"], 1)

            def mixture_bias(b, bank):
                mm(ps[:, bank, :], b2s[:, :], wdT[:, b * S:(b + 1) * S], start=True, stop=True).then_inc(s["acc_ps"], 1)

            def project(b, bank):
                te.wait_ge(s["mixed"], b + 1)
                for t in range(TB):
                    last = mm(ps[:, bank, t * P:(t + 1) * P], gd[:, b, t * P:(t + 1) * P], wmat(M_WO), start=True, stop=True)
                last.then_inc(s["proj_ps"], 1)

            te.wait_ge(s["p1_done"], 2 * NPAIR * NB)
            for b in range(NB - 1):
                gate(b, 2 + b)
            values(NB - 1, NPAIR - 1)
            te.wait_ge(s["wdT_made"], NB)
            te.wait_ge(s["b1_in"], 32)
            mixture_bias(0, 1)
            mixture_bias(1, 0)
            te.wait_ge(s["gate_done"], 1)
            mixture_bias(2, 2)
            te.wait_ge(s["gate_done"], 2)
            mixture_bias(3, 3)
            te.wait_ge(s["lin_free"], LIN_STEPS * NB)
            outputs_transposed(NB - 1)
            te.wait_ge(s["pv_taken"], NPAIR * NB)
            project(0, 6)
            te.wait_ge(s["oT_done"], NB)
            te.wait_ge(s["acc_made"], 2)
            gate_hidden(NB - 1, 1)
            project(1, 7)
            gate(NB - 1, 0)
            te.wait_ge(s["gate_done"], 3)
            project(2, 4)
            te.wait_ge(s["acc_made"], NB)
            te.wait_ge(s["gate_done"], NB)

            def first_layer(u):
                e, g = divmod(u, NB)
                c = slice(g * S, (g + 1) * S)
                te.wait_ge(s["w_split"], 4 * e + 2)
                if e == 0:
                    te.wait_ge(s["ffn_split"], g + 1)
                for j in range(2):
                    if u >= 1:
                        te.wait_ge(s["hid_done"], 4 * (u - 1) + 2 * j + 2)
                    for ch in (2 * j, 2 * j + 1):
                        o = ps[:, ch, :]
                        w = slice(ch * P, (ch + 1) * P)
                        mm(o, w1h[:, e % 2, w], hFh[:, c], start=True, stop=False)
                        mm(o, w1h[:, e % 2, w], hFl[:, c], start=False, stop=False)
                        mm(o, w1l[:, e % 2, w], hFh[:, c], start=False, stop=True).then_inc(s["h_ps"], 1)

            def second_layer(u):
                e = u // NB
                if u >= 2:
                    te.wait_ge(s["y_scaled"], u - 1)
                else:
                    te.wait_ge(s["proj_added"], NB - 1 + u)
                te.wait_ge(s["w_split"], 4 * e + 4)
                o = ps[:, 4 + u % 2, :]
                for ch in range(NC):
                    if ch % 2 == 0:
                        te.wait_ge(s["hidl_done"], 2 * u + ch // 2 + 1)
                        te.wait_ge(s["hidh_done"], 2 * u + ch // 2 + 1)
                    mm(o, w2h[:, e % 2, ch, :], hidh[:, u % 2, ch, :], start=(ch == 0), stop=False)
                    mm(o, w2h[:, e % 2, ch, :], hidl[:, u % 2, ch, :], start=False, stop=False)
                    last = mm(o, w2l[:, e % 2, ch, :], hidh[:, u % 2, ch, :], start=False, stop=(ch == NC - 1))
                last.then_inc(s["y_ps"], 1)

            def gelu_branch_steps():
                te.wait_ge(s["imix_made"], 1)
                for b in range(NB):
                    yield mm(ps[:, 7, :], wmat(M_ABEL), hF[:, b * S:(b + 1) * S], start=True, stop=True)
                    for j in range(2):
                        for i in range(2):
                            t = 2 * j + i
                            last = mm(ps[:, 7, i * (P + 1):(i + 1) * (P + 1)], ab[:, b % 2, t * P:(t + 1) * P],
                                      imix[:, :], start=True, stop=True)
                        yield last

            def expm_steps():
                gen = wm[:, M_GEN * P:(M_GEN + NG) * P].rearrange("p (i c) -> p i c", c=P)
                o = ps[:, 6, 0:NG * P].rearrange("p (i c) -> p i c", c=P)
                te.wait_ge(s["expm_seed"], 1)
                for i in range(NG):
                    last = nc.tensor.transpose(o[:, i, :], gen[:, i, :], ident[:, :])
                yield last
                k = 0
                for _ in range(EXPM_DEGREE - 1):
                    for i in range(NG):
                        last = mm(o[:, i, :], bt[:, i, :], pw[:, k % 2, i, :], start=True, stop=True)
                    yield last
                    k += 1
                for i in range(NG):
                    last = nc.tensor.transpose(o[:, i, :], pw[:, k % 2, i, :], ident[:, :])
                yield last
                kt = 0
                for _ in range(EXPM_SQUARINGS):
                    for i in range(NG):
                        last = mm(o[:, i, :], pwt[:, kt % 2, i, :], pw[:, k % 2, i, :], start=True, stop=True)
                    yield last
                    for i in range(NG):
                        last = mm(o[:, i, :], pw[:, k % 2, i, :], pwt[:, kt % 2, i, :], start=True, stop=True)
                    yield last
                    k += 1
                    kt += 1
                yield mm(o[:, 0, :], pw[:, k % 2, 1, :], pwt[:, kt % 2, 0, :], start=True, stop=True)
                mm(o[:, 0, :], mt[:, 0, :], pw[:, k % 2, 2, :], start=True, stop=True)
                yield mm(o[:, 1, :], pw[:, k % 2, 2, :], mt[:, 0, :], start=True, stop=True)
                yield mm(o[:, 0, 0:1], mt[:, 1, :], vcol(V_MIX2), start=True, stop=True)

            def rotation(b, banks):
                te.wait_ge(s["y_added"], NU - NB + b + 1)
                for j in range(2):
                    n = 2 * b + j
                    if 2 <= n < 2 * (NB - 1):
                        te.wait_ge(s["rot_done"], n - 1)
                    for i in range(2):
                        t = b * TB + 2 * j + i
                        last = mm(ps[:, banks[j], i * (P + 1):(i + 1) * (P + 1)], acc[:, t * P:(t + 1) * P], rr[:, :],
                                  start=True, stop=True)
                    last.then_inc(s["rot_ps"], 1)

            gelu_steps, ex_steps = gelu_branch_steps(), expm_steps()
            for u in range(NU + 1):
                if u < NU:
                    first_layer(u)
                if u == 0:
                    project(NB - 1, 5)
                if u >= 1:
                    second_layer(u - 1)
                if u < 3 * NB:
                    if u >= 1:
                        te.wait_ge(s["gelu_done"], u)
                    else:
                        te.wait_ge(s["proj_added"], 2)
                    next(gelu_steps).then_inc(s["gelu_ps"], 1)
                if u < EXPM_STEPS:
                    if u >= 1:
                        te.wait_ge(s["ex_done"], u)
                    next(ex_steps).then_inc(s["ex_ps"], 1)
                if u == NU - 2:
                    te.wait_ge(s["ex_done"], EXPM_STEPS)
                    te.wait_ge(s["gelu_done"], 3 * NB)
                if u >= NU - 2:
                    rotation(u - (NU - 2), (6, 7))
            assert next(gelu_steps, None) is None and next(ex_steps, None) is None
            te.wait_ge(s["hid_done"], NC * NU)
            rotation(NB - 1, (0, 1))

        @block.scalar
        def _(act):
            A = nc.scalar.activation

            def roots(g):
                t0, t1 = LN_GROUPS[g]
                for n in range(2):
                    act.wait_ge(s["z_used"], 2 * g + n + 1)
                    A(st[:, t0:t1, 9], st[:, t0:t1, 8], ACT.Sqrt).then_inc(s["sqrt_done"], 1)

            def attention_input(b):
                act.wait_ge(s["zT_done"], TB * (b + 1))
                A(hA[:, b, HALF:HALF + S], ps[:, b, :], ACT.Identity, bias=vcol(V_B), scale=vcol(V_G)).then_inc(s["hA_done"], 1)

            roots(0)
            act.wait_ge(s["vecs_in"], 16)
            act.wait_ge(s["rows_ps"], 1)
            A(rowb[:, :], ps[:, 7, 0:3 * P + E], ACT.Copy).then_inc(s["rowb_made"], 1)
            attention_input(0)
            roots(1)
            for b in range(1, NB):
                attention_input(b)
            def v_second(b):
                act.wait_ge(s["vres_done"], b + 1)
                A(vpart(b, 1), heads(vres), ACT.Copy).then_inc(s["v2_done"], 1)

            act.wait_ge(s["band_masked"], 4)
            A(thi[:, :, :], tb[:, :, :], ACT.Copy).then_inc(s["thi_done"], 1)
            act.wait_ge(s["small_made"], 1)
            for b in range(NB):
                act.wait_ge(s["qk_ps"], b + 1)
                if b >= 2:
                    act.wait_ge(s["part3_done"], b - 1)
                A(qk32[:, b % 2, 0:S], ps[:, 4, :], ACT.Identity, bias=small[:, 0:1], scale=SCALE).then_inc(s["qk32_done"], 1)
                A(qk32[:, b % 2, S:QK].rearrange("p (a c) -> p a c", a=2), ps[:, 5:7, 0:SP // 2], ACT.Identity,
                  bias=vcol(V_BKLOC)).then_inc(s["qk32_done"], 1)
                act.wait_ge(s["qk32_done"], 2 * (b + 1))
                if b >= 2:
                    act.wait_ge(scratch_out[b - 2], 32)
                A(qks[:, b % 2, 0, :], qk32[:, b % 2, :], ACT.Copy).then_inc(s["part1_done"], 1)
                act.wait_ge(s["v_ps"], b + 1)
                A(vpart(b, 0), v_bank(b), ACT.Copy).then_inc(s["v1_done"], 1)
                if b == 0:
                    act.wait_ge(s["tmid_done"], 1)
                    A(thi[:, :, :], tbr[:, :, :], ACT.Copy).then_inc(s["thi_done"], 1)
                if b >= 1:
                    v_second(b - 1)
            def spread(b, c):
                if c == 0:
                    act.wait_ge(q_in[b], 16 * 2 * NTERM)
                for half in range(2):
                    o = 64 * half
                    A(qst[o:o + 64, b % 2, 2 * c:2 * c + 2, :, o:o + BQ].rearrange("p n i c -> p (n i) c"),
                      qin[o:o + 64, 2 * c:2 * c + 2, :].rearrange("p n (i c) -> p (n i) c", c=BQ), ACT.Copy).then_inc(s["q_spread"], 1)

            act.wait_ge(s["qst_set"], 1)
            for c in range(4):
                spread(0, c)
            v_second(NB - 1)
            act.wait_ge(s["tmid_done"], 1)
            A(bhm[0:64, :, :], tb[0:64, :, :], ACT.Copy).then_inc(s["tables_made"], 1)
            A(bhm[64:128, :, :], tbr[64:128, :, :], ACT.Copy).then_inc(s["tables_made"], 1)
            for c in range(4):
                spread(1, c)
            A(small[:, 2:3], small[:, 1:2], ACT.Exp)
            act.wait_ge(s["part3_done"], NB)
            for b in range(NB):
                act.wait_ge(scratch_out[b], 32)
            def linear(k):
                b, j = divmod(k, LIN_STEPS)
                if j in (1, 2):
                    act.wait_ge(s["lin_min"], 2 * b + j)
                    A(lt[:, 1, :], lt[:, 1, :], ACT.Exp).then_inc(s["lin_exp"], 1)
                if j in (0, 3, 6):
                    act.wait_ge(s["lin_ps"], k + 1)
                if j == 0:
                    A(lt[:, 0, :], ps[:, 5, :], ACT.Identity, bias=vcol(V_BQLIN)).then_inc(s["lin_free"], 1)
                elif j == 3:
                    A(kvs[:, :], ps[:, 5, 0:P + 1], ACT.Copy).then_inc(s["lin_free"], 1)
                elif j == 6:
                    A(lin_t[:, b * S:(b + 1) * S], ps[:, 5, :], ACT.Copy).then_inc(s["lin_free"], 1)

            def outputs_transposed(b):
                act.wait_ge(s["oT_ps"], b + 1)
                src = ps[:, 5, :].rearrange("p (i a c) -> p i a c", a=2, c=BQ)
                for half in range(2):
                    dst = win_t[64 * half:64 * half + 64, b * S:(b + 1) * S].rearrange("p (i k c) -> p i k c", k=2, c=BQ)
                    for k in range(2):
                        o = 64 * k
                        v = V_BV0 if half == k else V_BV1
                        last = A(dst[:, :, k, :], src[o:o + 64, :, half, :], ACT.Identity, bias=vec[o:o + 64, v:v + 1])
                last.then_inc(s["oT_done"], 1)

            def gate_relu(b, bank):
                act.wait_ge(s["gh_ps"], b + 1)
                A(gh[:, b, :], ps[:, bank, :], ACT.Relu, bias=vcol(V_BG1)).then_inc(s["gh_done"], 1)

            def beside_last_batch(p):
                if 1 <= p <= 3:
                    gate_relu(p - 1, (p - 1) % 2)
                elif p >= 4:
                    b = p - 4
                    act.wait_ge(s["wdT_ps"], b + 1)
                    A(wdT[:, b * S:(b + 1) * S], ps[0:E, b % 2, :], ACT.Copy).then_inc(s["wdT_made"], 1)

            for n in range(NPAIR * NB):
                for g in range(2):
                    m = 2 * n + g
                    act.wait_ge(s["st_ps"], m + 1)
                    if n >= 2 and g == 0:
                        act.wait_ge(s["p2_done"], n - 1)
                        act.wait_ge(s["pv_ps"], n - 1)
                    src = ps[:, 2 + m % 3, :].rearrange("p (a i c) -> p i a c", a=2, c=BQ)
                    for buf, done in ((pe, "p_done"), (p1, "p1_done")):
                        A(buf[:, n % 2, g * 512:(g + 1) * 512].rearrange("p (i a c) -> p i a c", a=2, c=BQ),
                          src, ACT.Exp, bias=small[:, 1:2]).then_inc(s[done], 1)
                b, p = divmod(n, NPAIR)
                if p != 1:
                    linear(b * LIN_STEPS + p - (p > 1))
                elif b >= 1:
                    outputs_transposed(b - 1)
                if b == NB - 1:
                    beside_last_batch(p)
                    if p == 3:
                        act.wait_ge(s["top_gap"], 1)
                        A(r1[:, 4, :], r1[:, 3, :], ACT.Exp).then_inc(s["top_ratio"], 1)

            def sigmoid(b, bank):
                act.wait_ge(s["gate_ps"], b + 1)
                A(gg[:, b, :], ps[:, bank, :], ACT.Sigmoid, bias=vcol(V_BG2)).then_inc(s["gate_done"], 1)

            def mixture_bias(b, bank):
                act.wait_ge(s["acc_ps"], b + 1)
                A(acc[:, b * S:(b + 1) * S], ps[:, bank, :], ACT.Copy).then_inc(s["acc_made"], 1)

            for b in range(NB - 1):
                sigmoid(b, 2 + b)
            for b, bank in enumerate((1, 0, 2, 3)):
                mixture_bias(b, bank)
            outputs_transposed(NB - 1)
            gate_relu(NB - 1, 1)
            sigmoid(NB - 1, 0)
            for u in range(NU):
                e = u // NB
                if u >= 2:
                    act.wait_ge(s["y_ps"], u - 1)
                    act.wait_ge(s["hidl_done"], 2 * (u - 1))
                for j in range(2):
                    for ch in (2 * j, 2 * j + 1):
                        act.wait_ge(s["h_ps"], NC * u + ch + 1)
                        A(hid[:, u % 2, ch, :], ps[:, ch, :], ACT.Gelu, bias=b1c[:, e * NC + ch:e * NC + ch + 1]).then_inc(s["hid_done"], 1)
                    act.wait_ge(s["hid_done"], NC * u + 2 * j + 2)
                    c = slice(2 * j, 2 * j + 2)
                    A(hidh[:, u % 2, c, :], hid[:, u % 2, c, :], ACT.Copy).then_inc(s["hidh_done"], 1)
                if u < 3 * NB:
                    b, j = divmod(u, 3)
                    act.wait_ge(s["gelu_ps"], u + 1)
                    if j == 0:
                        A(ab[:, b % 2, :], ps[:, 7, :], ACT.Gelu, bias=vcol(V_ABEL)).then_inc(s["gelu_done"], 1)
                    else:
                        t = b * TB + 2 * (j - 1)
                        A(abn[:, t:t + 2, :].rearrange("p t c -> p (t c)"), ps[:, 7, 0:2 * (P + 1)], ACT.Copy).then_inc(s["gelu_done"], 1)
            for k, (t0, t1) in enumerate(((0, 2 * TB), (2 * TB, 3 * TB), (3 * TB, 4 * TB))):
                act.wait_ge(s["rot_done"], t1 // 2)
                A(gs[:, t0:t1], gl[:, t0:t1], ACT.Sigmoid, bias=vcol(V_MIXB)).then_inc(s["gs_done"], 1)

        @block.vector
        def _(dve):
            V = nc.vector
            steps = [0]

            def link(ins):
                steps[0] += 1
                ins.then_inc(s["dve_step"], 1)
                dve.wait_ge(s["dve_step"], steps[0])

            def rsqrt(v, root, r, t, n, g):
                dve.wait_ge(s["sqrt_done"], 2 * g + n + 1)
                link(V.reciprocal(r, root))
                link(V.tensor_tensor(t, r, r, ALU.mult))
                link(V.tensor_tensor(t, t, v, ALU.mult))
                link(V.tensor_scalar(t, t, -0.5, 1.5, ALU.mult, ALU.add))
                link(V.tensor_tensor(r, r, t, ALU.mult))

            def ffn_input(b):
                dve.wait_ge(s["hA_done"], b + 1)
                V.tensor_scalar(hF[:, b * S:(b + 1) * S], ps[:, b, :], vcol(V_FG), vcol(V_FB), ALU.mult, ALU.add).then_inc(s["hF_done"], 1)

            V.memset(ones1[:, :], 1.0).then_inc(s["ones_made"], 1)
            V.memset(vl[:, :, P:P + 1], 1.0).then_inc(s["vl_ones"], 1)
            V.memset(small[:, 1:2], P_SHIFT)
            dve.wait_ge(s["vecs_in"], 16)
            V.tensor_scalar(small[:, 0:1], vcol(V_BQLOC), SCALE, None, ALU.mult).then_inc(s["small_made"], 1)
            for g, (t0, t1) in enumerate(LN_GROUPS):
                if g == 1:
                    dve.wait_ge(s["rel_in"], 32)
                    turned = bass.AP(tensor=lin_t, offset=P - 1, ap=[[TOK, P], [P, NHEAD], [-1, P]])
                    V.tensor_copy(tb[:, :, :], turned).then_inc(s["rel_turned"], 1)
                for t in range(t0, t1):
                    if t % TB == 0:
                        dve.wait_ge(x_in[t // TB], 16)
                    last = V.bn_stats(st[:, t, 0:6], xs[:, t, :])
                link(last)
                for t in range(t0, t1):
                    last = V.bn_aggr(st[:, t, 6:8], st[:, t, 0:6])
                link(last)
                mean, var, ve, root = (st[:, t0:t1, i] for i in (6, 7, 8, 9))
                ra, rb, tmp = (st[:, t0:t1, i] for i in (10, 11, 12))
                V.tensor_scalar(ve, var, EPS, None, ALU.add).then_inc(s["z_used"], 1)
                dve.wait_ge(s["z_used"], 2 * g + 1)
                rsqrt(ve, root, ra, tmp, 0, g)
                link(V.tensor_tensor(tmp, ra, ra, ALU.mult))
                link(V.tensor_tensor(tmp, tmp, var, ALU.mult))
                V.tensor_scalar(ve, tmp, EPS, None, ALU.add).then_inc(s["z_used"], 1)
                dve.wait_ge(s["z_used"], 2 * g + 2)
                rsqrt(ve, root, rb, tmp, 1, g)
                link(V.tensor_tensor(rb, ra, rb, ALU.mult))
                for b in range(t0 // TB, t1 // TB):
                    for t in range(b * TB, (b + 1) * TB):
                        if b >= 1:
                            dve.wait_ge(s["zT_done"], t - TB + 1)
                        V.tensor_scalar(z[:, t % TB, :], xs[:, t, :], st[:, t, 6:7], st[:, t, 11:12], ALU.subtract, ALU.mult).then_inc(s["z_ready"], 1)
                    if b >= 1:
                        ffn_input(b - 1)
            ffn_input(NB - 1)
            V.tensor_copy(identh[:, :], ident[:, :]).then_inc(s["identh_made"], 1)
            dve.wait_ge(s["thi_done"], 1)
            th = thi[:, :, :].rearrange("p (n a) c -> p n a c", a=2)
            for half in range(2):
                V.tensor_copy(bs[64 * half:64 * half + 64, :, :], th[64 * half:64 * half + 64, :, half, :])
            V.tensor_tensor(tbr[:, :, :], tb[:, :, :], thi[:, :, :], ALU.subtract).then_inc(s["tmid_done"], 1)
            link(V.tensor_scalar(st[:, :, 13], st[:, :, 10], 2.0, 1.0, ALU.mult, ALU.add))
            link(V.tensor_tensor(st[:, :, 14], st[:, :, 6], st[:, :, 10], ALU.mult))
            V.tensor_scalar(st[:, :, 15], st[:, :, 14], -2.0, None, ALU.mult).then_inc(s["residual_cols"], 1)
            for b in range(NB):
                dve.wait_ge(s["part1_done"], b + 1)
                left = qk32[:, b % 2, :]
                V.tensor_tensor(left, left, qks[:, b % 2, 0, :], ALU.subtract).then_inc(s["res1_done"], 1)
                dve.wait_ge(s["res1_done"], b + 1)
                V.tensor_copy(qks[:, b % 2, 1, :], left).then_inc(s["part2_done"], 1)
                dve.wait_ge(s["part2_done"], b + 1)
                V.tensor_tensor(qks[:, b % 2, 2, :], left, qks[:, b % 2, 1, :], ALU.subtract).then_inc(s["part3_done"], 1)
                dve.wait_ge(s["v1_done"], b + 1)
                if b >= 1:
                    dve.wait_ge(s["v3_done"], b)
                V.tensor_tensor(heads(vres), v_bank(b), vpart(b, 0), ALU.subtract).then_inc(s["vres_done"], 1)
                if b == 0:
                    dve.wait_ge(s["thi_done"], 2)
                    V.tensor_tensor(blo[0:64, :, :], tbr[0:64, :, :], thi[0:64, :, :], ALU.subtract).then_inc(s["low_made"], 1)
            dve.wait_ge(s["logit_ps"], NB)
            V.tensor_tensor(logit[:, :, :], ps[:, 7, 0:NT * E].rearrange("p (t e) -> p t e", e=E),
                            rowb[:, 3 * P:3 * P + E].rearrange("p (t e) -> p t e", t=1).broadcast_to((P, NT, E)), ALU.add).then_inc(s["logit_made"], 1)
            def routing():
                L = lambda i: rt[:, i, :, :]
                R = lambda i: r1[:, i, :]
                col = lambda a: a.rearrange("p (t c) -> p t c", c=1).broadcast_to((P, NT, E))
                dve.wait_ge(s["logit_made"], 1)
                for e in range(E):
                    last = V.memset(rt[:, 0, :, e], float(e) - 100.0)
                link(last)
                src = logit[:, :, :]
                for k in range(2):
                    m, first = R(k), L(1 + k)
                    link(V.tensor_reduce(m, src, AX.X, ALU.max))
                    link(V.tensor_tensor(L(3), src, col(m), ALU.is_equal))
                    link(V.tensor_tensor(L(4), L(3), L(0), ALU.mult))
                    link(V.tensor_reduce(R(2), L(4), AX.X, ALU.min))
                    link(V.tensor_tensor(first, L(4), col(R(2)), ALU.is_equal))
                    yield
                    if k == 0:
                        link(V.tensor_scalar(L(3), first, -3e38, None, ALU.mult))
                        link(V.tensor_tensor(L(5), src, L(3), ALU.add))
                        src = L(5)
                V.tensor_tensor(R(3), R(1), R(0), ALU.subtract).then_inc(s["top_gap"], 1)
                yield
                dve.wait_ge(s["top_ratio"], 1)
                link(V.tensor_scalar(R(5), R(4), 1.0, None, ALU.add))
                link(V.reciprocal(R(6), R(5)))
                link(V.tensor_tensor(R(7), R(4), R(6), ALU.mult))
                link(V.tensor_tensor(L(3), L(1), col(R(6)), ALU.mult))
                link(V.tensor_tensor(L(4), L(2), col(R(7)), ALU.mult))
                V.tensor_tensor(L(6), L(3), L(4), ALU.add).then_inc(s["routed"], 1)

            def take_max(b, p):
                for g in range(2):
                    n = (b * NPAIR + p) * 2 + g
                    dve.wait_ge(s["s_ps"], n + 1)
                    if b >= 1 and p == 0 and g == 0:
                        dve.wait_ge(s["negmax_split"], b)
                    V.tensor_reduce(nm[:, 4 * g:4 * g + 4, p], ps[:, g, :].rearrange("p (i c) -> p i c", c=P),
                                    AX.X, ALU.max, negate=True).then_inc(s["max_taken"], 1)

            def split_max(b):
                dve.wait_ge(s["max_taken"], 2 * NPAIR * (b + 1))
                if b >= 1:
                    dve.wait_ge(s["negmaxT_ps"], b)
                link(V.tensor_copy(nms[:, :, 0, :], nm[:, :, :]))
                link(V.tensor_tensor(nmr[:, :, :], nm[:, :, :], nms[:, :, 0, :], ALU.subtract))
                link(V.tensor_copy(nms[:, :, 1, :], nmr[:, :, :]))
                V.tensor_tensor(nms[:, :, 2, :], nmr[:, :, :], nms[:, :, 1, :], ALU.subtract).then_inc(s["negmax_split"], 1)

            def negmax_rows(b):
                dve.wait_ge(s["negmaxT_ps"], b + 1)
                tv = ps[:, 0, :].bitcast(bf16).rearrange("p (i a c) -> p i a c", a=2, c=BQ)
                for half in range(2):
                    last = V.tensor_copy(mv[64:88, half, b * S:(b + 1) * S].rearrange("p (i c) -> p i c", c=BQ), tv[0:24, :, half, :])
                last.then_inc(s["negmaxT_done"], 1)

            def linear(k):
                b, j = divmod(k, LIN_STEPS)
                bank = ps[:, 5, :].rearrange("p (t c) -> p t c", c=P)
                raw, low = lt[:, 0, :], lt[:, 1, :]
                rows = lambda a: a.rearrange("p (t c) -> p t c", c=P)
                bias = lambda i: row_bias(i)
                if j == 0:
                    dve.wait_ge(s["lin_free"], k + 1)
                    V.tensor_scalar(low, raw, 0.0, None, ALU.min).then_inc(s["lin_min"], 1)
                elif j == 1:
                    dve.wait_ge(s["lin_exp"], 2 * b + 1)
                    V.scalar_tensor_tensor(qlT[:, :], raw, 0.0, low, ALU.max, ALU.add).then_inc(s["lin_q_made"], 1)
                    dve.wait_ge(s["lin_ps"], k + 1)
                    dve.wait_ge(s["lin_q_made"], b + 1)
                    V.tensor_tensor(rows(raw), bank, bias(0), ALU.add).then_inc(s["lin_free"], 1)
                    dve.wait_ge(s["lin_free"], k + 1)
                    V.tensor_scalar(low, raw, 0.0, None, ALU.min).then_inc(s["lin_min"], 1)
                elif j == 2:
                    dve.wait_ge(s["lin_exp"], 2 * b + 2)
                    V.scalar_tensor_tensor(kl[:, :, :].rearrange("p t c -> p (t c)"), raw, 0.0, low, ALU.max, ALU.add).then_inc(s["lin_k_made"], 1)
                    dve.wait_ge(s["lin_ps"], k + 1)
                    V.tensor_tensor(vl[:, :, 0:P], bank, bias(1), ALU.add).then_inc(s["lin_free"], 1)
                elif j in (4, 5):
                    g = j - 4
                    dve.wait_ge(s["lin_ps"], k + 1)
                    dve.wait_ge(s["lin_k_made"], b + 1)
                    if b >= 1:
                        dve.wait_ge(s["lin_free"], LIN_STEPS * b)
                    nat = ps[:, 5, 0:2 * (P + 1)].rearrange("p (t c) -> p t c", c=P + 1)
                    rec = lrec[:, 2 * g:2 * g + 2]
                    link(V.tensor_scalar(rec, nat[:, :, P], 1e-6, None, ALU.add))
                    link(V.reciprocal(rec, rec))
                    for i in range(2):
                        last = V.tensor_scalar(ln_[:, 2 * g + i, :], nat[:, i, 0:P], rec[:, i:i + 1], None, ALU.mult)
                    last.then_inc(s["lin_free"], 1)

            def take_values(n):
                b, p = divmod(n, NPAIR)
                dve.wait_ge(s["pv_ps"], n + 1)
                if p == 0 and b >= 1:
                    dve.wait_ge(s["o_normed"], b)
                for half in range(2):
                    o = 64 * half
                    src = ps[o:o + 64, 6 + p % 2, 0:NBLK * VW].rearrange("p (i k a c) -> p i a c k", i=NBLK, k=SPLITS, a=2)
                    last = V.tensor_reduce(ot[o:o + 64, :, p, :], src[:, :, half, :, :], AX.X, ALU.add)
                last.then_inc(s["pv_taken"], 1)

            def normalise(b):
                dve.wait_ge(s["pv_taken"], NPAIR * (b + 1))
                o3 = ot[:, :, :, :].rearrange("p i n c -> p (i n) c")
                link(V.reciprocal(orec[:, :, :].rearrange("p i n -> p (i n)"), o3[:, :, HD]))
                if b >= 1:
                    dve.wait_ge(s["oT_ps"], b)
                V.tensor_tensor(on[:, :, :].rearrange("p i (n c) -> p (i n) c", c=HD), o3[:, :, 0:HD],
                                orec[:, :, :].rearrange("p i (n c) -> p (i n) c", c=1).broadcast_to((P, NBLK * NPAIR, HD)),
                                ALU.mult).then_inc(s["o_normed"], 1)

            def spread(b, c):
                if c == 0:
                    dve.wait_ge(q_in[b], 16 * 2 * NTERM)
                    if b >= 2:
                        dve.wait_ge(s["st_ps"], 2 * NPAIR * (b - 1))
                for half in range(2):
                    o = 64 * half
                    V.tensor_copy(qst[o:o + 64, b % 2, 2 * c:2 * c + 2, :, o:o + BQ].rearrange("p n i c -> p (n i) c"),
                                  qin[o:o + 64, 2 * c:2 * c + 2, :].rearrange("p n (i c) -> p (n i) c", c=BQ)).then_inc(s["q_spread"], 1)

            def difference(b):
                c = slice(b * S, (b + 1) * S)
                dve.wait_ge(s["oT_done"], b + 1)
                dve.wait_ge(s["lin_free"], LIN_STEPS * (b + 1))
                V.tensor_tensor(gd[:, b, :], lin_t[:, c], win_t[:, c], ALU.subtract).then_inc(s["diff_made"], 1)

            def mix(b):
                c = slice(b * S, (b + 1) * S)
                dve.wait_ge(s["gate_done"], b + 1)
                dve.wait_ge(s["diff_made"], b + 1)
                link(V.tensor_tensor(gd[:, b, :], gd[:, b, :], gg[:, b, :], ALU.mult))
                V.tensor_tensor(gd[:, b, :], gd[:, b, :], win_t[:, c], ALU.add).then_inc(s["mixed"], 1)

            def ffn_high(b):
                c = slice(b * S, (b + 1) * S)
                V.tensor_copy(hFh[:, c], hF[:, c]).then_inc(s["ffn_high"], 1)

            def ffn_low(b):
                c = slice(b * S, (b + 1) * S)
                dve.wait_ge(s["ffn_high"], b + 1)
                V.tensor_tensor(hFl[:, c], hF[:, c], hFh[:, c].bitcast(f32), ALU.subtract).then_inc(s["ffn_split"], 1)

            def add_projection(b, bank):
                t = slice(b * TB, (b + 1) * TB)
                dve.wait_ge(s["proj_ps"], b + 1)
                V.tensor_tensor(xs[:, t, :], xs[:, t, :], ps[:, bank, :].rearrange("p (t c) -> p t c", c=P), ALU.add).then_inc(s["proj_added"], 1)

            def split_weights(e, layer):
                k = e % 2
                raw, high, low = (w1r, w1h, w1l) if layer == 0 else (w2r, w2h, w2l)
                at = (slice(None), k) + (slice(None),) * (1 + layer)
                if layer == 0:
                    dve.wait_ge(w_in[k], 32 * (e // 2 + 1))
                    if e >= 2:
                        dve.wait_ge(s["y_ps"], NB * (e - 1))
                V.tensor_copy(high[at], raw[at]).then_inc(s["w_split"], 1)
                dve.wait_ge(s["w_split"], 4 * e + 2 * layer + 1)
                V.tensor_tensor(low[at], raw[at], high[at].bitcast(f32), ALU.subtract).then_inc(s["w_split"], 1)

            route = routing()
            for p in range(NPAIR):
                take_max(0, p)
            split_max(0)
            negmax_rows(0)
            for b in range(NB):
                for p in range(NPAIR):
                    n = b * NPAIR + p
                    ahead = AHEAD[p] if b + 1 < NB else []
                    if ahead:
                        take_max(b + 1, ahead[0])
                    if b >= 1 and b + 1 < NB and p < 3:
                        spread(b + 1, p + 1)
                    if b + 1 < NB:
                        if p == 6:
                            split_max(b + 1)
                        if p == 7:
                            negmax_rows(b + 1)
                    if b == NB - 1:
                        if p in (1, 2, 3, 4):
                            next(route, None)
                            ffn_high(p - 1)
                        if p == 6:
                            split_weights(0, 0)
                    if n >= 1:
                        take_values(n - 1)
                    for q in ahead[1:]:
                        take_max(b + 1, q)
                    if p == 0 and b >= 1:
                        normalise(b - 1)
                    if p != 1:
                        linear(b * LIN_STEPS + p - (p > 1))
                if 2 <= b + 2 < NB:
                    spread(b + 2, 0)
            take_values(NB * NPAIR - 1)
            normalise(NB - 1)

            difference(0)
            mix(0)
            difference(1)
            mix(1)
            difference(2)
            mix(2)
            ffn_low(0)
            difference(3)
            split_weights(0, 1)
            dve.wait_ge(s["residual_biased"], NB)
            add_projection(0, 6)
            add_projection(1, 7)
            ffn_low(1)
            V.tensor_copy(imix[:, 0:P], ident[:, :])
            V.tensor_copy(imix[:, P:P + 1], vcol(V_MIX1)).then_inc(s["imix_made"], 1)
            gen = wm[:, M_GEN * P:(M_GEN + NG) * P].rearrange("p (i c) -> p i c", c=P)
            down = 2.0 ** -EXPM_SQUARINGS
            for i in range(NG):
                last = V.scalar_tensor_tensor(pw[:, 0, i, :], gen[:, i, :], down / EXPM_DEGREE, ident[:, :], ALU.mult, ALU.add)
            last.then_inc(s["expm_seed"], 1)
            mix(3)
            add_projection(2, 4)
            ffn_low(2)
            ffn_low(3)

            def expm_steps():
                o = ps[:, 6, 0:NG * P].rearrange("p (i c) -> p i c", c=P)
                yield V.tensor_scalar(bt[:, :, :], o, down, None, ALU.mult)
                k = 0
                for d in range(EXPM_DEGREE - 1, 0, -1):
                    for i in range(NG):
                        last = V.scalar_tensor_tensor(pw[:, (k + 1) % 2, i, :], o[:, i, :], 1.0 / d, ident[:, :], ALU.mult, ALU.add)
                    yield last
                    k += 1
                yield V.tensor_copy(pwt[:, 0, :, :], o)
                kt = 0
                for _ in range(EXPM_SQUARINGS):
                    yield V.tensor_copy(pw[:, (k + 1) % 2, :, :], o)
                    yield V.tensor_copy(pwt[:, (kt + 1) % 2, :, :], o)
                    k += 1
                    kt += 1
                yield V.tensor_copy(mt[:, 0, :], o[:, 0, :])
                V.tensor_copy(rr[:, 0:P], o[:, 0, :])
                yield V.tensor_copy(mt[:, 1, :], o[:, 1, :])
                yield V.tensor_copy(rr[:, P:P + 1], o[:, 0, 0:1])

            def add_expert(u):
                c = slice((u % NB) * S, (u % NB + 1) * S)
                dve.wait_ge(s["y_ps"], u + 1)
                dve.wait_ge(wb_in[u % WB], 16 * (u // WB + 1))
                if u == 0:
                    dve.wait_ge(s["acc_made"], NB)
                V.tensor_tensor(ysc[:, u % 2, :], ps[:, 4 + u % 2, :], wb[:, u % WB, :], ALU.mult).then_inc(s["y_scaled"], 1)
                dve.wait_ge(s["y_scaled"], u + 1)
                V.tensor_tensor(acc[:, c], acc[:, c], ysc[:, u % 2, :], ALU.add).then_inc(s["y_added"], 1)

            def unmix(b, banks):
                if b == 0:
                    dve.wait_ge(s["gelu_done"], 3 * NB)
                for j in range(2):
                    dve.wait_ge(s["rot_ps"], 2 * b + j + 1)
                    t = slice(b * TB + 2 * j, b * TB + 2 * j + 2)
                    n2 = ps[:, banks[j], 0:2 * (P + 1)].rearrange("p (t c) -> p t c", c=P + 1)
                    V.tensor_tensor(gl[:, t], n2[:, :, P], abn[:, t, P], ALU.add)
                    V.tensor_tensor(dif[:, t, :], n2[:, :, 0:P], abn[:, t, 0:P], ALU.subtract).then_inc(s["rot_done"], 1)

            def output(b, gates):
                dve.wait_ge(s["gs_done"], gates)
                dve.wait_ge(s["rot_done"], 2 * (b + 1))
                dve.wait_ge(s["base_made"], NB)
                for t in range(b * TB, (b + 1) * TB):
                    V.scalar_tensor_tensor(xs[:, t, :], dif[:, t, :], gs[:, t:t + 1], xs[:, t, :], ALU.mult, ALU.add).then_inc(s["tile_done"], 1)

            steps_ = expm_steps()
            for u in range(NU):
                for j in range(2):
                    dve.wait_ge(s["hidh_done"], 2 * u + j + 1)
                    c = slice(2 * j, 2 * j + 2)
                    if u >= 2:
                        dve.wait_ge(s["y_ps"], u - 1)
                    V.tensor_tensor(hidl[:, u % 2, c, :], hid[:, u % 2, c, :], hidh[:, u % 2, c, :].bitcast(f32),
                                    ALU.subtract).then_inc(s["hidl_done"], 1)
                if u >= 1:
                    add_expert(u - 1)
                if u == 0:
                    add_projection(3, 5)
                if u < EXPM_STEPS:
                    dve.wait_ge(s["ex_ps"], u + 1)
                    step = next(steps_, None)
                    step.then_inc(s["ex_done"], 1)
                if u % NB == 1 and u // NB + 1 < E:
                    split_weights(u // NB + 1, 0)
                    split_weights(u // NB + 1, 1)
                if u >= NU - 2:
                    unmix(u - (NU - 2), (6, 7))
            assert next(steps_, None) is None
            add_expert(NU - 1)
            unmix(NB - 2, (6, 7))
            output(0, 1)
            output(1, 1)
            unmix(NB - 1, (0, 1))
            output(2, 2)
            output(3, 3)



def kernel(**inputs):
    import numpy as np
    import concourse.bacc as bacc
    from concourse import mybir as mb
    from concourse.bass_utils import run_bass_kernel_spmd

    a = {k: np.ascontiguousarray(v) for k, v in inputs.items()}
    at = lambda n: a["L0_attn_" + n]
    ff = lambda n: a["L0_ffn_" + n]
    D, HD, NPAIR = 128, 8, 8
    perm = np.arange(D).reshape(NPAIR, 2, HD).transpose(1, 0, 2).reshape(D)
    perm_qk = np.arange(D).reshape(NPAIR, 2, HD).transpose(1, 2, 0).reshape(D)
    bv = at("bv_loc")[perm]
    cols = [at("bq_lin"), at("bq_loc")[perm_qk], at("bk_loc")[perm_qk], bv, np.roll(bv, -64), at("bg1"), at("bg2")[perm],
            at("ln_g"), at("ln_b"), ff("ln_g"), ff("ln_b"), ff("abel_b"), ff("mix_w")[0:D, 0], ff("mix_w")[D:2 * D, 0],
            np.repeat(ff("mix_b"), D)]
    wg1 = at("wg1")
    rel = at("rel_bias")
    rel_t = np.zeros((rel.shape[1], 192), rel.dtype)
    rel_t[:, 31:31 + rel.shape[0]] = rel.T[:, ::-1]
    gens = ff("gens")
    b1 = ff("b1")
    arrays = {
        "x": a["L0_attn_x"],
        "vecs": np.stack(cols, axis=1),
        "rows": np.concatenate([at("bk_lin"), at("bv_lin")[perm], at("bo"), ff("gate_b_moe")])[None, :],
        "w_loc": np.concatenate([at("wq_loc")[:, perm_qk], at("wk_loc")[:, perm_qk], at("wv_loc")], axis=1),
        "w_more": np.concatenate([at("wq_lin"), at("wk_lin"), at("wv_lin")[:, perm], at("wo")[perm, :],
                                  wg1[0:D][perm, :], wg1[D:2 * D][perm, :], wg1[2 * D:], at("wg2")[:, perm],
                                  ff("abel_w"), gens[0], gens[1], gens[2], ff("gate_w_moe")], axis=1),
        "rel_t": rel_t,
        "b1_cols": b1.reshape(b1.shape[0], -1, D).transpose(2, 0, 1).reshape(D, -1),
        "b2": ff("b2"), "w1": ff("w1"), "w2": ff("w2"),
    }
    arrays = {"in_" + k: np.ascontiguousarray(v) for k, v in arrays.items()}
    nc = bacc.Bacc("TRN2", target_bir_lowering=False, num_devices=1)
    args = {k: nc.dram_tensor(k, v.shape, mb.dt.from_np(v.dtype), kind="ExternalInput").ap() for k, v in arrays.items()}
    g = lambda n: args["in_" + n]
    q_scratch = nc.dram_tensor("q_scratch", [4, 3, D, 512], mb.dt.bfloat16, kind="Internal").ap()
    k_scratch = nc.dram_tensor("k_scratch", [4, 3, D, 576], mb.dt.bfloat16, kind="Internal").ap()
    routing_scratch = nc.dram_tensor("routing_scratch", [8, 4 * 512], mb.dt.float32, kind="Internal").ap()
    out = nc.dram_tensor("out_0_dram", (4, 512, D), mb.dt.float32, kind="ExternalOutput").ap()
    attention_and_moe_block(nc, g("x"), g("vecs"), g("rows"), g("w_loc"), g("w_more"), g("rel_t"), g("b1_cols"),
                            g("b2"), g("w1"), g("w2"), q_scratch, k_scratch, routing_scratch, out)
    r = run_bass_kernel_spmd(nc, [arrays], core_ids=[0])
    return r.results[0]["out_0_dram"]
```
